# Optimizing a Trainium2 kernel written in Bass

```python
import numpy as np
import jax
import jax.numpy as jnp

def _softmax(x, axis=-1):
    return jax.nn.softmax(x, axis=axis)

def _gelu(x):
    return jax.nn.gelu(x, approximate=True)

def _silu(x):
    return jax.nn.silu(x)

def _sigmoid(x):
    return jax.nn.sigmoid(x)

def _layernorm(x, axis=-1, eps=1e-05):
    m = jnp.mean(x, axis=axis, keepdims=True)
    v = jnp.var(x, axis=axis, keepdims=True)
    return (x - m) / jnp.sqrt(v + eps)

def _scatter_add(tgt, idx, src, axis=0):
    return tgt.at[idx].add(src)

def _segment_sum(src, seg, n):
    return jax.ops.segment_sum(src, seg, n)
kernel_name = 'mk_vit_tower_cls_d1_tok_img1024_r4_56a1a1'

def setup_inputs(seed: int=0):
    np.random.seed(seed)
    _w = jnp.asarray

    def _rec_inputs():
        import jax
        import jax.numpy as jnp
        _rk = jax.random.key(seed)
        x = -0.00150118 + 0.499729 * jax.random.normal(jax.random.fold_in(_rk, 1), (8, 256, 64, 2), jnp.float32)
        cls_tok = 0.02 * jax.random.normal(jax.random.fold_in(_rk, 5), (1, 1, 256), jnp.float32)
        return (x, cls_tok)
    x, cls_tok = _rec_inputs()

    def _L0_tok_setup():
        import jax, jax.numpy as jnp
        import numpy as np
        import math
        H = 256
        N = 64
        CH = 1
        SEQ_L = 256
        key = jax.random.key(seed)
        k1, k2, k3, k4 = jax.random.split(key, 4)
        log_dt = jax.random.uniform(k1, (H,), dtype=jnp.float32, minval=math.log(0.001), maxval=math.log(0.1))
        inv_A_real = jnp.log(0.5 * jnp.ones((H, N), jnp.float32)) + 0.1 * jax.random.normal(k2, (H, N), dtype=jnp.float32)
        A_imag = jnp.broadcast_to(math.pi * jnp.arange(N, dtype=jnp.float32), (H, N)).copy()
        B_ri = jax.random.normal(k3, (H, N, 2), dtype=jnp.float32) * 0.5
        C_ri = jax.random.normal(k4, (CH, H, N, 2), dtype=jnp.float32) * 0.5
        return {'log_dt': log_dt, 'inv_A_real': inv_A_real, 'A_imag': A_imag, 'B_ri': B_ri, 'C_ri': C_ri, 'L': SEQ_L}
    _L0_tok_all = _L0_tok_setup()
    _L0_tok_in = {k: v for k, v in _L0_tok_all.items() if k in ('log_dt', 'inv_A_real', 'A_imag', 'B_ri')}
    del _L0_tok_all

    def _L0_attn_setup():
        import jax, jax.numpy as jnp
        import numpy as np
        D_MODEL = 256
        D_STATE = 16
        D_CONV = 4
        EXPAND = 2
        D_INNER = EXPAND * D_MODEL
        BATCH = 2
        SEQ = 256

        def _mamba_fwd(x, in_proj_w, conv_w, conv_b, x_proj_w, dt_proj_w, dt_proj_b, A_log, D, out_proj_w, ln_gamma, ln_beta):
            B, L, _ = x.shape
            residual = x
            xz = x @ in_proj_w.T
            x_inner, z = jnp.split(xz, 2, axis=-1)
            xc = jnp.transpose(x_inner, (0, 2, 1))
            xc = jax.lax.conv_general_dilated(xc, conv_w, window_strides=(1,), padding=[(D_CONV - 1, 0)], dimension_numbers=('NCH', 'OIH', 'NCH'), feature_group_count=D_INNER)
            xc = xc + conv_b[None, :, None]
            xc = jax.nn.silu(jnp.transpose(xc, (0, 2, 1)))
            x_dbl = xc @ x_proj_w.T
            dt = jax.nn.softplus(x_dbl[..., :1] @ dt_proj_w.T + dt_proj_b)
            Bs = x_dbl[..., 1:1 + D_STATE]
            Cs = x_dbl[..., 1 + D_STATE:]
            A = -jnp.exp(A_log)
            dA = jnp.exp(jnp.einsum('bld,dn->bldn', dt, A))
            dBx = jnp.einsum('bld,bln,bld->bldn', dt, Bs, xc)

            def step(h, inp):
                dA_t, dBx_t, C_t = inp
                h = dA_t * h + dBx_t
                y_t = jnp.einsum('bdn,bn->bd', h, C_t)
                return (h, y_t)
            h0 = jnp.zeros((B, D_INNER, D_STATE), xc.dtype)
            _, ys = jax.lax.scan(step, h0, (jnp.moveaxis(dA, 1, 0), jnp.moveaxis(dBx, 1, 0), jnp.moveaxis(Cs, 1, 0)))
            y = jnp.moveaxis(ys, 0, 1) + D * xc
            y = y * jax.nn.silu(z)
            out = y @ out_proj_w.T
            o = out + residual
            mu = jnp.mean(o, axis=-1, keepdims=True)
            var = jnp.mean((o - mu) ** 2, axis=-1, keepdims=True)
            return (o - mu) / jnp.sqrt(var + 1e-05) * ln_gamma + ln_beta
        key = jax.random.key(seed)
        ks = jax.random.split(key, 9)
        s = lambda k, shape, scale: jax.random.normal(k, shape, dtype=jnp.float32) * scale
        x = s(ks[0], (BATCH, SEQ, D_MODEL), 1.0)
        in_proj_w = s(ks[1], (2 * D_INNER, D_MODEL), D_MODEL ** (-0.5))
        conv_w = s(ks[2], (D_INNER, 1, D_CONV), D_CONV ** (-0.5))
        conv_b = s(ks[3], (D_INNER,), 0.02)
        x_proj_w = s(ks[4], (1 + 2 * D_STATE, D_INNER), D_INNER ** (-0.5))
        dt_proj_w = s(ks[5], (D_INNER, 1), 1.0)
        dt_proj_b = jax.random.uniform(ks[6], (D_INNER,), minval=-4.0, maxval=-1.0, dtype=jnp.float32)
        A_log = jnp.log(jnp.broadcast_to(jnp.arange(1, D_STATE + 1, dtype=jnp.float32), (D_INNER, D_STATE)))
        D = jnp.ones((D_INNER,), jnp.float32)
        out_proj_w = s(ks[7], (D_MODEL, D_INNER), D_INNER ** (-0.5))
        ln_gamma = jnp.ones((D_MODEL,), jnp.float32)
        ln_beta = jnp.zeros((D_MODEL,), jnp.float32)
        return dict(x=x, in_proj_w=in_proj_w, conv_w=conv_w, conv_b=conv_b, x_proj_w=x_proj_w, dt_proj_w=dt_proj_w, dt_proj_b=dt_proj_b, A_log=A_log, D=D, out_proj_w=out_proj_w, ln_gamma=ln_gamma, ln_beta=ln_beta)
    _L0_attn_all = _L0_attn_setup()
    _L0_attn_in = {k: v for k, v in _L0_attn_all.items() if k in ('in_proj_w', 'conv_w', 'conv_b', 'x_proj_w', 'dt_proj_w', 'dt_proj_b', 'A_log', 'D', 'out_proj_w', 'ln_gamma', 'ln_beta')}
    del _L0_attn_all

    def _L0_ffn_setup():
        import jax, jax.numpy as jnp
        import numpy as np
        import math
        N_EXP = 8
        TOP_K = 2
        CAPACITY_FACTOR = 1.25

        def _capacity(num_tokens):
            cap = math.floor(TOP_K * CAPACITY_FACTOR * num_tokens / N_EXP)
            cap += cap % 2
            return int(cap)
        key = jax.random.key(seed)
        k1, k2, k3, k4 = jax.random.split(key, 4)
        B, C, d = (4, 256, 256)
        x = jax.random.normal(k1, (B, C, d), dtype=jnp.float32)
        w_g = jax.random.normal(k2, (d, N_EXP), dtype=jnp.float32) * 0.02
        c_fc = jax.random.normal(k3, (N_EXP, d, 4 * d), dtype=jnp.float32) * 0.02
        c_proj = jax.random.normal(k4, (N_EXP, 4 * d, d), dtype=jnp.float32) * 0.02
        return {'x': x, 'w_g': w_g, 'c_fc': c_fc, 'c_proj': c_proj}
    _L0_ffn_all = _L0_ffn_setup()
    _L0_ffn_in = {k: v for k, v in _L0_ffn_all.items() if k in ('w_g', 'c_fc', 'c_proj')}
    del _L0_ffn_all
    return {'x': x, 'cls_tok': cls_tok, 'L0_tok_log_dt': _L0_tok_in['log_dt'], 'L0_tok_inv_A_real': _L0_tok_in['inv_A_real'], 'L0_tok_A_imag': _L0_tok_in['A_imag'], 'L0_tok_B_ri': _L0_tok_in['B_ri'], 'L0_attn_in_proj_w': _L0_attn_in['in_proj_w'], 'L0_attn_conv_w': _L0_attn_in['conv_w'], 'L0_attn_conv_b': _L0_attn_in['conv_b'], 'L0_attn_x_proj_w': _L0_attn_in['x_proj_w'], 'L0_attn_dt_proj_w': _L0_attn_in['dt_proj_w'], 'L0_attn_dt_proj_b': _L0_attn_in['dt_proj_b'], 'L0_attn_A_log': _L0_attn_in['A_log'], 'L0_attn_D': _L0_attn_in['D'], 'L0_attn_out_proj_w': _L0_attn_in['out_proj_w'], 'L0_attn_ln_gamma': _L0_attn_in['ln_gamma'], 'L0_attn_ln_beta': _L0_attn_in['ln_beta'], 'L0_ffn_w_g': _L0_ffn_in['w_g'], 'L0_ffn_c_fc': _L0_ffn_in['c_fc'], 'L0_ffn_c_proj': _L0_ffn_in['c_proj']}

def reference(x, cls_tok, L0_tok_log_dt, L0_tok_inv_A_real, L0_tok_A_imag, L0_tok_B_ri, L0_attn_in_proj_w, L0_attn_conv_w, L0_attn_conv_b, L0_attn_x_proj_w, L0_attn_dt_proj_w, L0_attn_dt_proj_b, L0_attn_A_log, L0_attn_D, L0_attn_out_proj_w, L0_attn_ln_gamma, L0_attn_ln_beta, L0_ffn_w_g, L0_ffn_c_fc, L0_ffn_c_proj):
    import jax
    import jax.numpy as jnp

    def _L0_tok_ref(log_dt, inv_A_real, A_imag, B_ri, C_ri, L):
        import jax, jax.numpy as jnp
        import numpy as np
        import math
        H = 256
        N = 64
        CH = 1
        SEQ_L = 256
        dt = jnp.exp(log_dt)
        A = -jnp.exp(inv_A_real) + 1j * A_imag
        B = B_ri[..., 0] + 1j * B_ri[..., 1]
        C = C_ri[..., 0] + 1j * C_ri[..., 1]
        dtA = A * dt[:, None]
        dA = (1.0 + dtA / 2) / (1.0 - dtA / 2)
        C_term = C * B[None]
        log_dA = jnp.log(dA)
        V = jnp.exp(log_dA[:, :, None] * jnp.arange(L))
        K = 2.0 * jnp.einsum('chn,hnl->chl', C_term, V).real
        return K.astype(jnp.float32)

    def _L0_attn_ref(x, in_proj_w, conv_w, conv_b, x_proj_w, dt_proj_w, dt_proj_b, A_log, D, out_proj_w, ln_gamma, ln_beta):
        import jax, jax.numpy as jnp
        import numpy as np
        D_MODEL = 256
        D_STATE = 16
        D_CONV = 4
        EXPAND = 2
        D_INNER = EXPAND * D_MODEL
        BATCH = 2
        SEQ = 256

        def _mamba_fwd(x, in_proj_w, conv_w, conv_b, x_proj_w, dt_proj_w, dt_proj_b, A_log, D, out_proj_w, ln_gamma, ln_beta):
            B, L, _ = x.shape
            residual = x
            xz = x @ in_proj_w.T
            x_inner, z = jnp.split(xz, 2, axis=-1)
            xc = jnp.transpose(x_inner, (0, 2, 1))
            xc = jax.lax.conv_general_dilated(xc, conv_w, window_strides=(1,), padding=[(D_CONV - 1, 0)], dimension_numbers=('NCH', 'OIH', 'NCH'), feature_group_count=D_INNER)
            xc = xc + conv_b[None, :, None]
            xc = jax.nn.silu(jnp.transpose(xc, (0, 2, 1)))
            x_dbl = xc @ x_proj_w.T
            dt = jax.nn.softplus(x_dbl[..., :1] @ dt_proj_w.T + dt_proj_b)
            Bs = x_dbl[..., 1:1 + D_STATE]
            Cs = x_dbl[..., 1 + D_STATE:]
            A = -jnp.exp(A_log)
            dA = jnp.exp(jnp.einsum('bld,dn->bldn', dt, A))
            dBx = jnp.einsum('bld,bln,bld->bldn', dt, Bs, xc)

            def step(h, inp):
                dA_t, dBx_t, C_t = inp
                h = dA_t * h + dBx_t
                y_t = jnp.einsum('bdn,bn->bd', h, C_t)
                return (h, y_t)
            h0 = jnp.zeros((B, D_INNER, D_STATE), xc.dtype)
            _, ys = jax.lax.scan(step, h0, (jnp.moveaxis(dA, 1, 0), jnp.moveaxis(dBx, 1, 0), jnp.moveaxis(Cs, 1, 0)))
            y = jnp.moveaxis(ys, 0, 1) + D * xc
            y = y * jax.nn.silu(z)
            out = y @ out_proj_w.T
            o = out + residual
            mu = jnp.mean(o, axis=-1, keepdims=True)
            var = jnp.mean((o - mu) ** 2, axis=-1, keepdims=True)
            return (o - mu) / jnp.sqrt(var + 1e-05) * ln_gamma + ln_beta
        return _mamba_fwd(x, in_proj_w, conv_w, conv_b, x_proj_w, dt_proj_w, dt_proj_b, A_log, D, out_proj_w, ln_gamma, ln_beta)

    def _L0_ffn_ref(x, w_g, c_fc, c_proj):
        import jax, jax.numpy as jnp
        import numpy as np
        import math
        N_EXP = 8
        TOP_K = 2
        CAPACITY_FACTOR = 1.25

        def _capacity(num_tokens):
            cap = math.floor(TOP_K * CAPACITY_FACTOR * num_tokens / N_EXP)
            cap += cap % 2
            return int(cap)
        B, C, d = x.shape
        T = B * C
        cap = _capacity(T)
        xt = x.reshape(T, d)
        logits = xt @ w_g
        top_v, top_i = jax.lax.top_k(logits, TOP_K)
        full = jnp.full_like(logits, -jnp.inf)
        full = full.at[jnp.arange(T)[:, None], top_i].set(top_v)
        probs = jax.nn.softmax(full, axis=-1)
        exp_mask = jax.nn.one_hot(top_i, N_EXP, dtype=jnp.int32)
        exp_mask = jnp.transpose(exp_mask, (1, 0, 2))
        exp_rank = jnp.cumsum(exp_mask.reshape(TOP_K * T, N_EXP), axis=0) - 1
        exp_rank = exp_rank.reshape(TOP_K, T, N_EXP)
        exp_mask = exp_mask * (exp_rank < cap).astype(jnp.int32)
        exp_rank = jnp.sum(exp_mask * exp_rank, axis=-1)
        exp_weights = exp_mask.astype(x.dtype) * probs[None]
        rank_oh = jax.nn.one_hot(exp_rank, cap, dtype=x.dtype)
        cb_weight = jnp.einsum('kte,ktc->tec', exp_weights, rank_oh)
        sec_mask = (cb_weight != 0).astype(x.dtype)
        exp_batches = jnp.einsum('tec,td->ecd', sec_mask, xt)
        h = jax.nn.gelu(jnp.einsum('ecd,edf->ecf', exp_batches, c_fc), approximate=False)
        exp_out = jnp.einsum('ecf,efd->ecd', h, c_proj)
        out = cb_weight.reshape(T, N_EXP * cap) @ exp_out.reshape(N_EXP * cap, d)
        return out.reshape(B, C, d)
    h = _L0_tok_ref(L0_tok_log_dt, L0_tok_inv_A_real, L0_tok_A_imag, L0_tok_B_ri, x, 256)
    h = jnp.concatenate([jnp.broadcast_to(cls_tok, (h.shape[0], 1, h.shape[2])), h], axis=1)
    h = h + _L0_attn_ref(_layernorm(h, axis=-1), L0_attn_in_proj_w, L0_attn_conv_w, L0_attn_conv_b, L0_attn_x_proj_w, L0_attn_dt_proj_w, L0_attn_dt_proj_b, L0_attn_A_log, L0_attn_D, L0_attn_out_proj_w, L0_attn_ln_gamma, L0_attn_ln_beta)
    h = h + _L0_ffn_ref(_layernorm(h, axis=-1), L0_ffn_w_g, L0_ffn_c_fc, L0_ffn_c_proj)
    return h

_drawn_inputs = setup_inputs


def setup_inputs(seed=0):
    import zlib

    import numpy as np

    out = dict(_drawn_inputs(seed))
    spreads = {'L0_attn_D': (1.0, 0.6), 'L0_attn_ln_gamma': (1.0, 0.2), 'L0_attn_ln_beta': (0.0, 0.378)}
    factors = {'cls_tok': 4.23,
     'L0_attn_conv_b': 8.0,
     'L0_attn_dt_proj_w': 4.521,
     'L0_attn_dt_proj_b': 4.84,
     'L0_attn_A_log': 4.836,
     'L0_ffn_w_g': 4.379,
     'L0_ffn_c_fc': 3.816,
     'L0_ffn_c_proj': 3.726}
    for name, (base, spread) in spreads.items():
        noise = np.random.default_rng([zlib.crc32(name.encode()), seed]).standard_normal(out[name].shape)
        drawn = base * np.exp(spread * noise) if base else spread * noise
        out[name] = jnp.asarray(drawn.astype(out[name].dtype))
    for name, factor in factors.items():
        out[name] = (out[name] * factor).astype(out[name].dtype)
    return out
```

```python
import concourse.bass as bass
from concourse import mybir
from contextlib import ExitStack

F32 = mybir.dt.float32
BF16 = mybir.dt.bfloat16
U32 = mybir.dt.uint32
ALU = mybir.AluOpType
ACT = mybir.ActivationFunctionType
AX = mybir.AxisListType

P = 128
NSEQ, HEADS, NST, L = 8, 256, 64, 256
DI, NS, TAPS = 512, 16, 4
KD, KL = DI // P, L // P
NE, FF = 8, 1024
T = NSEQ * (HEADS + 1)
CAP = int(2 * 1.25 * T / NE)
CAP += CAP % 2
SLOT_P, SLOT_M = 112, 6
PITCH = SLOT_P * SLOT_M
NA, NB = 64, L // 64
GROUPS, GT = 4, 512
CH = GT // P
EPS = 1e-5
OUT_OF_RANGE = 16384.0
XD = 1 + 2 * NS


def wait(eng, sem, value):
    if isinstance(value, int) and value <= 0:
        return
    eng.wait_ge(sem, value)


def vit_tower_kernel(nc, x, s4, cls, w_in, dpar, d_row, dtw_row, w_xp, w_out, ln_rows, w_g, c_fc, c_proj,
                     ident_in, tri_in, iota_in, out):
    ctx = ExitStack()
    with ctx:
        def sem(name):
            return ctx.enter_context(nc.semaphore(name))

        def sb(name, shape, dt=F32, stack=ctx):
            return stack.enter_context(nc.sbuf_tensor(name, shape, dt))

        def sems(names):
            return [sem(n) for n in names.split()]

        bank = [ctx.enter_context(nc.psum_tensor(f"bank{i}", [P, 512], F32)) for i in range(8)]

        k_scr = nc.dram_tensor("k_scr", (8, P, 512), F32).ap()
        h1_scr = nc.dram_tensor("h1_scr", (NSEQ * HEADS, L), F32).ap()
        xt_scr = nc.dram_tensor("xt_scr", (NSEQ * HEADS, L), F32).ap()
        xe_scr = nc.dram_tensor("xe_scr", (NE * PITCH, L), F32).ap()
        eo_scr = nc.dram_tensor("eo_scr", (NE * PITCH, L), F32).ap()

        ident = sb("ident", [P, P])
        tri = sb("tri", [P, P])
        iota8 = sb("iota8", [P, NE])
        win = sb("win", [P, KL, 2 * DI])
        par = sb("par", [P, KD, 8 + NS])
        conv_w, conv_b, dt_w, dt_b, skip_d = par[:, :, 0:4], par[:, :, 4], par[:, :, 5], par[:, :, 6], par[:, :, 7]
        neg_a = sb("neg_a", [P, KD, NS])
        d_bc = sb("d_bc", [P, DI])
        dtw = sb("dtw", [1, DI])
        wxp = sb("wxp", [P, KD, XD])
        wout = sb("wout", [P, KD, L])
        ln_bc = sb("ln_bc", [P, 2, L])
        wg = sb("wg", [P, KL, NE])
        cls_row = sb("cls_row", [P, L])
        h1_cls = sb("h1_cls", [P, L])
        xt_cls = sb("xt_cls", [P, L])
        xin_cls = sb("xin_cls", [P, KD])
        h0 = sb("h0", [P, KD, NS])
        logits = sb("logits", [P, 17, NE])
        half_neg = sb("half_neg", [P, CH])
        zeros = sb("zeros", [16, L])

        ld_const, ld_cls, xe_zeroed, pool_const = sems("ld_const ld_cls xe_zeroed pool_const")

        stage = ExitStack()
        with stage:
            def sa(name, shape, dt=F32):
                return sb(name, shape, dt, stage)

            HP = HEADS // 2
            c_in = sa("c_in", [P, 2, HP, NSEQ])
            s4p = sa("s4p", [P, 5, HP])
            inv_a, a_im, b_re, b_im, log_dt = (s4p[:, i, :] for i in range(5))
            tmp = [sa(f"tmp{i}", [P, HP]) for i in range(8)]
            q_re = [sa(f"q_re{i}", [P, HP]) for i in range(7)]
            q_im = [sa(f"q_im{i}", [P, HP]) for i in range(7)]
            q_t = [sa(f"q_t{i}", [P, HP]) for i in range(3)]
            u_re = sa("u_re", [P, HP, NA])
            u_im = sa("u_im", [P, HP, NA])
            w_re = sa("w_re", [P, HP, NB, NSEQ])
            w_ni = sa("w_ni", [P, HP, NB, NSEQ])
            u_t = [sa(f"u_t{i}", [P, HP, NA // 2]) for i in range(2)]
            w_t = [sa(f"w_t{i}", [P, HP, NSEQ]) for i in range(2)]
            k_sb = sa("k_sb", [P, 8, 512])

            ld_s4, ld_c, s4_exp, pow_step, u_step, w_step, pow64, u_done, w_done, k_bank, k_evac, k_store = sems(
                "ld_s4 ld_c s4_exp pow_step u_step w_step pow64 u_done w_done k_bank k_evac k_store")
            block = stage.enter_context(nc.Block("states"))

            @block.sync
            def _(sp):
                sp.dma_start(s4p[:, :, :], s4).then_inc(ld_s4, 16)
                sp.dma_start(cls_row[:, :], cls.broadcast_to([P, L])).then_inc(ld_cls, 16)
                sp.dma_start(c_in[:, :, :, :], x).then_inc(ld_c, 16)
                sp.dma_start(ident[:, :], ident_in).then_inc(ld_const, 16)
                sp.dma_start(tri[:, :], tri_in).then_inc(ld_const, 16)
                sp.dma_start(iota8[:, :], iota_in.broadcast_to([P, NE])).then_inc(ld_const, 16)
                sp.dma_start(win[:, :, :], w_in).then_inc(ld_const, 16)
                sp.dma_start(par[:, :, :], dpar).then_inc(ld_const, 16)
                sp.dma_start(d_bc[:, :], d_row.broadcast_to([P, DI])).then_inc(ld_const, 16)
                sp.dma_start(dtw[:, :], dtw_row).then_inc(ld_const, 16)
                sp.dma_start(wxp[:, :, :], w_xp).then_inc(ld_const, 16)
                sp.dma_start(wout[:, :, :], w_out).then_inc(ld_const, 16)
                for i in range(2):
                    sp.dma_start(ln_bc[:, i, :], ln_rows[i:i + 1, :].broadcast_to([P, L])).then_inc(ld_const, 16)
                sp.dma_start(wg[:, :, :], w_g).then_inc(ld_const, 16)
                sp.wait_ge(pool_const, 2)
                sp.dma_start(xe_scr.rearrange("(p s) d -> p s d", p=16),
                             zeros[:, :].unsqueeze(1).broadcast_to([16, NE * PITCH // 16, L])).then_inc(xe_zeroed, 16)
                for i in range(8):
                    sp.wait_ge(k_evac, i + 1)
                    sp.dma_start(k_scr[i], k_sb[:, i, :]).then_inc(k_store, 16)
                sp.wait_ge(k_store, 8 * 16)
                sp.wait_ge(ld_const, 12 * 16)
                sp.wait_ge(ld_cls, 16)
                sp.wait_ge(xe_zeroed, 16)

            @block.scalar
            def _(act):
                act.wait_ge(ld_s4, 16)
                nc.scalar.activation(tmp[0][:, :], log_dt, ACT.Exp)
                nc.scalar.activation(tmp[1][:, :], inv_a, ACT.Exp).then_inc(s4_exp, 1)
                act.wait_ge(ld_const, 12 * 16)
                nc.scalar.activation(h0[:, :, :], par[:, :, 8:8 + NS], ACT.Exp).then_inc(s4_exp, 1)
                act.wait_ge(s4_exp, 2)
                nc.scalar.activation(neg_a[:, :, :], h0[:, :, :], ACT.Copy, scale=-1.0)
                for i in range(8):
                    act.wait_ge(k_bank, i + 1)
                    nc.scalar.activation(k_sb[:, i, :], bank[i][:, :], ACT.Copy).then_inc(k_evac, 1)

            @block.vector
            def _(dve):
                v = nc.vector
                done = [0]

                def step(ins):
                    done[0] += 1
                    ins.then_inc(pow_step, 1)
                    dve.wait_ge(pow_step, done[0])

                dt, ea, hr, zr, zi, den, num, rec = (t[:, :] for t in tmp)
                dve.wait_ge(s4_exp, 1)
                step(v.tensor_scalar(hr, dt, 0.5, None, ALU.mult))
                v.scalar_tensor_tensor(zr, ea, -1.0, hr, ALU.mult, ALU.mult)
                step(v.tensor_tensor(zi, a_im, hr, ALU.mult))
                v.tensor_scalar(num, zr, 1.0, None, ALU.add)
                step(v.tensor_scalar(rec, zr, -1.0, 1.0, ALU.mult, ALU.add))
                v.tensor_tensor(hr, zi, zi, ALU.mult)
                v.tensor_tensor(num, num, rec, ALU.mult)
                step(v.tensor_tensor(den, rec, rec, ALU.mult))
                v.tensor_tensor(num, num, hr, ALU.subtract)
                step(v.tensor_tensor(den, den, hr, ALU.add))
                step(v.reciprocal(rec, den))
                v.tensor_tensor(q_re[0][:, :], num, rec, ALU.mult)
                step(v.scalar_tensor_tensor(q_im[0][:, :], zi, 2.0, rec, ALU.mult, ALU.mult))
                for k in range(6):
                    v.tensor_tensor(q_t[0][:, :], q_re[k][:, :], q_re[k][:, :], ALU.mult)
                    v.tensor_tensor(q_t[1][:, :], q_im[k][:, :], q_im[k][:, :], ALU.mult)
                    step(v.scalar_tensor_tensor(q_im[k + 1][:, :], q_re[k][:, :], 2.0, q_im[k][:, :], ALU.mult, ALU.mult))
                    step(v.tensor_tensor(q_re[k + 1][:, :], q_t[0][:, :], q_t[1][:, :], ALU.subtract))
                v.memset(q_t[2][:, 0:1], 0.0).then_inc(pow64, 1)
                v.memset(u_re[:, :, 0:1], 1.0)
                step(v.memset(u_im[:, :, 0:1], 0.0))
                for k in range(6):
                    m = 1 << k
                    qr = q_re[k][:, :].unsqueeze(2).broadcast_to([P, HP, m])
                    qi = q_im[k][:, :].unsqueeze(2).broadcast_to([P, HP, m])
                    v.tensor_tensor(u_t[0][:, :, 0:m], u_re[:, :, 0:m], qr, ALU.mult)
                    step(v.tensor_tensor(u_t[1][:, :, 0:m], u_im[:, :, 0:m], qi, ALU.mult))
                    step(v.tensor_tensor(u_re[:, :, m:2 * m], u_t[0][:, :, 0:m], u_t[1][:, :, 0:m], ALU.subtract))
                    v.tensor_tensor(u_t[0][:, :, 0:m], u_re[:, :, 0:m], qi, ALU.mult)
                    step(v.tensor_tensor(u_t[1][:, :, 0:m], u_im[:, :, 0:m], qr, ALU.mult))
                    step(v.tensor_tensor(u_im[:, :, m:2 * m], u_t[0][:, :, 0:m], u_t[1][:, :, 0:m], ALU.add))
                v.memset(q_t[2][:, 1:2], 0.0).then_inc(u_done, 1)

            @block.gpsimd
            def _(pool):
                g = nc.gpsimd
                done = [0]

                def step(ins):
                    done[0] += 1
                    ins.then_inc(w_step, 1)
                    pool.wait_ge(w_step, done[0])

                g.memset(zeros[:, :], 0.0).then_inc(pool_const, 1)
                g.memset(half_neg[:, :], -0.5).then_inc(pool_const, 1)
                pool.wait_ge(ld_s4, 16)
                pool.wait_ge(ld_c, 16)
                cr, ci = c_in[:, 0, :, :], c_in[:, 1, :, :]
                br = b_re.unsqueeze(2).broadcast_to([P, HP, NSEQ])
                bi = b_im.unsqueeze(2).broadcast_to([P, HP, NSEQ])
                t0, t1 = w_t[0][:, :, :], w_t[1][:, :, :]
                step(g.tensor_tensor(t0, cr, br, ALU.mult))
                step(g.tensor_tensor(t1, ci, bi, ALU.mult))
                step(g.tensor_tensor(t0, t0, t1, ALU.subtract))
                step(g.tensor_tensor(w_re[:, :, 0, :], t0, t0, ALU.add))
                step(g.tensor_tensor(t0, cr, bi, ALU.mult))
                step(g.tensor_tensor(t1, ci, br, ALU.mult))
                step(g.tensor_tensor(t0, t0, t1, ALU.add))
                step(g.tensor_scalar(w_ni[:, :, 0, :], t0, -2.0, 1.0, ALU.mult, ALU.mult))
                pool.wait_ge(pow64, 1)
                pr = q_re[6][:, :].unsqueeze(2).broadcast_to([P, HP, NSEQ])
                pi = q_im[6][:, :].unsqueeze(2).broadcast_to([P, HP, NSEQ])
                for b in range(1, NB):
                    wr, wn = w_re[:, :, b - 1, :], w_ni[:, :, b - 1, :]
                    step(g.tensor_tensor(t0, wr, pr, ALU.mult))
                    step(g.tensor_tensor(t1, wn, pi, ALU.mult))
                    step(g.tensor_tensor(w_re[:, :, b, :], t0, t1, ALU.add))
                    step(g.tensor_tensor(t0, wn, pr, ALU.mult))
                    step(g.tensor_tensor(t1, wr, pi, ALU.mult))
                    step(g.tensor_tensor(w_ni[:, :, b, :], t0, t1, ALU.subtract))
                g.memset(w_t[0][:, 0, :], 0.0).then_inc(w_done, 1)

            @block.tensor
            def _(pe):
                pe.wait_ge(u_done, 1)
                pe.wait_ge(w_done, 1)
                for half in range(2):
                    rows = slice(64 * half, 64 * half + 64)
                    for hb in range(4):
                        for s in range(8):
                            for q in range(4):
                                h = hb * 32 + q * 8 + s
                                o = bank[half * 4 + hb][32 * q:32 * q + 32, s * NA:(s + 1) * NA]
                                nc.tensor.matmul(o, w_re[rows, h, :, :], u_re[rows, h, :], start=True, stop=False)
                                last = nc.tensor.matmul(o, w_ni[rows, h, :, :], u_im[rows, h, :], start=False, stop=True)
                        last.then_inc(k_bank, 1)

        stage = ExitStack()
        with stage:
            def sa(name, shape, dt=F32):
                return sb(name, shape, dt, stage)

            st = sa("c_st", [P, 6])
            mv = sa("c_mv", [P, 2])
            rstd = sa("c_rstd", [P, 1])
            xn = sa("c_xn", [P, L])
            xnt = sa("c_xnt", [P, KL, P])
            zs = sa("c_zs", [P, KD])
            cv = sa("c_cv", [P, KD])
            xc = sa("c_xc", [P, KD])
            xcb = sa("c_xcb", [P, KD, P])
            xd = sa("c_xd", [P, XD])
            vv = sa("c_vv", [P, KD])
            av = sa("c_av", [P, KD])
            uu = sa("c_uu", [P, KD])
            lw = sa("c_lw", [P, KD])
            w1 = sa("c_w1", [P, KD])
            dtx = sa("c_dtx", [P, KD])
            bcp = sa("c_bcp", [P, NS])
            bcs = sa("c_bcs", [P, 1])
            yy = sa("c_yy", [P, KD])
            ygb = sa("c_ygb", [P, KD, P])
            o = sa("c_o", [P, L])

            steps = ("stats1 rstd1 xn xnt xnt_sb inproj xin zs conv xc xcb xdbl xd v absv u lnw h0 ygb outproj "
                     "o stats2 rstd2 ln2 h1 stats3 rstd3 xt xtt xtt_sb logit logit_sb").split()
            cls_done, cls_own = sems("cls_done cls_own")

            def upto(name):
                return steps.index(name) + 1

            block = stage.enter_context(nc.Block("class_token"))

            @block.vector
            def _(dve):
                v = nc.vector
                own = [0]

                def step(ins):
                    own[0] += 1
                    ins.then_inc(cls_own, 1)
                    dve.wait_ge(cls_own, own[0])

                def stats(src, before):
                    if before:
                        dve.wait_ge(cls_done, upto(before))
                    step(v.bn_stats(st[:, :], src))
                    v.bn_aggr(mv[:, :], st[:, :]).then_inc(cls_done, 1)

                stats(cls_row[:, :], None)
                dve.wait_ge(cls_done, upto("rstd1"))
                v.tensor_scalar(xn[:, :], cls_row[:, :], mv[:, 0:1], rstd[:, 0:1], ALU.subtract, ALU.mult).then_inc(cls_done, 1)
                dve.wait_ge(cls_done, upto("zs"))
                step(v.tensor_tensor(cv[:, :], xin_cls[:, :], conv_w[:, :, 3], ALU.mult))
                v.tensor_tensor(cv[:, :], cv[:, :], conv_b, ALU.add).then_inc(cls_done, 1)
                dve.wait_ge(cls_done, upto("xc"))
                v.tensor_copy(xcb[:, :, :], xc[:, :].unsqueeze(2).broadcast_to([P, KD, P])).then_inc(cls_done, 1)
                dve.wait_ge(cls_done, upto("xdbl"))
                v.tensor_copy(xd[:, :], bank[2][:, 0:XD]).then_inc(cls_done, 1)
                dve.wait_ge(cls_done, upto("xd"))
                v.scalar_tensor_tensor(vv[:, :], dt_w, xd[:, 0:1], dt_b, ALU.mult, ALU.add).then_inc(cls_done, 1)
                dve.wait_ge(cls_done, upto("lnw"))
                step(v.tensor_scalar(w1[:, :], uu[:, :], 1.0, -1.0, ALU.add, ALU.add))
                step(v.tensor_tensor(w1[:, :], uu[:, :], w1[:, :], ALU.subtract))
                step(v.tensor_tensor(w1[:, :], w1[:, :], lw[:, :], ALU.add))
                step(v.scalar_tensor_tensor(vv[:, :], vv[:, :], 0.0, w1[:, :], ALU.max, ALU.add))
                step(v.tensor_tensor(dtx[:, :], vv[:, :], xc[:, :], ALU.mult))
                for k in range(KD):
                    v.tensor_scalar(h0[:, k, :], xd[:, 1:1 + NS], dtx[:, k:k + 1], None, ALU.mult)
                step(v.tensor_tensor(bcp[:, :], xd[:, 1:1 + NS], xd[:, 1 + NS:XD], ALU.mult))
                v.tensor_reduce(bcs[:, :], bcp[:, :], AX.X, ALU.add).then_inc(cls_done, 1)
                dve.wait_ge(cls_done, upto("h0"))
                step(v.tensor_tensor(yy[:, :], xc[:, :], skip_d, ALU.mult))
                step(v.scalar_tensor_tensor(yy[:, :], dtx[:, :], bcs[:, 0:1], yy[:, :], ALU.mult, ALU.add))
                step(v.tensor_tensor(yy[:, :], yy[:, :], zs[:, :], ALU.mult))
                v.tensor_copy(ygb[:, :, :], yy[:, :].unsqueeze(2).broadcast_to([P, KD, P])).then_inc(cls_done, 1)
                dve.wait_ge(cls_done, upto("outproj"))
                v.tensor_tensor(o[:, :], bank[3][:, 0:L], xn[:, :], ALU.add).then_inc(cls_done, 1)
                stats(o[:, :], "o")
                dve.wait_ge(cls_done, upto("rstd2"))
                v.tensor_scalar(o[:, :], o[:, :], mv[:, 0:1], rstd[:, 0:1], ALU.subtract, ALU.mult).then_inc(cls_done, 1)
                dve.wait_ge(cls_done, upto("ln2"))
                step(v.tensor_tensor(o[:, :], o[:, :], ln_bc[:, 0, :], ALU.mult))
                step(v.tensor_tensor(o[:, :], o[:, :], ln_bc[:, 1, :], ALU.add))
                v.tensor_tensor(h1_cls[:, :], o[:, :], cls_row[:, :], ALU.add).then_inc(cls_done, 1)
                stats(h1_cls[:, :], "h1")
                dve.wait_ge(cls_done, upto("rstd3"))
                v.tensor_scalar(xt_cls[:, :], h1_cls[:, :], mv[:, 0:1], rstd[:, 0:1], ALU.subtract, ALU.mult).then_inc(cls_done, 1)

            @block.gpsimd
            def _(pool):
                for n in (1, 2, 3):
                    pool.wait_ge(cls_done, upto(f"stats{n}"))
                    nc.gpsimd.tensor_scalar(rstd[:, :], mv[:, 1:2], EPS, 1.0, ALU.add, ALU.mult).then_inc(pool_const, 1)
                    pool.wait_ge(pool_const, 2 + n)
                    nc.gpsimd.tensor_tensor(rstd[:, :], rstd[:, :], half_neg[:, 0:1], ALU.pow).then_inc(cls_done, 1)

            @block.scalar
            def _(act):
                a = nc.scalar.activation
                act.wait_ge(cls_done, upto("xnt"))
                a(xnt[:, :, :], bank[0][:, 0:L].rearrange("p (j t) -> p j t", j=KL), ACT.Copy).then_inc(cls_done, 1)
                act.wait_ge(cls_done, upto("inproj"))
                a(xin_cls[:, :], bank[1][:, 0:KD], ACT.Copy).then_inc(cls_done, 1)
                act.wait_ge(cls_done, upto("xin"))
                a(zs[:, :], bank[1][:, KD:2 * KD], ACT.Silu).then_inc(cls_done, 1)
                act.wait_ge(cls_done, upto("conv"))
                a(xc[:, :], cv[:, :], ACT.Silu).then_inc(cls_done, 1)
                act.wait_ge(cls_done, upto("v"))
                a(av[:, :], vv[:, :], ACT.Abs).then_inc(cls_done, 1)
                act.wait_ge(cls_done, upto("absv"))
                a(uu[:, :], av[:, :], ACT.Exp, scale=-1.0).then_inc(cls_done, 1)
                act.wait_ge(cls_done, upto("u"))
                a(lw[:, :], uu[:, :], ACT.Ln, bias=1.0).then_inc(cls_done, 1)
                act.wait_ge(cls_done, upto("xtt"))
                a(xnt[:, :, :], bank[4][:, 0:L].rearrange("p (j t) -> p j t", j=KL), ACT.Copy).then_inc(cls_done, 1)
                act.wait_ge(cls_done, upto("logit"))
                a(logits[:, 16, :], bank[5][:, 0:NE], ACT.Copy).then_inc(cls_done, 1)

            @block.tensor
            def _(pe):
                mm = nc.tensor.matmul
                pe.wait_ge(cls_done, upto("xn"))
                for j in range(KL):
                    last = nc.tensor.transpose(bank[0][:, j * P:(j + 1) * P], xn[:, j * P:(j + 1) * P], ident[:, :])
                last.then_inc(cls_done, 1)
                pe.wait_ge(cls_done, upto("xnt_sb"))
                for m in range(2 * KD):
                    for j in range(KL):
                        last = mm(bank[1][:, m:m + 1], win[:, j, m * P:(m + 1) * P], xnt[:, j, 0:1],
                                  start=(j == 0), stop=(j == KL - 1))
                last.then_inc(cls_done, 1)
                pe.wait_ge(cls_done, upto("xcb"))
                for k in range(KD):
                    last = mm(bank[2][:, 0:XD], xcb[:, k, :], wxp[:, k, :], start=(k == 0), stop=(k == KD - 1))
                last.then_inc(cls_done, 1)
                pe.wait_ge(cls_done, upto("ygb"))
                for k in range(KD):
                    last = mm(bank[3][:, 0:L], ygb[:, k, :], wout[:, k, :], start=(k == 0), stop=(k == KD - 1))
                last.then_inc(cls_done, 1)
                pe.wait_ge(cls_done, upto("xt"))
                for j in range(KL):
                    last = nc.tensor.transpose(bank[4][:, j * P:(j + 1) * P], xt_cls[:, j * P:(j + 1) * P], ident[:, :])
                last.then_inc(cls_done, 1)
                pe.wait_ge(cls_done, upto("xtt_sb"))
                for j in range(KL):
                    last = mm(bank[5][:, 0:NE], xnt[:, j, :], wg[:, j, :], start=(j == 0), stop=(j == KL - 1))
                last.then_inc(cls_done, 1)

        stage = ExitStack()
        with stage:
            def sa(name, shape, dt=F32):
                return sb(name, shape, dt, stage)

            k_in = sa("k_in", [P, CH, L])
            st = sa("st", [P, CH, 6])
            mv = sa("mv", [P, CH, 2])
            rstd = sa("rstd", [P, CH])
            xn = sa("xn", [P, CH, L])
            xnt = sa("xnt", [P, KL, GT])
            xin = sa("xin", [P, KD, 2, TAPS + HEADS])
            cv = sa("cv", [P, KD, GT])
            xc = sa("xc", [P, KD, GT])
            uu = sa("uu", [P, KD, GT])
            lw = sa("lw", [P, KD, GT])
            vv = sa("vv", [P, KD, GT])
            dt = sa("dt", [P, KD, GT])
            dtx = sa("dtx", [P, KD, GT])
            dtxt = sa("dtxt", [P, CH, DI])
            yt = sa("yt", [P, CH, DI])
            zst = sa("zst", [P, CH, DI])
            bc = sa("bc", [P, CH, XD])
            raw = sa("raw", [1, GT])
            bcur = sa("bcur", [P, 2, CH])
            bx = sa("bx", [P, 2, CH, DI])
            da = sa("da", [P, 2, KD, GT])
            hs = sa("hs", [P, 2, KD, GT])
            o = sa("o", [P, CH, L])
            h1 = sa("h1", [P, CH, L])
            xt = sa("xt", [P, CH, L])

            UNITS = ([("xnt", j, "act") for j in range(KL)] + [("xin", k, "act") for k in range(KD)]
                     + [("z", c, "act") for c in range(CH)] + [("xdbl", 0, "act"), ("raw", 0, "act")]
                     + [("dtv", k, "dve") for k in range(KD)] + [("xct", c, "dve") for c in range(CH)]
                     + [("dtxt", c, "act") for c in range(CH)] + [("ygt", k, "act") for k in range(KD)]
                     + [("out", i, "dve") for i in range(2)] + [("xtt", j, "act") for j in range(KL)]
                     + [("logit", 0, "act")])
            NU = len(UNITS)
            NU_ACT = sum(u[2] == "act" for u in UNITS)
            NU_DVE = NU - NU_ACT
            unit_no = {u[:2]: i for i, u in enumerate(UNITS)}

            def ubank(name, i):
                return bank[6 + unit_no[name, i] % 2]

            def taken(name, i, who):
                return sum(u[2] == who for u in UNITS[:unit_no[name, i] + 1])

            (ld_k, k_free, mv_ready, rstd_ready, xn_ready, unit_ready, act_took, dve_took, conv_ready, xc_ready,
             absv_ready, u_ready, ln_ready, dt_ready, dtx_ready, bcur_ready, bx_ready, bt_ready, da_ready, scanned,
             ht_ready, y_added, gated, ln2_ready, ln2_scaled, h1_ready, xt_ready, stored, dve_step, pool_step,
             edge_ready, waits_apart) = sems(
                "ld_k k_free mv_ready rstd_ready xn_ready unit_ready act_took dve_took conv_ready xc_ready absv_ready "
                "u_ready ln_ready dt_ready dtx_ready bcur_ready bx_ready bt_ready da_ready scanned ht_ready y_added "
                "gated ln2_ready ln2_scaled h1_ready xt_ready stored dve_step pool_step edge_ready waits_apart")
            PER = NS * 4
            DVE_STEPS, POOL_STEPS = 37, 4
            block = stage.enter_context(nc.Block("mamba"))

            def groups(eng, body):
                body(0)
                with eng.Fori(1, GROUPS) as g:
                    body(g)

            def states(eng, body):
                body(0, 0)
                body(1, 1)
                with eng.Fori(1, NS // 2) as i:
                    body(2 * i, 0)
                    body(2 * i + 1, 1)

            def apart(eng):
                eng.sem_inc(waits_apart, 1)

            def at(n):
                return slice(n, n + 1) if isinstance(n, int) else bass.ds(n, 1)

            @block.sync
            def _(sp):
                def group(g):
                    wait(sp, k_free, g)
                    for c in range(CH):
                        for b in range(NB):
                            src = k_scr.rearrange("(u hb) (q b c) (s a) -> u b c (hb q) s a", u=2, q=4, b=NB, s=8)
                            src = src[c % 2, b, at(2 * g + c // 2), :, :, :].rearrange("c r s a -> (c r) s a")
                            sp.dma_start(k_in[:, c, b * NA:(b + 1) * NA], src).then_inc(ld_k, 16)

                def store(g):
                    for c in range(CH):
                        rows = slice((4 * g + c) * P, (4 * g + c + 1) * P) if isinstance(g, int) else bass.ds(g * GT + c * P, P)
                        wait(sp, h1_ready, 4 * g + c + 1)
                        sp.dma_start(h1_scr[rows, :], h1[:, c, :]).then_inc(stored, 16)
                        wait(sp, xt_ready, 4 * g + c + 1)
                        sp.dma_start(xt_scr[rows, :], xt[:, c, :]).then_inc(stored, 16)

                def both(g):
                    group(g)
                    store(g)

                groups(sp, both)
                sp.wait_ge(stored, GROUPS * 2 * CH * 16)

            @block.gpsimd
            def _(pool):
                g_ = nc.gpsimd
                g_.memset(xin[:, :, :, 0:TAPS - 1], 0.0).then_inc(edge_ready, 1)

                def group(g):
                    own = [0]

                    def step(ins):
                        own[0] += 1
                        ins.then_inc(pool_step, 1)
                        pool.wait_ge(pool_step, g * POOL_STEPS + own[0])

                    def inverse_root(n):
                        pool.wait_ge(mv_ready, 3 * g + n + 1)
                        apart(pool)
                        step(g_.tensor_scalar(rstd[:, :], mv[:, :, 1], EPS, 1.0, ALU.add, ALU.mult))
                        g_.tensor_tensor(rstd[:, :], rstd[:, :], half_neg[:, :], ALU.pow).then_inc(rstd_ready, 1)

                    inverse_root(0)
                    for k in range(KD):
                        pool.wait_ge(dt_ready, 4 * g + k + 1)
                        g_.tensor_tensor(dtx[:, k, :], dt[:, k, :], xc[:, k, :], ALU.mult).then_inc(dtx_ready, 1)
                    pool.wait_ge(act_took, g * NU_ACT + taken("dtxt", CH - 1, "act"))

                    def scale(n, slot):
                        it = g * NS + n
                        wait(pool, bx_ready, 4 * it)
                        apart(pool)
                        g_.tensor_copy(bcur[:, slot, :], bc[:, :, at(n + 1)].rearrange("p c o -> p (c o)")).then_inc(bcur_ready, 1)
                        wait(pool, bt_ready, (it - 1) * 4)
                        pool.wait_ge(bcur_ready, it + 1)
                        apart(pool)
                        for c in range(CH):
                            g_.tensor_scalar(bx[:, slot, c, :], dtxt[:, c, :], bcur[:, slot, c:c + 1], 1.0,
                                             ALU.mult, ALU.mult).then_inc(bx_ready, 1)

                    states(pool, scale)
                    inverse_root(1)
                    pool.wait_ge(ln2_ready, g + 1)
                    step(g_.tensor_tensor(o[:, :, :], o[:, :, :], ln_bc[:, 0:1, :].broadcast_to([P, CH, L]), ALU.mult))
                    g_.tensor_tensor(o[:, :, :], o[:, :, :], ln_bc[:, 1:2, :].broadcast_to([P, CH, L]), ALU.add).then_inc(ln2_scaled, 1)
                    inverse_root(2)
                    assert own[0] == POOL_STEPS

                groups(pool, group)

            @block.scalar
            def _(act):
                a = nc.scalar.activation

                def group(g):
                    def take(out_, name, i, func=ACT.Copy, src=None):
                        act.wait_ge(unit_ready, g * NU + unit_no[name, i] + 1)
                        a(out_, ubank(name, i)[:, :] if src is None else src, func).then_inc(act_took, 1)

                    for j in range(KL):
                        take(xnt[:, j, :], "xnt", j)
                    if isinstance(g, int):
                        act.wait_ge(edge_ready, 1)
                        for s in range(2):
                            a(xin[:, :, s, TAPS - 1], xin_cls[:, :], ACT.Copy).then_inc(edge_ready, 1)
                    for k in range(KD):
                        take(xin[:, k, :, TAPS:], "xin", k, src=ubank("xin", k)[:, :].rearrange("p (s t) -> p s t", s=2))
                    for c in range(CH):
                        take(zst[:, c, :], "z", c, ACT.Silu)
                    for k in range(KD):
                        act.wait_ge(conv_ready, 4 * g + k + 1)
                        a(xc[:, k, :], cv[:, k, :], ACT.Silu).then_inc(xc_ready, 1)
                    take(bc[:, :, :], "xdbl", 0, src=ubank("xdbl", 0)[:, 0:CH * XD].rearrange("p (c m) -> p c m", c=CH))
                    take(raw[:, :], "raw", 0, src=ubank("raw", 0)[0:1, :])
                    for k in range(KD):
                        act.wait_ge(dve_took, g * NU_DVE + taken("dtv", k, "dve"))
                        a(uu[:, k, :], vv[:, k, :], ACT.Abs).then_inc(absv_ready, 1)
                        act.wait_ge(absv_ready, 4 * g + k + 1)
                        a(uu[:, k, :], uu[:, k, :], ACT.Exp, scale=-1.0).then_inc(u_ready, 1)
                    for k in range(KD):
                        act.wait_ge(u_ready, 4 * g + k + 1)
                        a(lw[:, k, :], uu[:, k, :], ACT.Ln, bias=1.0).then_inc(ln_ready, 1)
                    for c in range(CH):
                        take(dtxt[:, c, :], "dtxt", c)

                    def decay(n, slot):
                        it = g * NS + n
                        for k in range(KD):
                            wait(act, scanned, 4 * (it - 2) + k + 1)
                            a(da[:, slot, k, :], dt[:, k, :], ACT.Exp, scale=neg_a[:, k, at(n)]).then_inc(da_ready, 1)

                    states(act, decay)
                    for k in range(KD):
                        take(dtx[:, k, :], "ygt", k)
                    for j in range(KL):
                        take(xnt[:, j, :], "xtt", j)
                    rows = slice(4 * g, 4 * g + 4) if isinstance(g, int) else bass.ds(4 * g, 4)
                    take(logits[:, rows, :], "logit", 0, src=ubank("logit", 0)[:, 0:CH * NE].rearrange("p (c m) -> p c m", c=CH))

                groups(act, group)

            @block.vector
            def _(dve):
                v = nc.vector

                def group(g):
                    own = [0]

                    def step(ins):
                        own[0] += 1
                        ins.then_inc(dve_step, 1)
                        dve.wait_ge(dve_step, g * DVE_STEPS + own[0])

                    def stats(src):
                        for c in range(CH):
                            ins = v.bn_stats(st[:, c, :], src[:, c, :])
                        own[0] += 1
                        ins.then_inc(dve_step, 1)
                        dve.wait_ge(dve_step, g * DVE_STEPS + own[0])
                        apart(dve)
                        for c in range(CH):
                            ins = v.bn_aggr(mv[:, c, :], st[:, c, :])
                        ins.then_inc(mv_ready, 1)

                    def norm(dst, src, c):
                        return v.tensor_scalar(dst[:, c, :], src[:, c, :], mv[:, c, 0:1], rstd[:, c:c + 1], ALU.subtract, ALU.mult)

                    dve.wait_ge(ld_k, (g + 1) * CH * NB * 16)
                    stats(k_in)
                    dve.wait_ge(rstd_ready, 3 * g + 1)
                    for c in range(CH):
                        norm(xn, k_in, c).then_inc(xn_ready, 1)
                    dve.wait_ge(edge_ready, 3)
                    for k in range(KD):
                        dve.wait_ge(act_took, g * NU_ACT + taken("xin", k, "act"))
                        acc = cv[:, k, :].rearrange("p (s t) -> p s t", s=2)
                        step(v.tensor_scalar(acc, xin[:, k, :, 1:1 + HEADS], conv_w[:, k, 0:1], par[:, k, 4:5],
                                             ALU.mult, ALU.add))
                        for tap in range(1, TAPS):
                            ins = v.scalar_tensor_tensor(acc, xin[:, k, :, 1 + tap:1 + tap + HEADS], conv_w[:, k, tap:tap + 1],
                                                         acc, ALU.mult, ALU.add)
                            if tap < TAPS - 1:
                                step(ins)
                        ins.then_inc(conv_ready, 1)
                    for k in range(KD):
                        dve.wait_ge(unit_ready, g * NU + unit_no["dtv", k] + 1)
                        v.tensor_scalar(vv[:, k, :], ubank("dtv", k)[:, :], par[:, k, 6:7], None, ALU.add).then_inc(dve_took, 1)
                    for c in range(CH):
                        dve.wait_ge(unit_ready, g * NU + unit_no["xct", c] + 1)
                        v.tensor_tensor(yt[:, c, :], ubank("xct", c)[:, :], d_bc[:, :], ALU.mult).then_inc(dve_took, 1)
                    for k in range(KD):
                        dve.wait_ge(u_ready, 4 * g + k + 1)
                        step(v.tensor_scalar(cv[:, k, :], uu[:, k, :], 1.0, -1.0, ALU.add, ALU.add))
                        step(v.tensor_tensor(cv[:, k, :], uu[:, k, :], cv[:, k, :], ALU.subtract))
                        dve.wait_ge(ln_ready, 4 * g + k + 1)
                        step(v.tensor_tensor(cv[:, k, :], cv[:, k, :], lw[:, k, :], ALU.add))
                        v.scalar_tensor_tensor(dt[:, k, :], vv[:, k, :], 0.0, cv[:, k, :], ALU.max, ALU.add).then_inc(dt_ready, 1)

                    def scan(n, slot):
                        it = g * NS + n
                        for k in range(KD):
                            dve.wait_ge(bt_ready, 4 * it + k + 1)
                            dve.wait_ge(da_ready, 4 * it + k + 1)
                            if k == 0:
                                wait(dve, ht_ready, 4 * (it - 1))
                            for s in range(2):
                                t = slice(s * HEADS, (s + 1) * HEADS)
                                ins = v.tensor_tensor_scan(hs[:, slot, k, t], da[:, slot, k, t], bank[k][:, t],
                                                           h0[:, k, at(n)], ALU.mult, ALU.add)
                            ins.then_inc(scanned, 1)

                    def add(n):
                        it = g * NS + n
                        for c in range(CH):
                            dve.wait_ge(ht_ready, 4 * it + c + 1)
                            wait(dve, y_added, 4 * (it - 1) + c + 1)
                            if isinstance(n, int) and n == 0 and c == 0:
                                dve.wait_ge(dve_took, g * NU_DVE + taken("xct", CH - 1, "dve"))
                            v.scalar_tensor_tensor(yt[:, c, :], bank[4 + c % 2][:, :], bc[:, c, at(n + 1 + NS)], yt[:, c, :],
                                                   ALU.mult, ALU.add).then_inc(y_added, 1)

                    scan(0, 0)
                    scan(1, 1)
                    add(0)
                    with dve.Fori(1, NS // 2) as i:
                        scan(2 * i, 0)
                        add(2 * i - 1)
                        scan(2 * i + 1, 1)
                        add(2 * i)
                    add(NS - 1)
                    for c in range(CH):
                        dve.wait_ge(y_added, PER * (g + 1) - CH + c + 1)
                        v.tensor_tensor(yt[:, c, :], yt[:, c, :], zst[:, c, :], ALU.mult).then_inc(gated, 1)
                    for i in range(2):
                        dve.wait_ge(unit_ready, g * NU + unit_no["out", i] + 1)
                        v.tensor_tensor(o[:, 2 * i:2 * i + 2, :], ubank("out", i)[:, :].rearrange("p (c d) -> p c d", c=2),
                                        xn[:, 2 * i:2 * i + 2, :], ALU.add).then_inc(dve_took, 1)
                    dve.wait_ge(dve_took, NU_DVE * (g + 1))
                    stats(o)
                    dve.wait_ge(rstd_ready, 3 * g + 2)
                    for c in range(CH):
                        ins = norm(o, o, c)
                    ins.then_inc(ln2_ready, 1)
                    dve.wait_ge(ln2_scaled, g + 1)
                    wait(dve, stored, g * 2 * CH * 16)
                    for c in range(CH):
                        v.tensor_tensor(h1[:, c, :], o[:, c, :], k_in[:, c, :], ALU.add).then_inc(h1_ready, 1)
                    dve.wait_ge(h1_ready, 4 * (g + 1))
                    stats(h1)
                    dve.wait_ge(rstd_ready, 3 * g + 3)
                    for c in range(CH):
                        norm(xt, h1, c).then_inc(xt_ready, 1)
                    dve.wait_ge(xt_ready, 4 * (g + 1))
                    v.tensor_copy(st[:, 0, 0:1], mv[:, 0, 0:1]).then_inc(k_free, 1)
                    dve.wait_ge(k_free, g + 1)
                    assert own[0] <= DVE_STEPS, own
                    while own[0] < DVE_STEPS:
                        step(v.tensor_copy(st[:, 0, 0:1], mv[:, 0, 0:1]))

                groups(dve, group)

            @block.tensor
            def _(pe):
                mm = nc.tensor.matmul

                def group(g):
                    def room(name, i):
                        at_, prev = g, unit_no[name, i] - 2
                        if prev < 0:
                            at_, prev = g - 1, max(i for i in range(NU) if i % 2 == prev % 2)
                        who = UNITS[prev][2]
                        count = taken(*UNITS[prev][:2], who)
                        if who == "act":
                            wait(pe, act_took, at_ * NU_ACT + count)
                        else:
                            wait(pe, dve_took, at_ * NU_DVE + count)
                        return ubank(name, i)

                    def took(name, i):
                        pe.wait_ge(act_took, g * NU_ACT + taken(name, i, "act"))

                    def transposed(name, i, src, before):
                        b = room(name, i)
                        for c in range(4):
                            before(c)
                            last = nc.tensor.transpose(b[:, c * P:(c + 1) * P], src(c), ident[:, :])
                        last.then_inc(unit_ready, 1)

                    for j in range(KL):
                        transposed("xnt", j, lambda c: xn[:, c, j * P:(j + 1) * P],
                                   lambda c: pe.wait_ge(xn_ready, 4 * g + c + 1))
                    took("xnt", KL - 1)
                    for k in range(KD):
                        b = room("xin", k)
                        for j in range(KL):
                            last = mm(b[:, :], win[:, j, k * P:(k + 1) * P], xnt[:, j, :], start=(j == 0), stop=(j == KL - 1))
                        last.then_inc(unit_ready, 1)
                    for c in range(CH):
                        b = room("z", c)
                        for j in range(KL):
                            last = mm(b[:, :], xnt[:, j, c * P:(c + 1) * P], win[:, j, DI:2 * DI], start=(j == 0), stop=(j == KL - 1))
                        last.then_inc(unit_ready, 1)
                    pe.wait_ge(xc_ready, 4 * (g + 1))
                    b = room("xdbl", 0)
                    for c in range(CH):
                        for k in range(KD):
                            last = mm(b[:, c * XD:(c + 1) * XD], xc[:, k, c * P:(c + 1) * P], wxp[:, k, :],
                                      start=(k == 0), stop=(k == KD - 1))
                    last.then_inc(unit_ready, 1)
                    b = room("raw", 0)
                    for k in range(KD):
                        last = mm(b[0:1, :], wxp[:, k, 0:1], xc[:, k, :], start=(k == 0), stop=(k == KD - 1))
                    last.then_inc(unit_ready, 1)
                    took("raw", 0)
                    for k in range(KD):
                        b = room("dtv", k)
                        mm(b[:, :], dtw[0:1, k * P:(k + 1) * P], raw[0:1, :], start=True, stop=True).then_inc(unit_ready, 1)
                    for c in range(CH):
                        transposed("xct", c, lambda k: xc[:, k, c * P:(c + 1) * P], lambda k: None)
                    for c in range(CH):
                        transposed("dtxt", c, lambda k: dtx[:, k, c * P:(c + 1) * P],
                                   lambda k: pe.wait_ge(dtx_ready, 4 * g + k + 1))

                    def to_channels(n, slot):
                        it = g * NS + n
                        pe.wait_ge(bx_ready, 4 * (it + 1))
                        for k in range(KD):
                            wait(pe, scanned, 4 * (it - 1) + k + 1)
                            for c in range(CH):
                                last = nc.tensor.transpose(bank[k][:, c * P:(c + 1) * P], bx[:, slot, c, k * P:(k + 1) * P], ident[:, :])
                            last.then_inc(bt_ready, 1)

                    def to_time(n, slot):
                        it = g * NS + n
                        pe.wait_ge(scanned, 4 * (it + 1))
                        for c in range(CH):
                            wait(pe, y_added, 4 * it + c - 1)
                            for k in range(KD):
                                last = nc.tensor.transpose(bank[4 + c % 2][:, k * P:(k + 1) * P], hs[:, slot, k, c * P:(c + 1) * P], ident[:, :])
                            last.then_inc(ht_ready, 1)

                    to_channels(0, 0)
                    to_channels(1, 1)
                    to_time(0, 0)
                    with pe.Fori(1, NS // 2) as i:
                        to_channels(2 * i, 0)
                        to_time(2 * i - 1, 1)
                        to_channels(2 * i + 1, 1)
                        to_time(2 * i, 0)
                    to_time(NS - 1, 1)
                    for k in range(KD):
                        transposed("ygt", k, lambda c: yt[:, c, k * P:(k + 1) * P],
                                   lambda c: pe.wait_ge(gated, 4 * g + c + 1))
                    took("ygt", KD - 1)
                    for i in range(2):
                        b = room("out", i)
                        for c in (2 * i, 2 * i + 1):
                            for k in range(KD):
                                last = mm(b[:, (c % 2) * L:(c % 2 + 1) * L], dtx[:, k, c * P:(c + 1) * P], wout[:, k, :],
                                          start=(k == 0), stop=(k == KD - 1))
                        last.then_inc(unit_ready, 1)
                    for j in range(KL):
                        transposed("xtt", j, lambda c: xt[:, c, j * P:(j + 1) * P],
                                   lambda c: pe.wait_ge(xt_ready, 4 * g + c + 1))
                    took("xtt", KL - 1)
                    b = room("logit", 0)
                    for c in range(CH):
                        for j in range(KL):
                            last = mm(b[:, c * NE:(c + 1) * NE], xnt[:, j, c * P:(c + 1) * P], wg[:, j, :],
                                      start=(j == 0), stop=(j == KL - 1))
                    last.then_inc(unit_ready, 1)

                groups(pe, group)

        stage = ExitStack()
        with stage:
            def sa(name, shape, dt=F32):
                return sb(name, shape, dt, stage)

            NT = 17
            xts = sa("xts", [P, 16, L])
            h1s = sa("h1s", [P, 16, L])
            top = sa("top", [P, NT, 8])
            topi = sa("topi", [P, NT, 8], U32)
            ef = sa("ef", [P, NT, 2])
            oh = sa("oh", [P, NT, 2, NE])
            ohb = sa("ohb", [P, NT, 2, NE], BF16)
            trib = sa("trib", [P, P], BF16)
            oneb = sa("oneb", [P, P], BF16)
            base = sa("base", [P, NT, 2, NE])
            cbase = sa("cbase", [P, NSEQ, 2, NE])
            run = sa("run", [P, 25, 2, NE])
            rank = sa("rank", [P, NT, 2, NE])
            rk = sa("rk", [P, NT, 2])
            keep = sa("keep", [P, NT, 2])
            slot_f = sa("slot_f", [P, NT, 2])
            drop = sa("drop", [P, NT, 2])
            gidx = sa("gidx", [P, NT, 2], U32)
            sidx = sa("sidx", [P, NT, 2], U32)
            ee = sa("ee", [P, NT])
            pw = sa("pw", [P, NT, 2])
            xr = sa("xr", [SLOT_P, 2, SLOT_M, L])
            w1 = sa("w1", [P, 2, KL, FF])
            w2 = sa("w2", [P, 2, FF // P, L])
            xet = sa("xet", [P, 2, KL, PITCH])
            ht = sa("ht", [P, FF // P, PITCH])
            eo = sa("eo", [SLOT_P, 2, SLOT_M, L])
            ga = sa("ga", [P, 4, 2, L])
            KF = FF // P
            HALF = CAP // 2

            (ld_rows0, ld_rows1, ld_w10, ld_w11, ld_w20, ld_w21, tok_loaded, h1_loaded, rt_step, oh_ready, counts_ready, ee_in, ee_ready, idx_ready,
             w_ready, scattered, pad_ready, tr_ready, tr_taken, up_ready, gelu_done, down_ready, eo_taken, eo_stored0, eo_stored1,
             gath0, gath1, gath2, gath3, mixed, out_stored, mix_step) = sems(
                "ld_rows0 ld_rows1 ld_w10 ld_w11 ld_w20 ld_w21 tok_loaded h1_loaded rt_step oh_ready counts_ready ee_in ee_ready idx_ready w_ready "
                "scattered pad_ready tr_ready tr_taken up_ready gelu_done down_ready eo_taken eo_stored0 eo_stored1 gath0 gath1 gath2 gath3 "
                "mixed out_stored mix_step")
            ld_rows, ld_w1, ld_w2, eo_stored = [ld_rows0, ld_rows1], [ld_w10, ld_w11], [ld_w20, ld_w21], [eo_stored0, eo_stored1]
            gathered = [gath0, gath1, gath2, gath3]
            block = stage.enter_context(nc.Block("experts"))
            pairs = NE // 2

            def experts(eng, body):
                body(0, 0)
                body(1, 1)
                with eng.Fori(1, pairs) as i:
                    body(2 * i, 0)
                    body(2 * i + 1, 1)

            def rows_of(e, n):
                return slice(e * n, (e + 1) * n) if isinstance(e, int) else bass.ds(e * n, n)

            @block.sync
            def _(sp):
                sp.dma_start(xts[:, :, :], xt_scr.rearrange("(j p) d -> p j d", p=P)).then_inc(tok_loaded, 16)
                sp.dma_start(h1s[:, :, :], h1_scr.rearrange("(j p) d -> p j d", p=P)).then_inc(h1_loaded, 16)
                fc, pj = c_fc.rearrange("e l f -> (e l) f"), c_proj.rearrange("e f d -> (e f) d")

                def load(e, s):
                    wait(sp, up_ready, 16 * (e - 1))
                    sp.dma_start(w1[:, s, :, :], fc[rows_of(e, L), :].rearrange("(j p) f -> p j f", p=P)).then_inc(ld_w1[s], 16)
                    wait(sp, down_ready, SLOT_M * (e - 1))
                    sp.dma_start(w2[:, s, :, :], pj[rows_of(e, FF), :].rearrange("(k p) d -> p k d", p=P)).then_inc(ld_w2[s], 16)
                    if isinstance(e, int) and e == 0:
                        sp.wait_ge(scattered, 2 * NT * 16)
                    wait(sp, tr_ready, 4 * (e - 1))
                    sp.dma_start(xr[:, s, :, :], xe_scr[rows_of(e, PITCH), :].rearrange("(m p) d -> p m d", p=SLOT_P)).then_inc(ld_rows[s], 16)

                experts(sp, load)
                for j in range(NT):
                    sp.wait_ge(mixed, j + 1)
                    if j < 16:
                        to, of = out[j // 2, 1 + (j % 2) * P:1 + (j % 2 + 1) * P, :], h1s[:, j, :]
                    else:
                        to, of = out[:, 0, :], h1_cls[0:NSEQ, :]
                    sp.dma_start(to, of).then_inc(out_stored, 16)
                sp.wait_ge(out_stored, NT * 16)

            @block.scalar
            def _(act):
                act.wait_ge(ee_in, 1)
                nc.scalar.activation(ee[:, :], ee[:, :], ACT.Exp).then_inc(ee_ready, 1)

                def gelu(e, s):
                    for f in range(KF):
                        if f == 0:
                            wait(act, down_ready, SLOT_M * e)
                        for h in range(2):
                            act.wait_ge(up_ready, 16 * e + 2 * f + h + 1)
                            nc.scalar.activation(ht[:, f, h * HALF:(h + 1) * HALF], bank[2 + (2 * f + h) % 4][:, 0:HALF],
                                                 ACT.Gelu).then_inc(gelu_done, 1)
                    act.wait_ge(eo_taken, SLOT_M * (e + 1))
                    act.dma_start(eo_scr[rows_of(e, PITCH), :].rearrange("(m p) d -> p m d", p=SLOT_P), eo[:, s, :, :])\
                        .then_inc(eo_stored[s], 16)

                experts(act, gelu)

            @block.vector
            def _(dve):
                v = nc.vector
                own = [0]

                def step(ins):
                    own[0] += 1
                    ins.then_inc(rt_step, 1)
                    dve.wait_ge(rt_step, own[0])

                v.memset(oneb[:, :], 1.0)
                v.tensor_copy(trib[:, :], tri[:, :])
                for j in range(NT):
                    ins = v.max(top[:, j, :], logits[:, j, :])
                step(ins)
                for j in range(NT):
                    ins = v.max_index(topi[:, j, :], top[:, j, :], logits[:, j, :])
                step(ins)
                v.tensor_tensor(ee[:, :], top[:, :, 1], top[:, :, 0], ALU.subtract).then_inc(ee_in, 1)
                step(v.tensor_copy(ef[:, :, :], topi[:, :, 0:2]))
                step(v.tensor_tensor(oh[:, :, :, :], iota8[:, :].unsqueeze(1).unsqueeze(1).broadcast_to([P, NT, 2, NE]),
                                     ef[:, :, :].unsqueeze(3).broadcast_to([P, NT, 2, NE]), ALU.is_equal))
                v.tensor_copy(ohb[:, :, :, :], oh[:, :, :, :]).then_inc(oh_ready, 1)
                dve.wait_ge(ee_ready, 1)
                step(v.tensor_scalar(keep[:, :, 0], ee[:, :], 1.0, None, ALU.add))
                step(v.reciprocal(pw[:, :, 0], keep[:, :, 0]))
                step(v.tensor_tensor(pw[:, :, 1], ee[:, :], pw[:, :, 0], ALU.mult))
                dve.wait_ge(counts_ready, 1)
                count = bank[0][:, 0:16 * 2 * NE].rearrange("p (j k e) -> p j k e", j=16, k=2)
                prefix = bank[1][:, 0:16 * 2 * NE].rearrange("p (j k e) -> p j k e", j=16, k=2)
                step(v.memset(run[:, 0, :, :], 0.0))
                r = 0
                for q in range(NSEQ):
                    v.tensor_copy(cbase[:, q, :, :], run[:, r, :, :])
                    step(v.tensor_tensor(run[:, r + 1, :, :], run[:, r, :, :], oh[:, 16, :, :], ALU.add))
                    for half in range(2):
                        r += 1
                        v.tensor_copy(base[:, 2 * q + half, :, :], run[:, r, :, :])
                        step(v.tensor_tensor(run[:, r + 1, :, :], run[:, r, :, :], count[:, 2 * q + half, :, :], ALU.add))
                    r += 1
                step(v.memset(base[:, 16, :, :], 0.0))
                for q in range(NSEQ):
                    step(v.scalar_tensor_tensor(base[:, 16, :, :], cbase[:, q, :, :], ident[:, q:q + 1], base[:, 16, :, :],
                                                ALU.mult, ALU.add))
                v.tensor_copy(rank[:, 16, :, :], base[:, 16, :, :])
                step(v.tensor_tensor(rank[:, 0:16, :, :], prefix, base[:, 0:16, :, :], ALU.add))
                step(v.tensor_tensor(rank[:, :, 1, :], rank[:, :, 1, :], run[:, r, 0:1, :].broadcast_to([P, NT, NE]), ALU.add))
                step(v.tensor_tensor(rank[:, :, :, :], rank[:, :, :, :], oh[:, :, :, :], ALU.mult))
                step(v.tensor_reduce(rk[:, :, :], rank[:, :, :, :], AX.X, ALU.add))
                v.tensor_scalar(keep[:, :, :], rk[:, :, :], float(CAP), None, ALU.is_lt)
                step(v.scalar_tensor_tensor(slot_f[:, :, :], ef[:, :, :], float(PITCH), rk[:, :, :], ALU.mult, ALU.add))
                v.tensor_scalar(drop[:, :, :], keep[:, :, :], -OUT_OF_RANGE, OUT_OF_RANGE, ALU.mult, ALU.add)
                step(v.tensor_tensor(slot_f[:, :, :], slot_f[:, :, :], keep[:, :, :], ALU.mult))
                v.tensor_copy(gidx[:, :, :], slot_f[:, :, :])
                step(v.tensor_tensor(drop[:, :, :], drop[:, :, :], slot_f[:, :, :], ALU.add))
                v.tensor_copy(sidx[:, :, :], drop[:, :, :]).then_inc(idx_ready, 1)
                v.tensor_tensor(pw[:, :, :], pw[:, :, :], keep[:, :, :], ALU.mult).then_inc(w_ready, 1)
                v.memset(ht[:, :, CAP:PITCH], 0.0).then_inc(pad_ready, 1)
                WIDE = SLOT_P * SLOT_M // 2

                def evacuate(e, s):
                    for i in range(4):
                        j, h = i % 2, i // 2
                        dve.wait_ge(tr_ready, 4 * e + i + 1)
                        if i == 0:
                            wait(dve, up_ready, 16 * (e - 1))
                        v.tensor_copy(xet[:, s, j, h * WIDE:(h + 1) * WIDE], bank[i % 2][:, 0:WIDE]).then_inc(tr_taken, 1)

                def outputs(e, s):
                    wait(dve, eo_stored[s], 8 * (e - s))
                    for m in range(SLOT_M):
                        dve.wait_ge(down_ready, SLOT_M * e + m + 1)
                        v.tensor_copy(eo[:, s, m, :], bank[6 + m % 2][0:SLOT_P, 0:L]).then_inc(eo_taken, 1)

                evacuate(0, 0)
                evacuate(1, 1)
                outputs(0, 0)
                with dve.Fori(0, pairs - 1) as i:
                    evacuate(2 * i + 2, 0)
                    outputs(2 * i + 1, 1)
                    evacuate(2 * i + 3, 1)
                    outputs(2 * i + 2, 0)
                outputs(NE - 1, 1)
                for j in range(NT):
                    n = P if j < 16 else NSEQ
                    src = h1s[:, j, :] if j < 16 else h1_cls[0:NSEQ, :]
                    dve.wait_ge(gathered[j % 4], 32 * (j // 4 + 1))
                    if j == 0:
                        dve.wait_ge(h1_loaded, 16)
                        dve.wait_ge(w_ready, 1)
                    v.scalar_tensor_tensor(src, ga[0:n, j % 4, 0, :], pw[0:n, j, 0:1], src, ALU.mult, ALU.add).then_inc(mix_step, 1)
                    dve.wait_ge(mix_step, j + 1)
                    v.scalar_tensor_tensor(src, ga[0:n, j % 4, 1, :], pw[0:n, j, 1:2], src, ALU.mult, ALU.add).then_inc(mixed, 1)

            @block.gpsimd
            def _(pool):
                pool.wait_ge(tok_loaded, 16)
                pool.wait_ge(idx_ready, 1)
                for j in range(NT):
                    n = P if j < 16 else NSEQ
                    src = xts[:, j, :] if j < 16 else xt_cls[0:NSEQ, :]
                    for k in range(2):
                        nc.gpsimd.indirect_dma_start(xe_scr, bass.IndirectOffsetOnAxis(ap=sidx[0:n, j, k:k + 1], axis=0), src, None,
                                                     bounds_check=NE * PITCH - 1, oob_is_err=False).then_inc(scattered, 16)
                for s in range(2):
                    pool.wait_ge(eo_stored[s], 8 * NE)
                for j in range(NT):
                    n = P if j < 16 else NSEQ
                    wait(pool, mixed, j - 3)
                    for k in range(2):
                        nc.gpsimd.indirect_dma_start(ga[0:n, j % 4, k, :], None, eo_scr,
                                                     bass.IndirectOffsetOnAxis(ap=gidx[0:n, j, k:k + 1], axis=0),
                                                     bounds_check=NE * PITCH - 1, oob_is_err=False).then_inc(gathered[j % 4], 16)

            @block.tensor
            def _(pe):
                mm = nc.tensor.matmul
                n = 16 * 2 * NE
                pe.wait_ge(oh_ready, 1)
                flat = ohb[:, 0:16, :, :].rearrange("p j k e -> p (j k e)")
                mm(bank[0][:, 0:n], oneb[:, :], flat, start=True, stop=True)
                mm(bank[1][:, 0:n], trib[:, :], flat, start=True, stop=True).then_inc(counts_ready, 1)
                pe.wait_ge(idx_ready, 1)

                def rows_in(e, s):
                    pe.wait_ge(ld_rows[s], 8 * (e - s) + 16)
                    for i in range(4):
                        j, h = i % 2, i // 2
                        wait(pe, tr_taken, 4 * e + i - 1)
                        for m in range(3):
                            last = nc.tensor.transpose(bank[i % 2][:, m * SLOT_P:(m + 1) * SLOT_P],
                                                       xr[:, s, 3 * h + m, j * P:(j + 1) * P], ident[0:SLOT_P, 0:SLOT_P])
                        last.then_inc(tr_ready, 1)

                def up(e, s):
                    pe.wait_ge(ld_w1[s], 8 * (e - s) + 16)
                    pe.wait_ge(tr_taken, 4 * (e + 1))
                    for f in range(KF):
                        for h in range(2):
                            i = 2 * f + h
                            wait(pe, gelu_done, 16 * e + i - 3)
                            for j in range(KL):
                                last = mm(bank[2 + i % 4][:, 0:HALF], w1[:, s, j, f * P:(f + 1) * P],
                                          xet[:, s, j, h * HALF:(h + 1) * HALF], start=(j == 0), stop=(j == KL - 1))
                            last.then_inc(up_ready, 1)

                def down(e, s):
                    pe.wait_ge(ld_w2[s], 8 * (e - s) + 16)
                    pe.wait_ge(gelu_done, 16 * (e + 1))
                    for m in range(SLOT_M):
                        wait(pe, eo_taken, SLOT_M * e + m - 1)
                        for f in range(KF):
                            last = mm(bank[6 + m % 2][0:SLOT_P, 0:L], ht[:, f, m * SLOT_P:(m + 1) * SLOT_P], w2[:, s, f, :],
                                      start=(f == 0), stop=(f == KF - 1))
                        last.then_inc(down_ready, 1)

                rows_in(0, 0)
                up(0, 0)
                rows_in(1, 1)
                pe.wait_ge(pad_ready, 1)
                down(0, 0)
                with pe.Fori(0, pairs - 1) as i:
                    up(2 * i + 1, 1)
                    rows_in(2 * i + 2, 0)
                    down(2 * i + 1, 1)
                    up(2 * i + 2, 0)
                    rows_in(2 * i + 3, 1)
                    down(2 * i + 2, 0)
                up(NE - 1, 1)
                down(NE - 1, 1)


_OUTS = [((NSEQ, HEADS + 1, L), 'float32')]


def kernel(**inputs):
    import numpy as _np
    import concourse.bacc as _bacc
    from concourse import mybir as _mybir
    from concourse.bass_utils import run_bass_kernel_spmd as _run

    i = {k: _np.asarray(v) for k, v in inputs.items()}

    def fold(a):
        return a.reshape(2, HEADS // 2, NST).transpose(0, 2, 1).reshape(P, HEADS // 2)

    def channels(a):
        return a.reshape((KD, P) + a.shape[1:]).swapaxes(0, 1)

    laid = {
        "x": i["x"].reshape(NSEQ, 2, HEADS // 2, NST, 2).transpose(1, 3, 4, 2, 0).reshape(P, 2, HEADS // 2, NSEQ),
        "s4": _np.stack([fold(i["L0_tok_inv_A_real"]), fold(i["L0_tok_A_imag"]), fold(i["L0_tok_B_ri"][..., 0]),
                         fold(i["L0_tok_B_ri"][..., 1]),
                         fold(_np.broadcast_to(i["L0_tok_log_dt"][:, None], (HEADS, NST)))], axis=1),
        "cls": i["cls_tok"].reshape(1, L),
        "w_in": i["L0_attn_in_proj_w"].T.reshape(KL, P, 2 * DI).transpose(1, 0, 2),
        "dpar": _np.concatenate([channels(i["L0_attn_conv_w"][:, 0, :]), channels(i["L0_attn_conv_b"][:, None]),
                                 channels(i["L0_attn_dt_proj_w"]), channels(i["L0_attn_dt_proj_b"][:, None]),
                                 channels(i["L0_attn_D"][:, None]), channels(i["L0_attn_A_log"])], axis=2),
        "d_row": i["L0_attn_D"][None, :],
        "dtw_row": i["L0_attn_dt_proj_w"].reshape(1, DI),
        "w_xp": channels(i["L0_attn_x_proj_w"].T),
        "w_out": channels(i["L0_attn_out_proj_w"].T),
        "ln_rows": _np.stack([i["L0_attn_ln_gamma"], i["L0_attn_ln_beta"]]),
        "w_g": i["L0_ffn_w_g"].reshape(KL, P, NE).transpose(1, 0, 2),
        "c_fc": i["L0_ffn_c_fc"],
        "c_proj": i["L0_ffn_c_proj"],
        "ident_in": _np.eye(P, dtype=_np.float32),
        "tri_in": _np.triu(_np.ones((P, P), _np.float32), 1),
        "iota_in": _np.arange(NE, dtype=_np.float32)[None, :],
    }
    nc = _bacc.Bacc("TRN2", target_bir_lowering=False, num_devices=1)
    arrays, args = {}, []
    for name, a in laid.items():
        a = _np.ascontiguousarray(a)
        arrays[f"in_{name}"] = a
        args.append(nc.dram_tensor(f"in_{name}", a.shape, _mybir.dt.from_np(a.dtype), kind="ExternalInput").ap())
    for n, (shape, dtype) in enumerate(_OUTS):
        dt = _mybir.dt.from_np(_np.dtype(dtype))
        args.append(nc.dram_tensor(f"out_{n}", shape, dt, kind="ExternalOutput").ap())
    vit_tower_kernel(nc, *args)
    r = _run(nc, [arrays], core_ids=[0])
    return r.results[0]["out_0"]
```

```python
import concourse.bass as bass
from concourse import mybir
from contextlib import ExitStack

F32 = mybir.dt.float32
BF16 = mybir.dt.bfloat16
U32 = mybir.dt.uint32
ALU = mybir.AluOpType
ACT = mybir.ActivationFunctionType
AX = mybir.AxisListType

P = 128
NSEQ, HEADS, NST, L = 8, 256, 64, 256
DI, NS, TAPS = 512, 16, 4
KD, KL = DI // P, L // P
NE, FF = 8, 1024
T = NSEQ * (HEADS + 1)
CAP = int(2 * 1.25 * T / NE)
CAP += CAP % 2
SLOT_P, SLOT_M = 112, 6
PITCH = SLOT_P * SLOT_M
NA, NB = 64, L // 64
GROUPS, GT = NSEQ, HEADS
CH = GT // P
EPS = 1e-5
OUT_OF_RANGE = 16384.0
XD = 1 + 2 * NS


def wait(eng, sem, value):
    if isinstance(value, int) and value <= 0:
        return
    eng.wait_ge(sem, value)


def vit_tower_kernel(nc, x, s4, cls, w_in, dpar, dtw_row, w_xp, w_out, ln_rows, w_g, c_fc, c_proj,
                     ident_in, tri_in, iota_in, out):
    ctx = ExitStack()
    with ctx:
        def sem(name):
            return ctx.enter_context(nc.semaphore(name))

        def sb(name, shape, dt=F32, stack=ctx):
            return stack.enter_context(nc.sbuf_tensor(name, shape, dt))

        def sems(names):
            return [sem(n) for n in names.split()]

        bank = [ctx.enter_context(nc.psum_tensor(f"bank{i}", [P, 512], F32)) for i in range(8)]

        k_scr = nc.dram_tensor("k_scr", (8, P, 512), F32).ap()
        h1_scr = nc.dram_tensor("h1_scr", (NSEQ * HEADS, L), F32).ap()
        xt_scr = nc.dram_tensor("xt_scr", (NSEQ * HEADS, L), F32).ap()
        xe_scr = nc.dram_tensor("xe_scr", (NE * PITCH, L), F32).ap()
        eo_scr = nc.dram_tensor("eo_scr", (NE * PITCH, L), F32).ap()

        ident = sb("ident", [P, P])
        tri = sb("tri", [P, P])
        iota8 = sb("iota8", [P, NE])
        win = sb("win", [P, KL, 2 * DI])
        par = sb("par", [P, KD, 8 + NS])
        conv_w, conv_b, dt_w, dt_b, skip_d = par[:, :, 0:4], par[:, :, 4], par[:, :, 5], par[:, :, 6], par[:, :, 7]
        neg_a = sb("neg_a", [P, KD, NS])
        dtw = sb("dtw", [1, DI])
        wxp = sb("wxp", [P, KD, XD])
        wout = sb("wout", [P, KD, L])
        ln_bc = sb("ln_bc", [P, 2, L])
        wg = sb("wg", [P, KL, NE])
        cls_row = sb("cls_row", [P, L])
        h1_cls = sb("h1_cls", [P, L])
        xt_cls = sb("xt_cls", [P, L])
        xin_cls = sb("xin_cls", [P, KD])
        h0 = sb("h0", [P, KD, NS])
        logits = sb("logits", [P, 17, NE])
        half_neg = sb("half_neg", [P, CH])
        zeros = sb("zeros", [16, L])

        ld_const, ld_cls, xe_zeroed, pool_const = sems("ld_const ld_cls xe_zeroed pool_const")

        stage = ExitStack()
        with stage:
            def sa(name, shape, dt=F32):
                return sb(name, shape, dt, stage)

            HP = HEADS // 2
            c_in = sa("c_in", [P, 2, HP, NSEQ])
            s4p = sa("s4p", [P, 5, HP])
            inv_a, a_im, b_re, b_im, log_dt = (s4p[:, i, :] for i in range(5))
            tmp = [sa(f"tmp{i}", [P, HP]) for i in range(8)]
            q_re = [sa(f"q_re{i}", [P, HP]) for i in range(7)]
            q_im = [sa(f"q_im{i}", [P, HP]) for i in range(7)]
            q_t = [sa(f"q_t{i}", [P, HP]) for i in range(3)]
            u_re = sa("u_re", [P, HP, NA])
            u_im = sa("u_im", [P, HP, NA])
            w_re = sa("w_re", [P, HP, NB, NSEQ])
            w_ni = sa("w_ni", [P, HP, NB, NSEQ])
            u_t = [sa(f"u_t{i}", [P, HP, NA // 2]) for i in range(2)]
            w_t = [sa(f"w_t{i}", [P, HP, NSEQ]) for i in range(2)]
            k_sb = sa("k_sb", [P, 8, 512])

            ld_s4, ld_c, s4_exp, pow_step, u_step, w_step, pow64, u_done, w_done, k_bank, k_evac, k_store = sems(
                "ld_s4 ld_c s4_exp pow_step u_step w_step pow64 u_done w_done k_bank k_evac k_store")
            block = stage.enter_context(nc.Block("states"))

            @block.sync
            def _(sp):
                sp.dma_start(s4p[:, :, :], s4).then_inc(ld_s4, 16)
                sp.dma_start(cls_row[:, :], cls.broadcast_to([P, L])).then_inc(ld_cls, 16)
                sp.dma_start(c_in[:, :, :, :], x).then_inc(ld_c, 16)
                sp.dma_start(ident[:, :], ident_in).then_inc(ld_const, 16)
                sp.dma_start(tri[:, :], tri_in).then_inc(ld_const, 16)
                sp.dma_start(iota8[:, :], iota_in.broadcast_to([P, NE])).then_inc(ld_const, 16)
                sp.dma_start(win[:, :, :], w_in).then_inc(ld_const, 16)
                sp.dma_start(par[:, :, :], dpar).then_inc(ld_const, 16)
                sp.dma_start(dtw[:, :], dtw_row).then_inc(ld_const, 16)
                sp.dma_start(wxp[:, :, :], w_xp).then_inc(ld_const, 16)
                sp.dma_start(wout[:, :, :], w_out).then_inc(ld_const, 16)
                for i in range(2):
                    sp.dma_start(ln_bc[:, i, :], ln_rows[i:i + 1, :].broadcast_to([P, L])).then_inc(ld_const, 16)
                sp.dma_start(wg[:, :, :], w_g).then_inc(ld_const, 16)
                sp.wait_ge(pool_const, 2)
                sp.dma_start(xe_scr.rearrange("(p s) d -> p s d", p=16),
                             zeros[:, :].unsqueeze(1).broadcast_to([16, NE * PITCH // 16, L])).then_inc(xe_zeroed, 16)
                for i in range(8):
                    sp.wait_ge(k_evac, i + 1)
                    sp.dma_start(k_scr[i], k_sb[:, i, :]).then_inc(k_store, 16)
                sp.wait_ge(k_store, 8 * 16)
                sp.wait_ge(ld_const, 11 * 16)
                sp.wait_ge(ld_cls, 16)
                sp.wait_ge(xe_zeroed, 16)

            @block.scalar
            def _(act):
                act.wait_ge(ld_s4, 16)
                nc.scalar.activation(tmp[0][:, :], log_dt, ACT.Exp)
                nc.scalar.activation(tmp[1][:, :], inv_a, ACT.Exp).then_inc(s4_exp, 1)
                act.wait_ge(ld_const, 11 * 16)
                nc.scalar.activation(h0[:, :, :], par[:, :, 8:8 + NS], ACT.Exp).then_inc(s4_exp, 1)
                act.wait_ge(s4_exp, 2)
                nc.scalar.activation(neg_a[:, :, :], h0[:, :, :], ACT.Copy, scale=-1.0)
                for i in range(8):
                    act.wait_ge(k_bank, i + 1)
                    nc.scalar.activation(k_sb[:, i, :], bank[i][:, :], ACT.Copy).then_inc(k_evac, 1)

            @block.vector
            def _(dve):
                v = nc.vector
                done = [0]

                def step(ins):
                    done[0] += 1
                    ins.then_inc(pow_step, 1)
                    dve.wait_ge(pow_step, done[0])

                dt, ea, hr, zr, zi, den, num, rec = (t[:, :] for t in tmp)
                dve.wait_ge(s4_exp, 1)
                step(v.tensor_scalar(hr, dt, 0.5, None, ALU.mult))
                v.scalar_tensor_tensor(zr, ea, -1.0, hr, ALU.mult, ALU.mult)
                step(v.tensor_tensor(zi, a_im, hr, ALU.mult))
                v.tensor_scalar(num, zr, 1.0, None, ALU.add)
                step(v.tensor_scalar(rec, zr, -1.0, 1.0, ALU.mult, ALU.add))
                v.tensor_tensor(hr, zi, zi, ALU.mult)
                v.tensor_tensor(num, num, rec, ALU.mult)
                step(v.tensor_tensor(den, rec, rec, ALU.mult))
                v.tensor_tensor(num, num, hr, ALU.subtract)
                step(v.tensor_tensor(den, den, hr, ALU.add))
                step(v.reciprocal(rec, den))
                v.tensor_tensor(q_re[0][:, :], num, rec, ALU.mult)
                step(v.scalar_tensor_tensor(q_im[0][:, :], zi, 2.0, rec, ALU.mult, ALU.mult))
                for k in range(6):
                    v.tensor_tensor(q_t[0][:, :], q_re[k][:, :], q_re[k][:, :], ALU.mult)
                    v.tensor_tensor(q_t[1][:, :], q_im[k][:, :], q_im[k][:, :], ALU.mult)
                    step(v.scalar_tensor_tensor(q_im[k + 1][:, :], q_re[k][:, :], 2.0, q_im[k][:, :], ALU.mult, ALU.mult))
                    step(v.tensor_tensor(q_re[k + 1][:, :], q_t[0][:, :], q_t[1][:, :], ALU.subtract))
                v.memset(q_t[2][:, 0:1], 0.0).then_inc(pow64, 1)
                v.memset(u_re[:, :, 0:1], 1.0)
                step(v.memset(u_im[:, :, 0:1], 0.0))
                for k in range(6):
                    m = 1 << k
                    qr = q_re[k][:, :].unsqueeze(2).broadcast_to([P, HP, m])
                    qi = q_im[k][:, :].unsqueeze(2).broadcast_to([P, HP, m])
                    v.tensor_tensor(u_t[0][:, :, 0:m], u_re[:, :, 0:m], qr, ALU.mult)
                    step(v.tensor_tensor(u_t[1][:, :, 0:m], u_im[:, :, 0:m], qi, ALU.mult))
                    step(v.tensor_tensor(u_re[:, :, m:2 * m], u_t[0][:, :, 0:m], u_t[1][:, :, 0:m], ALU.subtract))
                    v.tensor_tensor(u_t[0][:, :, 0:m], u_re[:, :, 0:m], qi, ALU.mult)
                    step(v.tensor_tensor(u_t[1][:, :, 0:m], u_im[:, :, 0:m], qr, ALU.mult))
                    step(v.tensor_tensor(u_im[:, :, m:2 * m], u_t[0][:, :, 0:m], u_t[1][:, :, 0:m], ALU.add))
                v.memset(q_t[2][:, 1:2], 0.0).then_inc(u_done, 1)

            @block.gpsimd
            def _(pool):
                g = nc.gpsimd
                done = [0]

                def step(ins):
                    done[0] += 1
                    ins.then_inc(w_step, 1)
                    pool.wait_ge(w_step, done[0])

                g.memset(zeros[:, :], 0.0).then_inc(pool_const, 1)
                g.memset(half_neg[:, :], -0.5).then_inc(pool_const, 1)
                pool.wait_ge(ld_s4, 16)
                pool.wait_ge(ld_c, 16)
                cr, ci = c_in[:, 0, :, :], c_in[:, 1, :, :]
                br = b_re.unsqueeze(2).broadcast_to([P, HP, NSEQ])
                bi = b_im.unsqueeze(2).broadcast_to([P, HP, NSEQ])
                t0, t1 = w_t[0][:, :, :], w_t[1][:, :, :]
                step(g.tensor_tensor(t0, cr, br, ALU.mult))
                step(g.tensor_tensor(t1, ci, bi, ALU.mult))
                step(g.tensor_tensor(t0, t0, t1, ALU.subtract))
                step(g.tensor_tensor(w_re[:, :, 0, :], t0, t0, ALU.add))
                step(g.tensor_tensor(t0, cr, bi, ALU.mult))
                step(g.tensor_tensor(t1, ci, br, ALU.mult))
                step(g.tensor_tensor(t0, t0, t1, ALU.add))
                step(g.tensor_scalar(w_ni[:, :, 0, :], t0, -2.0, 1.0, ALU.mult, ALU.mult))
                pool.wait_ge(pow64, 1)
                pr = q_re[6][:, :].unsqueeze(2).broadcast_to([P, HP, NSEQ])
                pi = q_im[6][:, :].unsqueeze(2).broadcast_to([P, HP, NSEQ])
                for b in range(1, NB):
                    wr, wn = w_re[:, :, b - 1, :], w_ni[:, :, b - 1, :]
                    step(g.tensor_tensor(t0, wr, pr, ALU.mult))
                    step(g.tensor_tensor(t1, wn, pi, ALU.mult))
                    step(g.tensor_tensor(w_re[:, :, b, :], t0, t1, ALU.add))
                    step(g.tensor_tensor(t0, wn, pr, ALU.mult))
                    step(g.tensor_tensor(t1, wr, pi, ALU.mult))
                    step(g.tensor_tensor(w_ni[:, :, b, :], t0, t1, ALU.subtract))
                g.memset(w_t[0][:, 0, :], 0.0).then_inc(w_done, 1)

            @block.tensor
            def _(pe):
                pe.wait_ge(u_done, 1)
                pe.wait_ge(w_done, 1)
                for half in range(2):
                    rows = slice(64 * half, 64 * half + 64)
                    for hb in range(4):
                        for s in range(8):
                            for q in range(4):
                                h = hb * 32 + q * 8 + s
                                o = bank[half * 4 + hb][32 * q:32 * q + 32, s * NA:(s + 1) * NA]
                                nc.tensor.matmul(o, w_re[rows, h, :, :], u_re[rows, h, :], start=True, stop=False)
                                last = nc.tensor.matmul(o, w_ni[rows, h, :, :], u_im[rows, h, :], start=False, stop=True)
                        last.then_inc(k_bank, 1)

        stage = ExitStack()
        with stage:
            def sa(name, shape, dt=F32):
                return sb(name, shape, dt, stage)

            st = sa("c_st", [P, 6])
            mv = sa("c_mv", [P, 2])
            rstd = sa("c_rstd", [P, 1])
            xn = sa("c_xn", [P, L])
            xnt = sa("c_xnt", [P, KL, P])
            zs = sa("c_zs", [P, KD])
            cv = sa("c_cv", [P, KD])
            xc = sa("c_xc", [P, KD])
            xcb = sa("c_xcb", [P, KD, P])
            xd = sa("c_xd", [P, XD])
            vv = sa("c_vv", [P, KD])
            av = sa("c_av", [P, KD])
            uu = sa("c_uu", [P, KD])
            lw = sa("c_lw", [P, KD])
            w1 = sa("c_w1", [P, KD])
            dtx = sa("c_dtx", [P, KD])
            bcp = sa("c_bcp", [P, NS])
            bcs = sa("c_bcs", [P, 1])
            yy = sa("c_yy", [P, KD])
            ygb = sa("c_ygb", [P, KD, P])
            o = sa("c_o", [P, L])

            steps = ("stats1 rstd1 xn xnt xnt_sb inproj xin zs conv xc xcb xdbl xd v absv u lnw h0 ygb outproj "
                     "o stats2 rstd2 ln2 h1 stats3 rstd3 xt xtt xtt_sb logit logit_sb").split()
            cls_done, cls_own = sems("cls_done cls_own")

            def upto(name):
                return steps.index(name) + 1

            block = stage.enter_context(nc.Block("class_token"))

            @block.vector
            def _(dve):
                v = nc.vector
                own = [0]

                def step(ins):
                    own[0] += 1
                    ins.then_inc(cls_own, 1)
                    dve.wait_ge(cls_own, own[0])

                def stats(src, before):
                    if before:
                        dve.wait_ge(cls_done, upto(before))
                    step(v.bn_stats(st[:, :], src))
                    v.bn_aggr(mv[:, :], st[:, :]).then_inc(cls_done, 1)

                stats(cls_row[:, :], None)
                dve.wait_ge(cls_done, upto("rstd1"))
                v.tensor_scalar(xn[:, :], cls_row[:, :], mv[:, 0:1], rstd[:, 0:1], ALU.subtract, ALU.mult).then_inc(cls_done, 1)
                dve.wait_ge(cls_done, upto("zs"))
                step(v.tensor_tensor(cv[:, :], xin_cls[:, :], conv_w[:, :, 3], ALU.mult))
                v.tensor_tensor(cv[:, :], cv[:, :], conv_b, ALU.add).then_inc(cls_done, 1)
                dve.wait_ge(cls_done, upto("xc"))
                v.tensor_copy(xcb[:, :, :], xc[:, :].unsqueeze(2).broadcast_to([P, KD, P])).then_inc(cls_done, 1)
                dve.wait_ge(cls_done, upto("xdbl"))
                v.tensor_copy(xd[:, :], bank[2][:, 0:XD]).then_inc(cls_done, 1)
                dve.wait_ge(cls_done, upto("xd"))
                v.scalar_tensor_tensor(vv[:, :], dt_w, xd[:, 0:1], dt_b, ALU.mult, ALU.add).then_inc(cls_done, 1)
                dve.wait_ge(cls_done, upto("lnw"))
                step(v.tensor_scalar(w1[:, :], uu[:, :], 1.0, -1.0, ALU.add, ALU.add))
                step(v.tensor_tensor(w1[:, :], uu[:, :], w1[:, :], ALU.subtract))
                step(v.tensor_tensor(w1[:, :], w1[:, :], lw[:, :], ALU.add))
                step(v.scalar_tensor_tensor(vv[:, :], vv[:, :], 0.0, w1[:, :], ALU.max, ALU.add))
                step(v.tensor_tensor(dtx[:, :], vv[:, :], xc[:, :], ALU.mult))
                for k in range(KD):
                    v.tensor_scalar(h0[:, k, :], xd[:, 1:1 + NS], dtx[:, k:k + 1], None, ALU.mult)
                step(v.tensor_tensor(bcp[:, :], xd[:, 1:1 + NS], xd[:, 1 + NS:XD], ALU.mult))
                v.tensor_reduce(bcs[:, :], bcp[:, :], AX.X, ALU.add).then_inc(cls_done, 1)
                dve.wait_ge(cls_done, upto("h0"))
                step(v.tensor_tensor(yy[:, :], xc[:, :], skip_d, ALU.mult))
                step(v.scalar_tensor_tensor(yy[:, :], dtx[:, :], bcs[:, 0:1], yy[:, :], ALU.mult, ALU.add))
                step(v.tensor_tensor(yy[:, :], yy[:, :], zs[:, :], ALU.mult))
                v.tensor_copy(ygb[:, :, :], yy[:, :].unsqueeze(2).broadcast_to([P, KD, P])).then_inc(cls_done, 1)
                dve.wait_ge(cls_done, upto("outproj"))
                v.tensor_tensor(o[:, :], bank[3][:, 0:L], xn[:, :], ALU.add).then_inc(cls_done, 1)
                stats(o[:, :], "o")
                dve.wait_ge(cls_done, upto("rstd2"))
                v.tensor_scalar(o[:, :], o[:, :], mv[:, 0:1], rstd[:, 0:1], ALU.subtract, ALU.mult).then_inc(cls_done, 1)
                dve.wait_ge(cls_done, upto("ln2"))
                step(v.tensor_tensor(o[:, :], o[:, :], ln_bc[:, 0, :], ALU.mult))
                step(v.tensor_tensor(o[:, :], o[:, :], ln_bc[:, 1, :], ALU.add))
                v.tensor_tensor(h1_cls[:, :], o[:, :], cls_row[:, :], ALU.add).then_inc(cls_done, 1)
                stats(h1_cls[:, :], "h1")
                dve.wait_ge(cls_done, upto("rstd3"))
                v.tensor_scalar(xt_cls[:, :], h1_cls[:, :], mv[:, 0:1], rstd[:, 0:1], ALU.subtract, ALU.mult).then_inc(cls_done, 1)

            @block.gpsimd
            def _(pool):
                for n in (1, 2, 3):
                    pool.wait_ge(cls_done, upto(f"stats{n}"))
                    nc.gpsimd.tensor_scalar(rstd[:, :], mv[:, 1:2], EPS, 1.0, ALU.add, ALU.mult).then_inc(pool_const, 1)
                    pool.wait_ge(pool_const, 2 + n)
                    nc.gpsimd.tensor_tensor(rstd[:, :], rstd[:, :], half_neg[:, 0:1], ALU.pow).then_inc(cls_done, 1)

            @block.scalar
            def _(act):
                a = nc.scalar.activation
                act.wait_ge(cls_done, upto("xnt"))
                a(xnt[:, :, :], bank[0][:, 0:L].rearrange("p (j t) -> p j t", j=KL), ACT.Copy).then_inc(cls_done, 1)
                act.wait_ge(cls_done, upto("inproj"))
                a(xin_cls[:, :], bank[1][:, 0:KD], ACT.Copy).then_inc(cls_done, 1)
                act.wait_ge(cls_done, upto("xin"))
                a(zs[:, :], bank[1][:, KD:2 * KD], ACT.Silu).then_inc(cls_done, 1)
                act.wait_ge(cls_done, upto("conv"))
                a(xc[:, :], cv[:, :], ACT.Silu).then_inc(cls_done, 1)
                act.wait_ge(cls_done, upto("v"))
                a(av[:, :], vv[:, :], ACT.Abs).then_inc(cls_done, 1)
                act.wait_ge(cls_done, upto("absv"))
                a(uu[:, :], av[:, :], ACT.Exp, scale=-1.0).then_inc(cls_done, 1)
                act.wait_ge(cls_done, upto("u"))
                a(lw[:, :], uu[:, :], ACT.Ln, bias=1.0).then_inc(cls_done, 1)
                act.wait_ge(cls_done, upto("xtt"))
                a(xnt[:, :, :], bank[4][:, 0:L].rearrange("p (j t) -> p j t", j=KL), ACT.Copy).then_inc(cls_done, 1)
                act.wait_ge(cls_done, upto("logit"))
                a(logits[:, 16, :], bank[5][:, 0:NE], ACT.Copy).then_inc(cls_done, 1)

            @block.tensor
            def _(pe):
                mm = nc.tensor.matmul
                pe.wait_ge(cls_done, upto("xn"))
                for j in range(KL):
                    last = nc.tensor.transpose(bank[0][:, j * P:(j + 1) * P], xn[:, j * P:(j + 1) * P], ident[:, :])
                last.then_inc(cls_done, 1)
                pe.wait_ge(cls_done, upto("xnt_sb"))
                for m in range(2 * KD):
                    for j in range(KL):
                        last = mm(bank[1][:, m:m + 1], win[:, j, m * P:(m + 1) * P], xnt[:, j, 0:1],
                                  start=(j == 0), stop=(j == KL - 1))
                last.then_inc(cls_done, 1)
                pe.wait_ge(cls_done, upto("xcb"))
                for k in range(KD):
                    last = mm(bank[2][:, 0:XD], xcb[:, k, :], wxp[:, k, :], start=(k == 0), stop=(k == KD - 1))
                last.then_inc(cls_done, 1)
                pe.wait_ge(cls_done, upto("ygb"))
                for k in range(KD):
                    last = mm(bank[3][:, 0:L], ygb[:, k, :], wout[:, k, :], start=(k == 0), stop=(k == KD - 1))
                last.then_inc(cls_done, 1)
                pe.wait_ge(cls_done, upto("xt"))
                for j in range(KL):
                    last = nc.tensor.transpose(bank[4][:, j * P:(j + 1) * P], xt_cls[:, j * P:(j + 1) * P], ident[:, :])
                last.then_inc(cls_done, 1)
                pe.wait_ge(cls_done, upto("xtt_sb"))
                for j in range(KL):
                    last = mm(bank[5][:, 0:NE], xnt[:, j, :], wg[:, j, :], start=(j == 0), stop=(j == KL - 1))
                last.then_inc(cls_done, 1)

        stage = ExitStack()
        with stage:
            def sa(name, shape, dt=F32):
                return sb(name, shape, dt, stage)

            k_in = sa("k_in", [P, CH, L])
            k_res = sa("k_res", [P, 2, CH, L])
            xn = sa("xn", [P, CH, L])
            x_res = sa("x_res", [P, 2, CH, L])
            xnt = sa("xnt", [P, KL, GT])
            xin = sa("xin", [P, KD, TAPS + GT])
            cv = sa("cv", [P, KD, GT])
            xc = sa("xc", [P, 2, KD, GT])
            zs = sa("zs", [P, 2, KD, GT])
            xdt = sa("xdt", [XD, GT])
            bc = sa("bc", [P, 2, CH, XD])
            absv = sa("absv", [P, KD, GT])
            relv = sa("relv", [P, KD, GT])
            uu = sa("uu", [P, KD, GT])
            ww = sa("ww", [P, KD, GT])
            lw = sa("lw", [P, KD, GT])
            dt = sa("dt", [P, 2, KD, GT])
            dtx = sa("dtx", [P, KD, GT])
            dtxt = sa("dtxt", [P, 2, CH, DI])
            st = [sa(f"st{i}", [P, CH, 6]) for i in range(2)]
            mv = [sa(f"mv{i}", [P, CH, 2]) for i in range(2)]
            rstd = [sa(f"rstd{i}", [P, CH]) for i in range(2)]
            bx = sa("bx", [P, 4, CH, DI])
            da = sa("da", [P, 4, KD, GT])
            hs = sa("hs", [P, 2, KD, GT])
            yt = sa("yt", [P, 2, CH, DI])
            yp = sa("yp", [P, 2, DI])
            cy = sa("cy", [P, 2, DI])
            yg = sa("yg", [P, KD, GT])
            o = sa("o", [P, CH, L])
            h1 = sa("h1", [P, CH, L])
            xt = sa("xt", [P, CH, L])
            xtt = sa("xtt", [P, KL, GT])

            P_UNITS = "xnt xin0 xin1 z0 z1 xd dtv0 dtv1 bc dtxt0 dtxt1".split()
            T_UNITS = {"ygt0": "dve", "ygt1": "dve", "out": "dve", "xtt": "act", "logit": "act"}
            T_NAMES = list(T_UNITS)
            NPU, NTU, NTD, NTA = len(P_UNITS), 5, 3, 2
            P_BANK, T_BANK = bank[6], bank[7]

            (ld_k, edge_ready, mvp_ready, rstdp_ready, xn_ready, copied_x, copied_k, pu_ready, pu_took, tap0_ready,
             conv_ready, xc_ready, absv_ready, u_ready, one_u_ready, lnw_ready, lw_fixed, dt_ready, dtx_ready, bx_ready,
             bt_ready, da_ready, scanned, ht_ready, y0_added, y1_added, cy_ready, yp_added, merged, tu_ready, tu_dve,
             tu_act, gated, mvt_ready, rstdt_ready, ln2_ready, h1_ready, xt_ready, h1_stored, xt_stored, dve_p, dve_t,
             pool_step, rstdp_step, rstdt_step, w_fix, waits_apart) = sems(
                "ld_k edge_ready mvp_ready rstdp_ready xn_ready copied_x copied_k pu_ready pu_took tap0_ready "
                "conv_ready xc_ready absv_ready u_ready one_u_ready lnw_ready lw_fixed dt_ready dtx_ready bx_ready "
                "bt_ready da_ready scanned ht_ready y0_added y1_added cy_ready yp_added merged tu_ready tu_dve "
                "tu_act gated mvt_ready rstdt_ready ln2_ready h1_ready xt_ready h1_stored xt_stored dve_p dve_t "
                "pool_step rstdp_step rstdt_step w_fix waits_apart")
            rstd_step = [rstdp_step, rstdt_step]
            DVE_P_STEPS, DVE_T_STEPS = 5, 2
            W_TURN = 10
            NY1, NYP = NS // 2, NS // 2 - 1
            block = stage.enter_context(nc.Block("mamba"))


            def steps(eng, scan, project, finish, flush):
                for n in range(NS):
                    project(0, 0, n)
                def step(g, s, first=False, last=False):
                    for n in range(NS):
                        scan(g, s, n, first, last)
                        if not first:
                            finish(g - 1, 1 - s, n)
                        if not last:
                            project(g + 1, 1 - s, n)
                flush(0, 0, True)
                step(0, 0, first=True)
                with eng.Fori(0, GROUPS // 2 - 1) as i:
                    step(2 * i + 1, 1)
                    step(2 * i + 2, 0)
                step(GROUPS - 1, 1, last=True)
                flush(GROUPS - 1, 1, False)
                for n in range(NS):
                    finish(GROUPS - 1, 1, n)

            def apart(eng):
                eng.sem_inc(waits_apart, 1)

            def pu_index(name):
                return P_UNITS.index(name)

            def tu_taken(name, who):
                return sum(T_UNITS[u] == who for u in T_NAMES[:T_NAMES.index(name) + 1])

            @block.sync
            def _(sp):
                def load(g):
                    wait(sp, copied_k, 16 * g)
                    wait(sp, xn_ready, CH * g)
                    apart(sp)
                    for c in range(CH):
                        for b in range(NB):
                            src = k_scr.rearrange("(u hb) (q b c) (s a) -> u b c (hb q) s a", u=2, q=4, b=NB, s=8)
                            rows = slice(g, g + 1) if isinstance(g, int) else bass.ds(g, 1)
                            src = src[c, b, rows, :, :, :].rearrange("c r s a -> (c r) s a")
                            sp.dma_start(k_in[:, c, b * NA:(b + 1) * NA], src).then_inc(ld_k, 16)

                def keep_x(g, s):
                    sp.wait_ge(xn_ready, CH * (g + 1))
                    sp.dma_start(x_res[:, s, :, :], xn[:, :, :]).then_inc(copied_x, 16)

                def keep_k(g, s):
                    sp.wait_ge(ld_k, CH * NB * 16 * (g + 1))
                    sp.dma_start(k_res[:, s, :, :], k_in[:, :, :]).then_inc(copied_k, 16)

                def store(g):
                    rows = slice(g * GT, (g + 1) * GT) if isinstance(g, int) else bass.ds(g * GT, GT)
                    sp.wait_ge(h1_ready, g + 1)
                    sp.dma_start(h1_scr[rows, :].rearrange("(c p) d -> p c d", p=P), h1[:, :, :]).then_inc(h1_stored, 16)
                    sp.wait_ge(xt_ready, CH * (g + 1))
                    sp.dma_start(xt_scr[rows, :].rearrange("(c p) d -> p c d", p=P), xt[:, :, :]).then_inc(xt_stored, 16)

                def step(g, s):
                    if not (isinstance(g, int) and g == 0):
                        sp.wait_ge(tu_dve, NTD * g)
                        keep_x(g + 1, 1 - s)
                        sp.wait_ge(h1_ready, g)
                        apart(sp)
                        keep_k(g + 1, 1 - s)
                    else:
                        keep_x(g + 1, 1 - s)
                        keep_k(g + 1, 1 - s)
                    if not (isinstance(g, int) and g == GROUPS - 2):
                        load(g + 2)
                    if not (isinstance(g, int) and g == 0):
                        store(g - 1)

                load(0)
                keep_x(0, 0)
                keep_k(0, 0)
                load(1)
                step(0, 0)
                with sp.Fori(0, GROUPS // 2 - 2) as i:
                    step(2 * i + 1, 1)
                    step(2 * i + 2, 0)
                step(GROUPS - 3, 1)
                step(GROUPS - 2, 0)
                store(GROUPS - 2)
                store(GROUPS - 1)
                sp.wait_ge(h1_stored, GROUPS * 16)
                sp.wait_ge(xt_stored, GROUPS * 16)

            @block.gpsimd
            def _(pool):
                g_ = nc.gpsimd
                g_.memset(xin[:, :, 0:TAPS - 1], 0.0).then_inc(edge_ready, 1)

                def chained(ins, count):
                    ins.then_inc(pool_step, 1)
                    pool.wait_ge(pool_step, count)

                def inverse_root(which, ready, value, done):
                    pool.wait_ge(ready, value)
                    apart(pool)
                    g_.tensor_scalar(rstd[which][:, :], mv[which][:, :, 1], EPS, 1.0, ALU.add, ALU.mult).then_inc(rstd_step[which], 1)
                    pool.wait_ge(rstd_step[which], value)
                    g_.tensor_tensor(rstd[which][:, :], rstd[which][:, :], half_neg[:, 0:CH], ALU.pow).then_inc(done, 1)

                def bx_of(g, s, n):
                    it = g * NS + n
                    wait(pool, bt_ready, 2 * (it - 3))
                    if n == 0:
                        pool.wait_ge(pu_took, NPU * (g + 1))
                    apart(pool)
                    for c in range(CH):
                        g_.tensor_scalar(bx[:, n % 4, c, :], dtxt[:, s, c, :], bc[:, s, c, n + 1:n + 2], 1.0,
                                         ALU.mult, ALU.mult).then_inc(bx_ready, 1)

                def yp_of(g, s, n):
                    if n % 2 and n > 1:
                        i = n // 2
                        pool.wait_ge(cy_ready, NY1 * g + i + 1)
                        wait(pool, yp_added, NYP * g + i - 1)
                        g_.tensor_tensor(yp[:, s, :], yp[:, s, :], cy[:, i % 2, :], ALU.add).then_inc(yp_added, 1)

                def scan(g, s, n, first, last):
                    if n < NS - 2:
                        bx_of(g, s, n + 2)
                    elif not last:
                        bx_of(g + 1, 1 - s, n + 2 - NS)
                    if n >= 2:
                        yp_of(g, s, n - 2)
                    elif not first:
                        yp_of(g - 1, 1 - s, n - 2 + NS)

                def project(g, s, n):
                    if n == 0:
                        inverse_root(0, mvp_ready, g + 1, rstdp_ready)
                    if n in (3, 4):
                        kk = n - 3
                        wait(pool, conv_ready, 2 * g)
                        wait(pool, xc_ready, 2 * g)
                        if kk == 0:
                            pool.wait_ge(edge_ready, 2)
                        pool.wait_ge(pu_took, NPU * g + pu_index(f"xin{kk}") + 1)
                        apart(pool)
                        for k in (2 * kk, 2 * kk + 1):
                            g_.tensor_scalar(cv[:, k, :], xin[:, k, 1:1 + GT], conv_w[:, k, 0:1], par[:, k, 4:5],
                                             ALU.mult, ALU.add).then_inc(tap0_ready, 1)
                    if n == W_TURN - 1:
                        pool.wait_ge(u_ready, g + 1)
                        apart(pool)
                        g_.tensor_scalar(ww[:, :, :], uu[:, :, :], 1.0, 1.0, ALU.add, ALU.mult).then_inc(one_u_ready, 1)
                    if n == W_TURN + 1:
                        pool.wait_ge(dt_ready, g + 1)
                        g_.tensor_tensor(dtx[:, :, :], dt[:, s, :, :], xc[:, s, :, :], ALU.mult).then_inc(dtx_ready, 1)

                def finish(g, s, n):
                    if n == 1:
                        pool.wait_ge(y1_added, NY1 * (g + 1))
                        pool.wait_ge(yp_added, NYP * (g + 1))
                        g_.tensor_tensor(yt[:, s, 1, :], yt[:, s, 1, :], yp[:, s, :], ALU.add).then_inc(merged, 1)
                    if n == 3:
                        pool.wait_ge(tu_dve, NTD * g + 2)
                        g_.tensor_tensor(yg[:, :, :], yg[:, :, :], zs[:, s, :, :], ALU.mult).then_inc(gated, 1)
                    if n == 5:
                        inverse_root(1, mvt_ready, 2 * g + 1, rstdt_ready)
                    if n == 6:
                        pool.wait_ge(ln2_ready, g + 1)
                        pool.wait_ge(copied_k, 16 * (g + 1))
                        chained(g_.tensor_tensor(o[:, :, :], o[:, :, :], ln_bc[:, 0:1, :].broadcast_to([P, CH, L]), ALU.mult), 2 * g + 1)
                        chained(g_.tensor_tensor(o[:, :, :], o[:, :, :], ln_bc[:, 1:2, :].broadcast_to([P, CH, L]), ALU.add), 2 * g + 2)
                        wait(pool, h1_stored, 16 * g)
                        g_.tensor_tensor(h1[:, :, :], o[:, :, :], k_res[:, s, :, :], ALU.add).then_inc(h1_ready, 1)
                    if n == 7:
                        inverse_root(1, mvt_ready, 2 * g + 2, rstdt_ready)

                def flush(g, s, front):
                    if front:
                        bx_of(0, 0, 0)
                        bx_of(0, 0, 1)
                    else:
                        yp_of(g, s, NS - 1)

                steps(pool, scan, project, finish, flush)

            @block.scalar
            def _(act):
                a = nc.scalar.activation

                def da_of(g, s, n):
                    it = g * NS + n
                    if n == 0:
                        act.wait_ge(dt_ready, g + 1)
                    for k in range(KD):
                        if k % 2 == 0:
                            wait(act, scanned, 2 * (it - 4) + k // 2 + 1)
                        ins = a(da[:, n % 4, k, :], dt[:, s, k, :], ACT.Exp, scale=neg_a[:, k, n:n + 1])
                        if k % 2:
                            ins.then_inc(da_ready, 1)

                def cy_of(g, s, n):
                    if n % 2:
                        i = n // 2
                        act.wait_ge(ht_ready, 2 * (g * NS + n) + 2)
                        if i == 0:
                            dst = yp[:, s, :]
                        else:
                            wait(act, yp_added, NYP * g + max(i - 2, 0))
                            dst = cy[:, i % 2, :]
                        a(dst, bank[5][:, :], ACT.Copy, scale=bc[:, s, 1, n + 1 + NS:n + 2 + NS]).then_inc(cy_ready, 1)

                def scan(g, s, n, first, last):
                    if n < NS - 1:
                        da_of(g, s, n + 1)
                    elif not last:
                        da_of(g + 1, 1 - s, 0)
                    if n >= 1:
                        cy_of(g, s, n - 1)
                    elif not first:
                        cy_of(g - 1, 1 - s, NS - 1)

                def project(g, s, n):
                    def unit(name):
                        act.wait_ge(pu_ready, NPU * g + pu_index(name) + 1)

                    if n == 1:
                        unit("xnt")
                        a(xnt[:, :, :], P_BANK[:, :].rearrange("p (j t) -> p j t", j=KL), ACT.Copy).then_inc(pu_took, 1)
                        if isinstance(g, int) and g == 0:
                            a(xin[:, :, TAPS - 1], xin_cls[:, :], ACT.Copy).then_inc(edge_ready, 1)
                    if n in (2, 3):
                        kk = n - 2
                        unit(f"xin{kk}")
                        wait(act, conv_ready, 2 * g)
                        a(xin[:, 2 * kk:2 * kk + 2, TAPS:], P_BANK[:, :].rearrange("p (k t) -> p k t", k=2), ACT.Copy).then_inc(pu_took, 1)
                    if n in (4, 5):
                        kk = n - 4
                        act.wait_ge(conv_ready, 2 * g + kk + 1)
                        a(xc[:, s, 2 * kk:2 * kk + 2, :], cv[:, 2 * kk:2 * kk + 2, :], ACT.Silu).then_inc(xc_ready, 1)
                        unit(f"z{kk}")
                        a(zs[:, s, 2 * kk:2 * kk + 2, :], P_BANK[:, :].rearrange("p (k t) -> p k t", k=2), ACT.Silu).then_inc(pu_took, 1)
                    if n == 6:
                        unit("xd")
                        a(xdt[:, :], P_BANK[0:XD, 0:GT], ACT.Copy).then_inc(pu_took, 1)
                    if n in (7, 8):
                        kk = n - 7
                        unit(f"dtv{kk}")
                        wait(act, dt_ready, g)
                        for i in range(2):
                            k = 2 * kk + i
                            a(absv[:, k, :], P_BANK[:, i * GT:(i + 1) * GT], ACT.Abs, bias=par[:, k, 6:7]).then_inc(absv_ready, 1)
                            ins = a(relv[:, k, :], P_BANK[:, i * GT:(i + 1) * GT], ACT.Relu, bias=par[:, k, 6:7])
                        ins.then_inc(pu_took, 1)
                    if n == 8:
                        act.wait_ge(absv_ready, KD * (g + 1))
                        a(uu[:, :, :], absv[:, :, :], ACT.Exp, scale=-1.0).then_inc(u_ready, 1)
                    if n == 9:
                        unit("bc")
                        a(bc[:, s, :, :], P_BANK[:, 0:CH * XD].rearrange("p (c m) -> p c m", c=CH), ACT.Copy).then_inc(pu_took, 1)
                        act.wait_ge(one_u_ready, g + 1)
                        a(lw[:, :, :], ww[:, :, :], ACT.Ln).then_inc(lnw_ready, 1)
                    if n in (12, 13):
                        c = n - 12
                        unit(f"dtxt{c}")
                        a(dtxt[:, s, c, :], P_BANK[:, :], ACT.Copy).then_inc(pu_took, 1)

                def finish(g, s, n):
                    if n == 9:
                        act.wait_ge(tu_ready, NTU * g + 4)
                        a(xtt[:, :, :], T_BANK[:, :].rearrange("p (j t) -> p j t", j=KL), ACT.Copy).then_inc(tu_act, 1)
                    if n == 10:
                        act.wait_ge(tu_ready, NTU * g + 5)
                        rows = slice(CH * g, CH * g + CH) if isinstance(g, int) else bass.ds(CH * g, CH)
                        a(logits[:, rows, :], T_BANK[:, 0:CH * NE].rearrange("p (c m) -> p c m", c=CH), ACT.Copy).then_inc(tu_act, 1)

                def flush(g, s, front):
                    if front:
                        da_of(0, 0, 0)
                    else:
                        cy_of(g, s, NS - 1)

                steps(act, scan, project, finish, flush)

            @block.vector
            def _(dve):
                v = nc.vector

                def stats(which, src, chain, count, done):
                    for c in range(CH):
                        ins = v.bn_stats(st[which][:, c, :], src[:, c, :])
                    ins.then_inc(chain, 1)
                    dve.wait_ge(chain, count)
                    apart(dve)
                    for c in range(CH):
                        ins = v.bn_aggr(mv[which][:, c, :], st[which][:, c, :])
                    ins.then_inc(done, 1)

                def norm(which, dst, src, c):
                    return v.tensor_scalar(dst[:, c, :], src[:, c, :], mv[which][:, c, 0:1], rstd[which][:, c:c + 1],
                                           ALU.subtract, ALU.mult)

                def scan_of(g, s, n):
                    it = g * NS + n
                    wait(dve, ht_ready, 2 * (it - 1))
                    for k in range(KD):
                        if k % 2 == 0:
                            dve.wait_ge(bt_ready, 2 * it + k // 2 + 1)
                            dve.wait_ge(da_ready, 2 * it + k // 2 + 1)
                        ins = v.tensor_tensor_scan(hs[:, n % 2, k, :], da[:, n % 4, k, :],
                                                   bank[2 * (n % 2) + k // 2][:, (k % 2) * GT:(k % 2 + 1) * GT],
                                                   h0[:, k, n:n + 1], ALU.mult, ALU.add)
                        if k % 2:
                            ins.then_inc(scanned, 1)

                def add_of(g, s, n):
                    it = g * NS + n
                    for c in range(CH):
                        if c == 1 and n % 2:
                            continue
                        dve.wait_ge(ht_ready, 2 * it + c + 1)
                        scale = bc[:, s, c, n + 1 + NS:n + 2 + NS]
                        done = (y0_added, y1_added)[c]
                        if n == 0:
                            ins = v.tensor_scalar(yt[:, s, c, :], bank[4 + c][:, :], scale, None, ALU.mult)
                        else:
                            dve.wait_ge(done, it if c == 0 else NY1 * g + n // 2)
                            ins = v.scalar_tensor_tensor(yt[:, s, c, :], bank[4 + c][:, :], scale, yt[:, s, c, :], ALU.mult, ALU.add)
                        ins.then_inc(done, 1)

                def scan(g, s, n, first, last):
                    scan_of(g, s, n)
                    if n >= 1:
                        add_of(g, s, n - 1)
                    elif not first:
                        add_of(g - 1, 1 - s, NS - 1)

                def project(g, s, n):
                    if n == 0:
                        dve.wait_ge(ld_k, (g + 1) * CH * NB * 16)
                        stats(0, k_in, dve_p, DVE_P_STEPS * g + 1, mvp_ready)
                    if n == 1:
                        wait(dve, copied_x, 16 * g)
                        wait(dve, pu_took, NPU * (g - 1) + 1)
                        dve.wait_ge(rstdp_ready, g + 1)
                        for c in range(CH):
                            norm(0, xn, k_in, c).then_inc(xn_ready, 1)
                    if n in (3, 4):
                        kk = n - 3
                        dve.wait_ge(tap0_ready, KD * g + 2 * kk + 2)
                        for tap in range(1, TAPS):
                            for k in (2 * kk, 2 * kk + 1):
                                ins = v.scalar_tensor_tensor(cv[:, k, :], xin[:, k, 1 + tap:1 + tap + GT], conv_w[:, k, tap:tap + 1],
                                                             cv[:, k, :], ALU.mult, ALU.add)
                            if tap < TAPS - 1:
                                ins.then_inc(dve_p, 1)
                                dve.wait_ge(dve_p, DVE_P_STEPS * g + 1 + 2 * kk + tap)
                        ins.then_inc(conv_ready, 1)
                    if n == W_TURN:
                        dve.wait_ge(one_u_ready, g + 1)
                        v.scalar_tensor_tensor(absv[:, :, :], ww[:, :, :], -1.0, uu[:, :, :], ALU.add, ALU.subtract).then_inc(w_fix, 1)
                        dve.wait_ge(w_fix, g + 1)
                        dve.wait_ge(lnw_ready, g + 1)
                        v.tensor_tensor(lw[:, :, :], lw[:, :, :], absv[:, :, :], ALU.subtract).then_inc(lw_fixed, 1)
                        dve.wait_ge(lw_fixed, g + 1)
                        v.tensor_tensor(dt[:, s, :, :], lw[:, :, :], relv[:, :, :], ALU.add).then_inc(dt_ready, 1)

                def finish(g, s, n):
                    if n in (1, 2):
                        kk = n - 1
                        dve.wait_ge(tu_ready, NTU * g + kk + 1)
                        for i in range(2):
                            k = 2 * kk + i
                            ins = v.scalar_tensor_tensor(yg[:, k, :], xc[:, s, k, :], par[:, k, 7:8], T_BANK[:, i * GT:(i + 1) * GT],
                                                         ALU.mult, ALU.add)
                        ins.then_inc(tu_dve, 1)
                    if n == 4:
                        dve.wait_ge(tu_ready, NTU * g + 3)
                        dve.wait_ge(copied_x, 16 * (g + 1))
                        v.tensor_tensor(o[:, :, :], T_BANK[:, :].rearrange("p (c d) -> p c d", c=CH), x_res[:, s, :, :],
                                        ALU.add).then_inc(tu_dve, 1)
                        dve.wait_ge(tu_dve, NTD * (g + 1))
                        stats(1, o, dve_t, DVE_T_STEPS * g + 1, mvt_ready)
                    if n == 5:
                        dve.wait_ge(rstdt_ready, 2 * g + 1)
                        for c in range(CH):
                            ins = norm(1, o, o, c)
                        ins.then_inc(ln2_ready, 1)
                    if n == 7:
                        dve.wait_ge(h1_ready, g + 1)
                        stats(1, h1, dve_t, DVE_T_STEPS * g + 2, mvt_ready)
                    if n == 8:
                        wait(dve, xt_stored, 16 * g)
                        dve.wait_ge(rstdt_ready, 2 * g + 2)
                        for c in range(CH):
                            norm(1, xt, h1, c).then_inc(xt_ready, 1)

                def flush(g, s, front):
                    if not front:
                        add_of(g, s, NS - 1)

                steps(dve, scan, project, finish, flush)

            @block.tensor
            def _(pe):
                mm = nc.tensor.matmul

                def to_channels(g, s, n):
                    it = g * NS + n
                    pe.wait_ge(bx_ready, CH * (it + 1))
                    for kk in range(2):
                        b = bank[2 * (n % 2) + kk]
                        wait(pe, scanned, 2 * (it - 2) + kk + 1)
                        for i in range(2):
                            for c in range(CH):
                                k = 2 * kk + i
                                last = nc.tensor.transpose(b[:, i * GT + c * P:i * GT + (c + 1) * P],
                                                           bx[:, n % 4, c, k * P:(k + 1) * P], ident[:, :])
                        last.then_inc(bt_ready, 1)

                def to_time(g, s, n):
                    it = g * NS + n
                    pe.wait_ge(scanned, 2 * (it + 1))
                    for c in range(CH):
                        if c == 0:
                            wait(pe, y0_added, it)
                        elif n % 2:
                            pe.wait_ge(y1_added, NY1 * g + n // 2 + 1)
                        else:
                            wait(pe, cy_ready, NY1 * g + n // 2)
                        for k in range(KD):
                            last = nc.tensor.transpose(bank[4 + c][:, k * P:(k + 1) * P], hs[:, n % 2, k, c * P:(c + 1) * P], ident[:, :])
                        last.then_inc(ht_ready, 1)

                def scan(g, s, n, first, last):
                    if n >= 1:
                        to_time(g, s, n - 1)
                    elif not first:
                        to_time(g - 1, 1 - s, NS - 1)
                    if n < NS - 1:
                        to_channels(g, s, n + 1)
                    elif not last:
                        to_channels(g + 1, 1 - s, 0)

                def project(g, s, n):
                    def room(name):
                        wait(pe, pu_took, NPU * g + pu_index(name))

                    if n == 1:
                        room("xnt")
                        for c in range(CH):
                            pe.wait_ge(xn_ready, CH * g + c + 1)
                            for j in range(KL):
                                last = nc.tensor.transpose(P_BANK[:, j * GT + c * P:j * GT + (c + 1) * P],
                                                           xn[:, c, j * P:(j + 1) * P], ident[:, :])
                        last.then_inc(pu_ready, 1)
                    if n in (2, 3, 4, 5):
                        kk, at = n % 2, (0 if n < 4 else DI)
                        name = ("xin" if n < 4 else "z") + str(kk)
                        room(name)
                        for i in range(2):
                            for j in range(KL):
                                cols = slice(at + (2 * kk + i) * P, at + (2 * kk + i + 1) * P)
                                last = mm(P_BANK[:, i * GT:(i + 1) * GT], win[:, j, cols], xnt[:, j, :], start=(j == 0), stop=(j == KL - 1))
                        last.then_inc(pu_ready, 1)
                    if n == 6:
                        room("xd")
                        pe.wait_ge(xc_ready, 2 * (g + 1))
                        for k in range(KD):
                            last = mm(P_BANK[0:XD, 0:GT], wxp[:, k, :], xc[:, s, k, :], start=(k == 0), stop=(k == KD - 1))
                        last.then_inc(pu_ready, 1)
                    if n in (7, 8):
                        kk = n - 7
                        room(f"dtv{kk}")
                        for i in range(2):
                            k = 2 * kk + i
                            last = mm(P_BANK[:, i * GT:(i + 1) * GT], dtw[0:1, k * P:(k + 1) * P], xdt[0:1, :], start=True, stop=True)
                        last.then_inc(pu_ready, 1)
                    if n == 9:
                        room("bc")
                        apart(pe)
                        for c in range(CH):
                            last = nc.tensor.transpose(P_BANK[:, c * XD:(c + 1) * XD], xdt[:, c * P:(c + 1) * P], ident[0:XD, 0:XD])
                        last.then_inc(pu_ready, 1)
                    if n in (12, 13):
                        c = n - 12
                        room(f"dtxt{c}")
                        pe.wait_ge(dtx_ready, g + 1)
                        for k in range(KD):
                            last = nc.tensor.transpose(P_BANK[:, k * P:(k + 1) * P], dtx[:, k, c * P:(c + 1) * P], ident[:, :])
                        last.then_inc(pu_ready, 1)

                def finish(g, s, n):
                    if n in (1, 2):
                        kk = n - 1
                        if kk == 0:
                            wait(pe, tu_act, NTA * g)
                            pe.wait_ge(y0_added, NS * (g + 1))
                            pe.wait_ge(merged, g + 1)
                        else:
                            pe.wait_ge(tu_dve, NTD * g + 1)
                        for i in range(2):
                            for c in range(CH):
                                k = 2 * kk + i
                                last = nc.tensor.transpose(T_BANK[:, i * GT + c * P:i * GT + (c + 1) * P],
                                                           yt[:, s, c, k * P:(k + 1) * P], ident[:, :])
                        last.then_inc(tu_ready, 1)
                    if n == 4:
                        pe.wait_ge(tu_dve, NTD * g + 2)
                        pe.wait_ge(gated, g + 1)
                        for c in range(CH):
                            for k in range(KD):
                                last = mm(T_BANK[:, c * L:(c + 1) * L], yg[:, k, c * P:(c + 1) * P], wout[:, k, :],
                                          start=(k == 0), stop=(k == KD - 1))
                        last.then_inc(tu_ready, 1)
                    if n == 9:
                        pe.wait_ge(tu_dve, NTD * (g + 1))
                        for c in range(CH):
                            pe.wait_ge(xt_ready, CH * g + c + 1)
                            for j in range(KL):
                                last = nc.tensor.transpose(T_BANK[:, j * GT + c * P:j * GT + (c + 1) * P],
                                                           xt[:, c, j * P:(j + 1) * P], ident[:, :])
                        last.then_inc(tu_ready, 1)
                    if n == 10:
                        pe.wait_ge(tu_act, NTA * g + 1)
                        for c in range(CH):
                            for j in range(KL):
                                last = mm(T_BANK[:, c * NE:(c + 1) * NE], xtt[:, j, c * P:(c + 1) * P], wg[:, j, :],
                                          start=(j == 0), stop=(j == KL - 1))
                        last.then_inc(tu_ready, 1)

                def flush(g, s, front):
                    if front:
                        to_channels(0, 0, 0)
                    else:
                        to_time(g, s, NS - 1)

                steps(pe, scan, project, finish, flush)

        stage = ExitStack()
        with stage:
            def sa(name, shape, dt=F32):
                return sb(name, shape, dt, stage)

            NT = 17
            xts = sa("xts", [P, 16, L])
            h1s = sa("h1s", [P, 16, L])
            top = sa("top", [P, NT, 8])
            topi = sa("topi", [P, NT, 8], U32)
            ef = sa("ef", [P, NT, 2])
            oh = sa("oh", [P, NT, 2, NE])
            ohb = sa("ohb", [P, NT, 2, NE], BF16)
            trib = sa("trib", [P, P], BF16)
            oneb = sa("oneb", [P, P], BF16)
            base = sa("base", [P, NT, 2, NE])
            cbase = sa("cbase", [P, NSEQ, 2, NE])
            run = sa("run", [P, 25, 2, NE])
            rank = sa("rank", [P, NT, 2, NE])
            rk = sa("rk", [P, NT, 2])
            keep = sa("keep", [P, NT, 2])
            slot_f = sa("slot_f", [P, NT, 2])
            drop = sa("drop", [P, NT, 2])
            gidx = sa("gidx", [P, NT, 2], U32)
            sidx = sa("sidx", [P, NT, 2], U32)
            ee = sa("ee", [P, NT])
            pw = sa("pw", [P, NT, 2])
            xr = sa("xr", [SLOT_P, 2, SLOT_M, L])
            w1 = sa("w1", [P, 2, KL, FF])
            w2 = sa("w2", [P, 2, FF // P, L])
            xet = sa("xet", [P, 2, KL, PITCH])
            ht = sa("ht", [P, FF // P, PITCH])
            eo = sa("eo", [SLOT_P, 2, SLOT_M, L])
            ga = sa("ga", [P, 4, 2, L])
            KF = FF // P
            HALF = CAP // 2

            (ld_rows0, ld_rows1, ld_w10, ld_w11, ld_w20, ld_w21, tok_loaded, h1_loaded, rt_step, oh_ready, counts_ready, ee_in, ee_ready, idx_ready,
             w_ready, scattered, pad_ready, tr_ready, tr_taken, up_ready, gelu_done, down_ready, eo_taken, eo_stored0, eo_stored1,
             gath0, gath1, gath2, gath3, mixed, out_stored, mix_step) = sems(
                "ld_rows0 ld_rows1 ld_w10 ld_w11 ld_w20 ld_w21 tok_loaded h1_loaded rt_step oh_ready counts_ready ee_in ee_ready idx_ready w_ready "
                "scattered pad_ready tr_ready tr_taken up_ready gelu_done down_ready eo_taken eo_stored0 eo_stored1 gath0 gath1 gath2 gath3 "
                "mixed out_stored mix_step")
            ld_rows, ld_w1, ld_w2, eo_stored = [ld_rows0, ld_rows1], [ld_w10, ld_w11], [ld_w20, ld_w21], [eo_stored0, eo_stored1]
            gathered = [gath0, gath1, gath2, gath3]
            block = stage.enter_context(nc.Block("experts"))
            pairs = NE // 2

            def experts(eng, body):
                body(0, 0)
                body(1, 1)
                with eng.Fori(1, pairs) as i:
                    body(2 * i, 0)
                    body(2 * i + 1, 1)

            def rows_of(e, n):
                return slice(e * n, (e + 1) * n) if isinstance(e, int) else bass.ds(e * n, n)

            @block.sync
            def _(sp):
                sp.dma_start(xts[:, :, :], xt_scr.rearrange("(j p) d -> p j d", p=P)).then_inc(tok_loaded, 16)
                sp.dma_start(h1s[:, :, :], h1_scr.rearrange("(j p) d -> p j d", p=P)).then_inc(h1_loaded, 16)
                fc, pj = c_fc.rearrange("e l f -> (e l) f"), c_proj.rearrange("e f d -> (e f) d")

                def load(e, s):
                    wait(sp, up_ready, 16 * (e - 1))
                    sp.dma_start(w1[:, s, :, :], fc[rows_of(e, L), :].rearrange("(j p) f -> p j f", p=P)).then_inc(ld_w1[s], 16)
                    wait(sp, down_ready, SLOT_M * (e - 1))
                    sp.dma_start(w2[:, s, :, :], pj[rows_of(e, FF), :].rearrange("(k p) d -> p k d", p=P)).then_inc(ld_w2[s], 16)
                    if isinstance(e, int) and e == 0:
                        sp.wait_ge(scattered, 2 * NT * 16)
                    wait(sp, tr_ready, 4 * (e - 1))
                    sp.dma_start(xr[:, s, :, :], xe_scr[rows_of(e, PITCH), :].rearrange("(m p) d -> p m d", p=SLOT_P)).then_inc(ld_rows[s], 16)

                experts(sp, load)
                for j in range(NT):
                    sp.wait_ge(mixed, j + 1)
                    if j < 16:
                        to, of = out[j // 2, 1 + (j % 2) * P:1 + (j % 2 + 1) * P, :], h1s[:, j, :]
                    else:
                        to, of = out[:, 0, :], h1_cls[0:NSEQ, :]
                    sp.dma_start(to, of).then_inc(out_stored, 16)
                sp.wait_ge(out_stored, NT * 16)

            @block.scalar
            def _(act):
                act.wait_ge(ee_in, 1)
                nc.scalar.activation(ee[:, :], ee[:, :], ACT.Exp).then_inc(ee_ready, 1)

                def gelu(e, s):
                    for f in range(KF):
                        if f == 0:
                            wait(act, down_ready, SLOT_M * e)
                        for h in range(2):
                            act.wait_ge(up_ready, 16 * e + 2 * f + h + 1)
                            nc.scalar.activation(ht[:, f, h * HALF:(h + 1) * HALF], bank[2 + (2 * f + h) % 4][:, 0:HALF],
                                                 ACT.Gelu).then_inc(gelu_done, 1)
                    act.wait_ge(eo_taken, SLOT_M * (e + 1))
                    act.dma_start(eo_scr[rows_of(e, PITCH), :].rearrange("(m p) d -> p m d", p=SLOT_P), eo[:, s, :, :])\
                        .then_inc(eo_stored[s], 16)

                experts(act, gelu)

            @block.vector
            def _(dve):
                v = nc.vector
                own = [0]

                def step(ins):
                    own[0] += 1
                    ins.then_inc(rt_step, 1)
                    dve.wait_ge(rt_step, own[0])

                v.memset(oneb[:, :], 1.0)
                v.tensor_copy(trib[:, :], tri[:, :])
                for j in range(NT):
                    ins = v.max(top[:, j, :], logits[:, j, :])
                step(ins)
                for j in range(NT):
                    ins = v.max_index(topi[:, j, :], top[:, j, :], logits[:, j, :])
                step(ins)
                v.tensor_tensor(ee[:, :], top[:, :, 1], top[:, :, 0], ALU.subtract).then_inc(ee_in, 1)
                step(v.tensor_copy(ef[:, :, :], topi[:, :, 0:2]))
                step(v.tensor_tensor(oh[:, :, :, :], iota8[:, :].unsqueeze(1).unsqueeze(1).broadcast_to([P, NT, 2, NE]),
                                     ef[:, :, :].unsqueeze(3).broadcast_to([P, NT, 2, NE]), ALU.is_equal))
                v.tensor_copy(ohb[:, :, :, :], oh[:, :, :, :]).then_inc(oh_ready, 1)
                dve.wait_ge(ee_ready, 1)
                step(v.tensor_scalar(keep[:, :, 0], ee[:, :], 1.0, None, ALU.add))
                step(v.reciprocal(pw[:, :, 0], keep[:, :, 0]))
                step(v.tensor_tensor(pw[:, :, 1], ee[:, :], pw[:, :, 0], ALU.mult))
                dve.wait_ge(counts_ready, 1)
                count = bank[0][:, 0:16 * 2 * NE].rearrange("p (j k e) -> p j k e", j=16, k=2)
                prefix = bank[1][:, 0:16 * 2 * NE].rearrange("p (j k e) -> p j k e", j=16, k=2)
                step(v.memset(run[:, 0, :, :], 0.0))
                r = 0
                for q in range(NSEQ):
                    v.tensor_copy(cbase[:, q, :, :], run[:, r, :, :])
                    step(v.tensor_tensor(run[:, r + 1, :, :], run[:, r, :, :], oh[:, 16, :, :], ALU.add))
                    for half in range(2):
                        r += 1
                        v.tensor_copy(base[:, 2 * q + half, :, :], run[:, r, :, :])
                        step(v.tensor_tensor(run[:, r + 1, :, :], run[:, r, :, :], count[:, 2 * q + half, :, :], ALU.add))
                    r += 1
                step(v.memset(base[:, 16, :, :], 0.0))
                for q in range(NSEQ):
                    step(v.scalar_tensor_tensor(base[:, 16, :, :], cbase[:, q, :, :], ident[:, q:q + 1], base[:, 16, :, :],
                                                ALU.mult, ALU.add))
                v.tensor_copy(rank[:, 16, :, :], base[:, 16, :, :])
                step(v.tensor_tensor(rank[:, 0:16, :, :], prefix, base[:, 0:16, :, :], ALU.add))
                step(v.tensor_tensor(rank[:, :, 1, :], rank[:, :, 1, :], run[:, r, 0:1, :].broadcast_to([P, NT, NE]), ALU.add))
                step(v.tensor_tensor(rank[:, :, :, :], rank[:, :, :, :], oh[:, :, :, :], ALU.mult))
                step(v.tensor_reduce(rk[:, :, :], rank[:, :, :, :], AX.X, ALU.add))
                v.tensor_scalar(keep[:, :, :], rk[:, :, :], float(CAP), None, ALU.is_lt)
                step(v.scalar_tensor_tensor(slot_f[:, :, :], ef[:, :, :], float(PITCH), rk[:, :, :], ALU.mult, ALU.add))
                v.tensor_scalar(drop[:, :, :], keep[:, :, :], -OUT_OF_RANGE, OUT_OF_RANGE, ALU.mult, ALU.add)
                step(v.tensor_tensor(slot_f[:, :, :], slot_f[:, :, :], keep[:, :, :], ALU.mult))
                v.tensor_copy(gidx[:, :, :], slot_f[:, :, :])
                step(v.tensor_tensor(drop[:, :, :], drop[:, :, :], slot_f[:, :, :], ALU.add))
                v.tensor_copy(sidx[:, :, :], drop[:, :, :]).then_inc(idx_ready, 1)
                v.tensor_tensor(pw[:, :, :], pw[:, :, :], keep[:, :, :], ALU.mult).then_inc(w_ready, 1)
                v.memset(ht[:, :, CAP:PITCH], 0.0).then_inc(pad_ready, 1)
                WIDE = SLOT_P * SLOT_M // 2

                def evacuate(e, s):
                    for i in range(4):
                        j, h = i % 2, i // 2
                        dve.wait_ge(tr_ready, 4 * e + i + 1)
                        if i == 0:
                            wait(dve, up_ready, 16 * (e - 1))
                        v.tensor_copy(xet[:, s, j, h * WIDE:(h + 1) * WIDE], bank[i % 2][:, 0:WIDE]).then_inc(tr_taken, 1)

                def outputs(e, s):
                    wait(dve, eo_stored[s], 8 * (e - s))
                    for m in range(SLOT_M):
                        dve.wait_ge(down_ready, SLOT_M * e + m + 1)
                        v.tensor_copy(eo[:, s, m, :], bank[6 + m % 2][0:SLOT_P, 0:L]).then_inc(eo_taken, 1)

                evacuate(0, 0)
                evacuate(1, 1)
                outputs(0, 0)
                with dve.Fori(0, pairs - 1) as i:
                    evacuate(2 * i + 2, 0)
                    outputs(2 * i + 1, 1)
                    evacuate(2 * i + 3, 1)
                    outputs(2 * i + 2, 0)
                outputs(NE - 1, 1)
                for j in range(NT):
                    n = P if j < 16 else NSEQ
                    src = h1s[:, j, :] if j < 16 else h1_cls[0:NSEQ, :]
                    dve.wait_ge(gathered[j % 4], 32 * (j // 4 + 1))
                    if j == 0:
                        dve.wait_ge(h1_loaded, 16)
                        dve.wait_ge(w_ready, 1)
                    v.scalar_tensor_tensor(src, ga[0:n, j % 4, 0, :], pw[0:n, j, 0:1], src, ALU.mult, ALU.add).then_inc(mix_step, 1)
                    dve.wait_ge(mix_step, j + 1)
                    v.scalar_tensor_tensor(src, ga[0:n, j % 4, 1, :], pw[0:n, j, 1:2], src, ALU.mult, ALU.add).then_inc(mixed, 1)

            @block.gpsimd
            def _(pool):
                pool.wait_ge(tok_loaded, 16)
                pool.wait_ge(idx_ready, 1)
                for j in range(NT):
                    n = P if j < 16 else NSEQ
                    src = xts[:, j, :] if j < 16 else xt_cls[0:NSEQ, :]
                    for k in range(2):
                        nc.gpsimd.indirect_dma_start(xe_scr, bass.IndirectOffsetOnAxis(ap=sidx[0:n, j, k:k + 1], axis=0), src, None,
                                                     bounds_check=NE * PITCH - 1, oob_is_err=False).then_inc(scattered, 16)
                for s in range(2):
                    pool.wait_ge(eo_stored[s], 8 * NE)
                for j in range(NT):
                    n = P if j < 16 else NSEQ
                    wait(pool, mixed, j - 3)
                    for k in range(2):
                        nc.gpsimd.indirect_dma_start(ga[0:n, j % 4, k, :], None, eo_scr,
                                                     bass.IndirectOffsetOnAxis(ap=gidx[0:n, j, k:k + 1], axis=0),
                                                     bounds_check=NE * PITCH - 1, oob_is_err=False).then_inc(gathered[j % 4], 16)

            @block.tensor
            def _(pe):
                mm = nc.tensor.matmul
                n = 16 * 2 * NE
                pe.wait_ge(oh_ready, 1)
                flat = ohb[:, 0:16, :, :].rearrange("p j k e -> p (j k e)")
                mm(bank[0][:, 0:n], oneb[:, :], flat, start=True, stop=True)
                mm(bank[1][:, 0:n], trib[:, :], flat, start=True, stop=True).then_inc(counts_ready, 1)
                pe.wait_ge(idx_ready, 1)

                def rows_in(e, s):
                    pe.wait_ge(ld_rows[s], 8 * (e - s) + 16)
                    for i in range(4):
                        j, h = i % 2, i // 2
                        wait(pe, tr_taken, 4 * e + i - 1)
                        for m in range(3):
                            last = nc.tensor.transpose(bank[i % 2][:, m * SLOT_P:(m + 1) * SLOT_P],
                                                       xr[:, s, 3 * h + m, j * P:(j + 1) * P], ident[0:SLOT_P, 0:SLOT_P])
                        last.then_inc(tr_ready, 1)

                def up(e, s):
                    pe.wait_ge(ld_w1[s], 8 * (e - s) + 16)
                    pe.wait_ge(tr_taken, 4 * (e + 1))
                    for f in range(KF):
                        for h in range(2):
                            i = 2 * f + h
                            wait(pe, gelu_done, 16 * e + i - 3)
                            for j in range(KL):
                                last = mm(bank[2 + i % 4][:, 0:HALF], w1[:, s, j, f * P:(f + 1) * P],
                                          xet[:, s, j, h * HALF:(h + 1) * HALF], start=(j == 0), stop=(j == KL - 1))
                            last.then_inc(up_ready, 1)

                def down(e, s):
                    pe.wait_ge(ld_w2[s], 8 * (e - s) + 16)
                    pe.wait_ge(gelu_done, 16 * (e + 1))
                    for m in range(SLOT_M):
                        wait(pe, eo_taken, SLOT_M * e + m - 1)
                        for f in range(KF):
                            last = mm(bank[6 + m % 2][0:SLOT_P, 0:L], ht[:, f, m * SLOT_P:(m + 1) * SLOT_P], w2[:, s, f, :],
                                      start=(f == 0), stop=(f == KF - 1))
                        last.then_inc(down_ready, 1)

                rows_in(0, 0)
                up(0, 0)
                rows_in(1, 1)
                pe.wait_ge(pad_ready, 1)
                down(0, 0)
                with pe.Fori(0, pairs - 1) as i:
                    up(2 * i + 1, 1)
                    rows_in(2 * i + 2, 0)
                    down(2 * i + 1, 1)
                    up(2 * i + 2, 0)
                    rows_in(2 * i + 3, 1)
                    down(2 * i + 2, 0)
                up(NE - 1, 1)
                down(NE - 1, 1)


_OUTS = [((NSEQ, HEADS + 1, L), 'float32')]


def kernel(**inputs):
    import numpy as _np
    import concourse.bacc as _bacc
    from concourse import mybir as _mybir
    from concourse.bass_utils import run_bass_kernel_spmd as _run

    i = {k: _np.asarray(v) for k, v in inputs.items()}

    def fold(a):
        return a.reshape(2, HEADS // 2, NST).transpose(0, 2, 1).reshape(P, HEADS // 2)

    def channels(a):
        return a.reshape((KD, P) + a.shape[1:]).swapaxes(0, 1)

    laid = {
        "x": i["x"].reshape(NSEQ, 2, HEADS // 2, NST, 2).transpose(1, 3, 4, 2, 0).reshape(P, 2, HEADS // 2, NSEQ),
        "s4": _np.stack([fold(i["L0_tok_inv_A_real"]), fold(i["L0_tok_A_imag"]), fold(i["L0_tok_B_ri"][..., 0]),
                         fold(i["L0_tok_B_ri"][..., 1]),
                         fold(_np.broadcast_to(i["L0_tok_log_dt"][:, None], (HEADS, NST)))], axis=1),
        "cls": i["cls_tok"].reshape(1, L),
        "w_in": i["L0_attn_in_proj_w"].T.reshape(KL, P, 2 * DI).transpose(1, 0, 2),
        "dpar": _np.concatenate([channels(i["L0_attn_conv_w"][:, 0, :]), channels(i["L0_attn_conv_b"][:, None]),
                                 channels(i["L0_attn_dt_proj_w"]), channels(i["L0_attn_dt_proj_b"][:, None]),
                                 channels(i["L0_attn_D"][:, None]), channels(i["L0_attn_A_log"])], axis=2),
        "dtw_row": i["L0_attn_dt_proj_w"].reshape(1, DI),
        "w_xp": channels(i["L0_attn_x_proj_w"].T),
        "w_out": channels(i["L0_attn_out_proj_w"].T),
        "ln_rows": _np.stack([i["L0_attn_ln_gamma"], i["L0_attn_ln_beta"]]),
        "w_g": i["L0_ffn_w_g"].reshape(KL, P, NE).transpose(1, 0, 2),
        "c_fc": i["L0_ffn_c_fc"],
        "c_proj": i["L0_ffn_c_proj"],
        "ident_in": _np.eye(P, dtype=_np.float32),
        "tri_in": _np.triu(_np.ones((P, P), _np.float32), 1),
        "iota_in": _np.arange(NE, dtype=_np.float32)[None, :],
    }
    nc = _bacc.Bacc("TRN2", target_bir_lowering=False, num_devices=1)
    arrays, args = {}, []
    for name, a in laid.items():
        a = _np.ascontiguousarray(a)
        arrays[f"in_{name}"] = a
        args.append(nc.dram_tensor(f"in_{name}", a.shape, _mybir.dt.from_np(a.dtype), kind="ExternalInput").ap())
    for n, (shape, dtype) in enumerate(_OUTS):
        dt = _mybir.dt.from_np(_np.dtype(dtype))
        args.append(nc.dram_tensor(f"out_{n}", shape, dt, kind="ExternalOutput").ap())
    vit_tower_kernel(nc, *args)
    r = _run(nc, [arrays], core_ids=[0])
    return r.results[0]["out_0"]
```

```python
import concourse.bass as bass
from concourse import mybir
from contextlib import ExitStack

F32 = mybir.dt.float32
F32R = mybir.dt.float32r
BF16 = mybir.dt.bfloat16
U32 = mybir.dt.uint32
ALU = mybir.AluOpType
ACT = mybir.ActivationFunctionType
AX = mybir.AxisListType

P = 128
NSEQ, HEADS, NST, L = 8, 256, 64, 256
DI, NS, TAPS = 512, 16, 4
KD, KL = DI // P, L // P
NE, FF = 8, 1024
T = NSEQ * (HEADS + 1)
CAP = int(2 * 1.25 * T / NE)
CAP += CAP % 2
SLOT_P, SLOT_M = 112, 6
PITCH = SLOT_P * SLOT_M
NA, NB = 64, L // 64
GROUPS, GT = NSEQ, HEADS
CH = GT // P
EPS = 1e-5
OUT_OF_RANGE = 16384.0
XD = 1 + 2 * NS


def wait(eng, sem, value):
    if isinstance(value, int) and value <= 0:
        return
    eng.wait_ge(sem, value)


def vit_tower_kernel(nc, x, s4, cls, w_in, dpar, dtw_row, w_xp, w_out, ln_rows, w_g, c_fc, c_proj,
                     ident_in, tri_in, iota_in, out):
    ctx = ExitStack()
    with ctx:
        def sem(name):
            return ctx.enter_context(nc.semaphore(name))

        def sb(name, shape, dt=F32, stack=ctx):
            return stack.enter_context(nc.sbuf_tensor(name, shape, dt))

        def sems(names):
            return [sem(n) for n in names.split()]

        bank = [ctx.enter_context(nc.psum_tensor(f"bank{i}", [P, 512], F32)) for i in range(8)]

        k_scr = nc.dram_tensor("k_scr", (8, P, 512), F32).ap()
        h1_scr = nc.dram_tensor("h1_scr", (NSEQ * HEADS, L), F32).ap()
        xt_scr = nc.dram_tensor("xt_scr", (NSEQ * HEADS, L), F32).ap()
        xe_scr = nc.dram_tensor("xe_scr", (NE * PITCH, L), F32).ap()
        eo_scr = nc.dram_tensor("eo_scr", (NE * PITCH, L), F32).ap()

        ident = sb("ident", [P, P])
        tri = sb("tri", [P, P])
        iota8 = sb("iota8", [P, NE])
        win = sb("win", [P, KL, 2 * DI])
        par = sb("par", [P, KD, 8 + NS])
        conv_w, conv_b, dt_w, dt_b, skip_d = par[:, :, 0:4], par[:, :, 4], par[:, :, 5], par[:, :, 6], par[:, :, 7]
        neg_a = sb("neg_a", [P, KD, NS])
        dtw = sb("dtw", [1, DI])
        wxp = sb("wxp", [P, KD, XD])
        wout = sb("wout", [P, KD, L])
        ln_bc = sb("ln_bc", [P, 2, L])
        wg = sb("wg", [P, KL, NE])
        cls_row = sb("cls_row", [P, L])
        h1_cls = sb("h1_cls", [P, L])
        xt_cls = sb("xt_cls", [P, L])
        xin_cls = sb("xin_cls", [P, KD])
        h0 = sb("h0", [P, KD, NS])
        logits = sb("logits", [P, 17, NE])
        half_neg = sb("half_neg", [P, CH])
        zeros = sb("zeros", [16, L])

        ld_const, ld_cls, xe_zeroed, pool_const = sems("ld_const ld_cls xe_zeroed pool_const")

        stage = ExitStack()
        with stage:
            def sa(name, shape, dt=F32):
                return sb(name, shape, dt, stage)

            HP = HEADS // 2
            c_in = sa("c_in", [P, 2, HP, NSEQ])
            s4p = sa("s4p", [P, 5, HP])
            inv_a, a_im, b_re, b_im, log_dt = (s4p[:, i, :] for i in range(5))
            tmp = [sa(f"tmp{i}", [P, HP]) for i in range(8)]
            q_re = [sa(f"q_re{i}", [P, HP]) for i in range(7)]
            q_im = [sa(f"q_im{i}", [P, HP]) for i in range(7)]
            q_t = [sa(f"q_t{i}", [P, HP]) for i in range(3)]
            u_re = sa("u_re", [P, HP, NA])
            u_im = sa("u_im", [P, HP, NA])
            w_re = sa("w_re", [P, HP, NB, NSEQ])
            w_ni = sa("w_ni", [P, HP, NB, NSEQ])
            HQ = HP // 4
            u_t = [sa(f"u_t{i}", [P, HQ, NA // 2]) for i in range(2)]
            w_t = [sa(f"w_t{i}", [P, HQ, NSEQ]) for i in range(2)]
            k_sb = sa("k_sb", [P, 8, 512])

            cst = sa("c_st", [P, 6])
            mv = sa("c_mv", [P, 2])
            rstd = sa("c_rstd", [P, 1])
            xn = sa("c_xn", [P, L])
            xnt = sa("c_xnt", [P, KL, P])
            zs = sa("c_zs", [P, KD])
            cv = sa("c_cv", [P, KD])
            xc = sa("c_xc", [P, KD])
            xcb = sa("c_xcb", [P, KD, P])
            xd = sa("c_xd", [P, XD])
            vv = sa("c_vv", [P, KD])
            av = sa("c_av", [P, KD])
            uu = sa("c_uu", [P, KD])
            lw = sa("c_lw", [P, KD])
            w1 = sa("c_w1", [P, KD])
            dtx = sa("c_dtx", [P, KD])
            bcp = sa("c_bcp", [P, NS])
            bcs = sa("c_bcs", [P, 1])
            yy = sa("c_yy", [P, KD])
            ygb = sa("c_ygb", [P, KD, P])
            o = sa("c_o", [P, L])

            steps = ("stats1 rstd1 xn xnt xnt_sb inproj xin zs conv xc xcb xdbl xd v absv u lnw h0 ygb outproj "
                     "o stats2 rstd2 ln2 h1 stats3 rstd3 xt xtt xtt_sb logit logit_sb").split()
            cls_done, cls_own = sems("cls_done cls_own")

            def upto(name):
                return steps.index(name) + 1

            ld_s4, ld_c, s4_exp, pow_step, u_step, w_step, pow64, u_done, w_done, k_bank, k_evac, k_store = sems(
                "ld_s4 ld_c s4_exp pow_step u_step w_step pow64 u_done w_done k_bank k_evac k_store")
            BANKS = [half * 4 + hq for hq in range(4) for half in range(2)]
            block = stage.enter_context(nc.Block("states"))

            @block.sync
            def _(sp):
                sp.dma_start(s4p[:, :, :], s4).then_inc(ld_s4, 16)
                sp.dma_start(cls_row[:, :], cls.broadcast_to([P, L])).then_inc(ld_cls, 16)
                sp.dma_start(c_in[:, :, :, :], x).then_inc(ld_c, 16)
                sp.dma_start(ident[:, :], ident_in).then_inc(ld_const, 16)
                sp.dma_start(tri[:, :], tri_in).then_inc(ld_const, 16)
                sp.dma_start(iota8[:, :], iota_in.broadcast_to([P, NE])).then_inc(ld_const, 16)
                sp.dma_start(win[:, :, :], w_in).then_inc(ld_const, 16)
                sp.dma_start(par[:, :, :], dpar).then_inc(ld_const, 16)
                sp.dma_start(dtw[:, :], dtw_row).then_inc(ld_const, 16)
                sp.dma_start(wxp[:, :, :], w_xp).then_inc(ld_const, 16)
                sp.dma_start(wout[:, :, :], w_out).then_inc(ld_const, 16)
                for i in range(2):
                    sp.dma_start(ln_bc[:, i, :], ln_rows[i:i + 1, :].broadcast_to([P, L])).then_inc(ld_const, 16)
                sp.dma_start(wg[:, :, :], w_g).then_inc(ld_const, 16)
                sp.wait_ge(pool_const, 2)
                sp.dma_start(xe_scr.rearrange("(p s) d -> p s d", p=16),
                             zeros[:, :].unsqueeze(1).broadcast_to([16, NE * PITCH // 16, L])).then_inc(xe_zeroed, 16)
                for i in range(8):
                    sp.wait_ge(k_evac, i + 1)
                    sp.dma_start(k_scr[BANKS[i]], k_sb[:, i, :]).then_inc(k_store, 16)
                sp.wait_ge(k_store, 8 * 16)
                sp.wait_ge(ld_const, 11 * 16)
                sp.wait_ge(ld_cls, 16)
                sp.wait_ge(xe_zeroed, 16)

            @block.scalar
            def _(act):
                act.wait_ge(ld_s4, 16)
                nc.scalar.activation(tmp[0][:, :], log_dt, ACT.Exp)
                nc.scalar.activation(tmp[1][:, :], inv_a, ACT.Exp).then_inc(s4_exp, 1)
                act.wait_ge(ld_const, 11 * 16)
                nc.scalar.activation(h0[:, :, :], par[:, :, 8:8 + NS], ACT.Exp).then_inc(s4_exp, 1)
                act.wait_ge(s4_exp, 2)
                nc.scalar.activation(neg_a[:, :, :], h0[:, :, :], ACT.Copy, scale=-1.0).then_inc(s4_exp, 1)

                def evacuate(i):
                    act.wait_ge(k_bank, i + 1)
                    nc.scalar.activation(k_sb[:, i, :], bank[BANKS[i]][:, :], ACT.Copy).then_inc(k_evac, 1)

                a = nc.scalar.activation
                act.wait_ge(cls_done, upto("xnt"))
                a(xnt[:, :, :], bank[3][:, 0:L].rearrange("p (j t) -> p j t", j=KL), ACT.Copy).then_inc(cls_done, 1)
                act.wait_ge(cls_done, upto("inproj"))
                a(xin_cls[:, :], bank[7][:, 0:KD], ACT.Copy).then_inc(cls_done, 1)
                act.wait_ge(cls_done, upto("xin"))
                a(zs[:, :], bank[7][:, KD:2 * KD], ACT.Silu).then_inc(cls_done, 1)
                act.wait_ge(cls_done, upto("conv"))
                a(xc[:, :], cv[:, :], ACT.Silu).then_inc(cls_done, 1)
                act.wait_ge(cls_done, upto("v"))
                a(av[:, :], vv[:, :], ACT.Abs).then_inc(cls_done, 1)
                act.wait_ge(cls_done, upto("absv"))
                a(uu[:, :], av[:, :], ACT.Exp, scale=-1.0).then_inc(cls_done, 1)
                act.wait_ge(cls_done, upto("u"))
                a(lw[:, :], uu[:, :], ACT.Ln, bias=1.0).then_inc(cls_done, 1)
                for i in range(6):
                    evacuate(i)
                act.wait_ge(cls_done, upto("xtt"))
                a(xnt[:, :, :], bank[3][:, 0:L].rearrange("p (j t) -> p j t", j=KL), ACT.Copy).then_inc(cls_done, 1)
                act.wait_ge(cls_done, upto("logit"))
                a(logits[:, 16, :], bank[7][:, 0:NE], ACT.Copy).then_inc(cls_done, 1)
                evacuate(6)
                evacuate(7)

            @block.vector
            def _(dve):
                v = nc.vector
                done = [0]

                def step(ins):
                    done[0] += 1
                    ins.then_inc(pow_step, 1)
                    dve.wait_ge(pow_step, done[0])

                dt, ea, hr, zr, zi, den, num, rec = (t[:, :] for t in tmp)
                dve.wait_ge(s4_exp, 1)
                step(v.tensor_scalar(hr, dt, 0.5, None, ALU.mult))
                v.scalar_tensor_tensor(zr, ea, -1.0, hr, ALU.mult, ALU.mult)
                step(v.tensor_tensor(zi, a_im, hr, ALU.mult))
                v.tensor_scalar(num, zr, 1.0, None, ALU.add)
                step(v.tensor_scalar(rec, zr, -1.0, 1.0, ALU.mult, ALU.add))
                v.tensor_tensor(hr, zi, zi, ALU.mult)
                v.tensor_tensor(num, num, rec, ALU.mult)
                step(v.tensor_tensor(den, rec, rec, ALU.mult))
                v.tensor_tensor(num, num, hr, ALU.subtract)
                step(v.tensor_tensor(den, den, hr, ALU.add))
                step(v.reciprocal(rec, den))
                v.tensor_tensor(q_re[0][:, :], num, rec, ALU.mult)
                step(v.scalar_tensor_tensor(q_im[0][:, :], zi, 2.0, rec, ALU.mult, ALU.mult))
                for k in range(6):
                    v.tensor_tensor(q_t[0][:, :], q_re[k][:, :], q_re[k][:, :], ALU.mult)
                    v.tensor_tensor(q_t[1][:, :], q_im[k][:, :], q_im[k][:, :], ALU.mult)
                    step(v.scalar_tensor_tensor(q_im[k + 1][:, :], q_re[k][:, :], 2.0, q_im[k][:, :], ALU.mult, ALU.mult))
                    step(v.tensor_tensor(q_re[k + 1][:, :], q_t[0][:, :], q_t[1][:, :], ALU.subtract))
                v.memset(q_t[2][:, 0:1], 0.0).then_inc(pow64, 1)
                v.memset(u_re[:, :, 0:1], 1.0)
                step(v.memset(u_im[:, :, 0:1], 0.0))
                own = [0]

                def chain(ins):
                    own[0] += 1
                    ins.then_inc(cls_own, 1)
                    dve.wait_ge(cls_own, own[0])

                def stats(src, before):
                    if before:
                        dve.wait_ge(cls_done, upto(before))
                    chain(v.bn_stats(cst[:, :], src))
                    v.bn_aggr(mv[:, :], cst[:, :]).then_inc(cls_done, 1)

                def cls_stats():
                    dve.wait_ge(ld_const, 11 * 16)
                    dve.wait_ge(ld_cls, 16)
                    dve.wait_ge(s4_exp, 3)
                    stats(cls_row[:, :], None)

                def cls_norm():
                    dve.wait_ge(cls_done, upto("rstd1"))
                    v.tensor_scalar(xn[:, :], cls_row[:, :], mv[:, 0:1], rstd[:, 0:1], ALU.subtract, ALU.mult).then_inc(cls_done, 1)

                def cls_conv():
                    dve.wait_ge(cls_done, upto("zs"))
                    chain(v.tensor_tensor(cv[:, :], xin_cls[:, :], conv_w[:, :, 3], ALU.mult))
                    v.tensor_tensor(cv[:, :], cv[:, :], conv_b, ALU.add).then_inc(cls_done, 1)

                def cls_spread():
                    dve.wait_ge(cls_done, upto("xc"))
                    v.tensor_copy(xcb[:, :, :], xc[:, :].unsqueeze(2).broadcast_to([P, KD, P])).then_inc(cls_done, 1)

                def cls_xdbl():
                    dve.wait_ge(cls_done, upto("xdbl"))
                    v.tensor_copy(xd[:, :], bank[3][:, 0:XD]).then_inc(cls_done, 1)

                def cls_v():
                    dve.wait_ge(cls_done, upto("xd"))
                    v.scalar_tensor_tensor(vv[:, :], dt_w, xd[:, 0:1], dt_b, ALU.mult, ALU.add).then_inc(cls_done, 1)

                def cls_dt():
                    dve.wait_ge(cls_done, upto("lnw"))
                    chain(v.tensor_scalar(w1[:, :], uu[:, :], 1.0, -1.0, ALU.add, ALU.add))
                    chain(v.tensor_tensor(w1[:, :], uu[:, :], w1[:, :], ALU.subtract))
                    chain(v.tensor_tensor(w1[:, :], w1[:, :], lw[:, :], ALU.add))
                    chain(v.scalar_tensor_tensor(vv[:, :], vv[:, :], 0.0, w1[:, :], ALU.max, ALU.add))
                    chain(v.tensor_tensor(dtx[:, :], vv[:, :], xc[:, :], ALU.mult))
                    for k in range(KD):
                        v.tensor_scalar(h0[:, k, :], xd[:, 1:1 + NS], dtx[:, k:k + 1], None, ALU.mult)
                    chain(v.tensor_tensor(bcp[:, :], xd[:, 1:1 + NS], xd[:, 1 + NS:XD], ALU.mult))
                    v.tensor_reduce(bcs[:, :], bcp[:, :], AX.X, ALU.add).then_inc(cls_done, 1)

                def cls_gate():
                    dve.wait_ge(cls_done, upto("h0"))
                    chain(v.tensor_tensor(yy[:, :], xc[:, :], skip_d, ALU.mult))
                    chain(v.scalar_tensor_tensor(yy[:, :], dtx[:, :], bcs[:, 0:1], yy[:, :], ALU.mult, ALU.add))
                    chain(v.tensor_tensor(yy[:, :], yy[:, :], zs[:, :], ALU.mult))
                    v.tensor_copy(ygb[:, :, :], yy[:, :].unsqueeze(2).broadcast_to([P, KD, P])).then_inc(cls_done, 1)

                def cls_residual():
                    dve.wait_ge(cls_done, upto("outproj"))
                    v.tensor_tensor(o[:, :], bank[7][:, 0:L], xn[:, :], ALU.add).then_inc(cls_done, 1)
                    stats(o[:, :], "o")

                def cls_norm2():
                    dve.wait_ge(cls_done, upto("rstd2"))
                    v.tensor_scalar(o[:, :], o[:, :], mv[:, 0:1], rstd[:, 0:1], ALU.subtract, ALU.mult).then_inc(cls_done, 1)

                def cls_sum():
                    dve.wait_ge(cls_done, upto("ln2"))
                    chain(v.tensor_tensor(o[:, :], o[:, :], ln_bc[:, 0, :], ALU.mult))
                    chain(v.tensor_tensor(o[:, :], o[:, :], ln_bc[:, 1, :], ALU.add))
                    v.tensor_tensor(h1_cls[:, :], o[:, :], cls_row[:, :], ALU.add).then_inc(cls_done, 1)
                    stats(h1_cls[:, :], "h1")

                def cls_norm3():
                    dve.wait_ge(cls_done, upto("rstd3"))
                    v.tensor_scalar(xt_cls[:, :], h1_cls[:, :], mv[:, 0:1], rstd[:, 0:1], ALU.subtract, ALU.mult).then_inc(cls_done, 1)

                between = {(0, 1, 0): cls_stats, (0, 3, 0): cls_norm, (0, 4, 1): cls_conv, (0, 5, 0): cls_spread,
                           (0, 5, 1): cls_xdbl, (0, 5, 2): cls_v, (1, 3, 0): cls_dt, (1, 4, 0): cls_gate,
                           (2, 1, 0): cls_residual, (2, 4, 2): cls_norm2, (2, 5, 0): cls_sum, (3, 1, 0): cls_norm3}
                for hq in range(4):
                    hs = slice(hq * HQ, (hq + 1) * HQ)
                    for k in range(6):
                        m = 1 << k
                        qr = q_re[k][:, hs].unsqueeze(2).broadcast_to([P, HQ, m])
                        qi = q_im[k][:, hs].unsqueeze(2).broadcast_to([P, HQ, m])
                        t0, t1 = u_t[0][:, :, 0:m], u_t[1][:, :, 0:m]

                        def also(i):
                            if (hq, k, i) in between:
                                between[hq, k, i]()

                        v.tensor_tensor(t0, u_re[:, hs, 0:m], qr, ALU.mult)
                        step(v.tensor_tensor(t1, u_im[:, hs, 0:m], qi, ALU.mult))
                        also(0)
                        step(v.tensor_tensor(u_re[:, hs, m:2 * m], t0, t1, ALU.subtract))
                        also(1)
                        v.tensor_tensor(t0, u_re[:, hs, 0:m], qi, ALU.mult)
                        step(v.tensor_tensor(t1, u_im[:, hs, 0:m], qr, ALU.mult))
                        also(2)
                        ins = v.tensor_tensor(u_im[:, hs, m:2 * m], t0, t1, ALU.add)
                        if m < NA // 2:
                            step(ins)
                    ins.then_inc(u_done, 1)
                    dve.wait_ge(u_done, hq + 1)


            @block.gpsimd
            def _(pool):
                g = nc.gpsimd
                done = [0]

                def step(ins):
                    done[0] += 1
                    ins.then_inc(w_step, 1)
                    pool.wait_ge(w_step, done[0])

                g.memset(zeros[:, :], 0.0).then_inc(pool_const, 1)
                g.memset(half_neg[:, :], -0.5).then_inc(pool_const, 1)
                pool.wait_ge(ld_s4, 16)
                pool.wait_ge(ld_c, 16)
                def cls_root(n):
                    pool.wait_ge(cls_done, upto(f"stats{n}"))
                    nc.gpsimd.tensor_scalar(rstd[:, :], mv[:, 1:2], EPS, 1.0, ALU.add, ALU.mult).then_inc(pool_const, 1)
                    pool.wait_ge(pool_const, 2 + n)
                    nc.gpsimd.tensor_tensor(rstd[:, :], rstd[:, :], half_neg[:, 0:1], ALU.pow).then_inc(cls_done, 1)

                t0, t1 = w_t[0][:, :, :], w_t[1][:, :, :]
                for hq in range(4):
                    hs = slice(hq * HQ, (hq + 1) * HQ)
                    cr, ci = c_in[:, 0, hs, :], c_in[:, 1, hs, :]
                    br = b_re[:, hs].unsqueeze(2).broadcast_to([P, HQ, NSEQ])
                    bi = b_im[:, hs].unsqueeze(2).broadcast_to([P, HQ, NSEQ])
                    step(g.tensor_tensor(t0, cr, br, ALU.mult))
                    step(g.tensor_tensor(t1, ci, bi, ALU.mult))
                    step(g.tensor_tensor(t0, t0, t1, ALU.subtract))
                    step(g.tensor_tensor(w_re[:, hs, 0, :], t0, t0, ALU.add))
                    step(g.tensor_tensor(t0, cr, bi, ALU.mult))
                    step(g.tensor_tensor(t1, ci, br, ALU.mult))
                    step(g.tensor_tensor(t0, t0, t1, ALU.add))
                    step(g.tensor_scalar(w_ni[:, hs, 0, :], t0, -2.0, 1.0, ALU.mult, ALU.mult))
                    if hq == 0:
                        cls_root(1)
                        pool.wait_ge(pow64, 1)
                    pr = q_re[6][:, hs].unsqueeze(2).broadcast_to([P, HQ, NSEQ])
                    pi = q_im[6][:, hs].unsqueeze(2).broadcast_to([P, HQ, NSEQ])
                    for b in range(1, NB):
                        wr, wn = w_re[:, hs, b - 1, :], w_ni[:, hs, b - 1, :]
                        step(g.tensor_tensor(t0, wr, pr, ALU.mult))
                        step(g.tensor_tensor(t1, wn, pi, ALU.mult))
                        step(g.tensor_tensor(w_re[:, hs, b, :], t0, t1, ALU.add))
                        step(g.tensor_tensor(t0, wn, pr, ALU.mult))
                        step(g.tensor_tensor(t1, wr, pi, ALU.mult))
                        ins = g.tensor_tensor(w_ni[:, hs, b, :], t0, t1, ALU.subtract)
                        if (hq, b) == (2, 1):
                            cls_root(2)
                        if b < NB - 1:
                            step(ins)
                    ins.then_inc(w_done, 1)
                    pool.wait_ge(w_done, hq + 1)
                    if hq == 2:
                        cls_root(3)

            @block.tensor
            def _(pe):
                mm = nc.tensor.matmul

                def transpose_xn():
                    pe.wait_ge(cls_done, upto("xn"))
                    for j in range(KL):
                        last = nc.tensor.transpose(bank[3][:, j * P:(j + 1) * P], xn[:, j * P:(j + 1) * P], ident[:, :])
                    last.then_inc(cls_done, 1)

                def inproj():
                    pe.wait_ge(cls_done, upto("xnt_sb"))
                    for m in range(2 * KD):
                        for j in range(KL):
                            last = mm(bank[7][:, m:m + 1], win[:, j, m * P:(m + 1) * P], xnt[:, j, 0:1],
                                      start=(j == 0), stop=(j == KL - 1))
                    last.then_inc(cls_done, 1)

                def xdbl():
                    pe.wait_ge(cls_done, upto("xcb"))
                    for k in range(KD):
                        last = mm(bank[3][:, 0:XD], xcb[:, k, :], wxp[:, k, :], start=(k == 0), stop=(k == KD - 1))
                    last.then_inc(cls_done, 1)

                def outproj():
                    pe.wait_ge(cls_done, upto("ygb"))
                    for k in range(KD):
                        last = mm(bank[7][:, 0:L], ygb[:, k, :], wout[:, k, :], start=(k == 0), stop=(k == KD - 1))
                    last.then_inc(cls_done, 1)

                def transpose_xt():
                    pe.wait_ge(cls_done, upto("xt"))
                    for j in range(KL):
                        last = nc.tensor.transpose(bank[3][:, j * P:(j + 1) * P], xt_cls[:, j * P:(j + 1) * P], ident[:, :])
                    last.then_inc(cls_done, 1)

                def logit():
                    pe.wait_ge(cls_done, upto("xtt_sb"))
                    for j in range(KL):
                        last = mm(bank[7][:, 0:NE], xnt[:, j, :], wg[:, j, :], start=(j == 0), stop=(j == KL - 1))
                    last.then_inc(cls_done, 1)

                between = {0: (transpose_xn, inproj, xdbl), 1: (outproj,), 3: (transpose_xt, logit)}
                for hb in range(4):
                    if hb == 0:
                        pe.wait_ge(ld_const, 11 * 16)
                    for product in between.get(hb, ()):
                        product()
                    if hb == 3:
                        pe.wait_ge(cls_done, upto("logit_sb"))
                    pe.wait_ge(u_done, hb + 1)
                    pe.wait_ge(w_done, hb + 1)
                    for half in range(2):
                        rows = slice(64 * half, 64 * half + 64)
                        for s in range(8):
                            for q in range(4):
                                h = hb * 32 + q * 8 + s
                                o = bank[half * 4 + hb][32 * q:32 * q + 32, s * NA:(s + 1) * NA]
                                mm(o, w_re[rows, h, :, :], u_re[rows, h, :], start=True, stop=False)
                                last = mm(o, w_ni[rows, h, :, :], u_im[rows, h, :], start=False, stop=True)
                        last.then_inc(k_bank, 1)

        stage = ExitStack()
        with stage:
            def sa(name, shape, dt=F32):
                return sb(name, shape, dt, stage)

            k_in = sa("k_in", [P, CH, L])
            k_res = sa("k_res", [P, 2, CH, L])
            xn = sa("xn", [P, CH, L])
            x_res = sa("x_res", [P, 2, CH, L])
            xnt = sa("xnt", [P, KL, GT])
            xin = sa("xin", [P, KD, TAPS + GT])
            cv = sa("cv", [P, KD, GT])
            xc = sa("xc", [P, 2, KD, GT])
            zs = sa("zs", [P, 2, KD, GT])
            xdt = sa("xdt", [XD, GT])
            bc = sa("bc", [P, 2, CH, XD])
            absv = sa("absv", [P, KD, GT])
            relv = sa("relv", [P, KD, GT])
            uu = sa("uu", [P, KD, GT])
            ww = sa("ww", [P, KD, GT])
            lw = sa("lw", [P, KD, GT])
            dt = sa("dt", [P, 2, KD, GT])
            dtx = sa("dtx", [P, KD, GT])
            dtxt = sa("dtxt", [P, 2, CH, DI])
            st = [sa(f"st{i}", [P, CH, 6]) for i in range(2)]
            mv = [sa(f"mv{i}", [P, CH, 2]) for i in range(2)]
            rstd = [sa(f"rstd{i}", [P, CH]) for i in range(2)]
            bx = sa("bx", [P, 4, CH, DI])
            da = sa("da", [P, 4, KD, GT])
            hs = sa("hs", [P, 2, KD, GT])
            yt = sa("yt", [P, 2, CH, DI])
            yp = sa("yp", [P, 2, DI])
            cy = sa("cy", [P, 2, DI])
            yg = sa("yg", [P, KD, GT])
            o = sa("o", [P, CH, L])
            h1 = sa("h1", [P, CH, L])
            xt = sa("xt", [P, CH, L])
            xtt = sa("xtt", [P, KL, GT])

            P_UNITS = "xnt xin0 xin1 z0 z1 xd dtv0 dtv1 bc dtxt0 dtxt1".split()
            T_UNITS = {"ygt0": "dve", "ygt1": "dve", "out": "dve", "xtt": "act", "logit": "act"}
            T_NAMES = list(T_UNITS)
            NPU, NTU, NTD, NTA = len(P_UNITS), 5, 3, 2
            P_BANK, T_BANK = bank[6], bank[7]

            (ld_k, edge_ready, mvp_ready, rstdp_ready, xn_ready, copied_x, copied_k, pu_ready, pu_took, tap0_ready,
             conv_ready, xc_ready, absv_ready, u_ready, one_u_ready, lnw_ready, rel_fixed, dt_ready, dtx_ready, bx_ready,
             bt_ready, da_ready, scanned, ht_ready, y0_added, y1_added, cy_ready, yp_added, merged, tu_ready, tu_dve,
             tu_act, gated, mvt_ready, rstdt_ready, ln2_ready, h1_ready, xt_ready, h1_stored, xt_stored, dve_p, dve_t,
             pool_step, rstdp_step, rstdt_step, w_fix, turn_ends, waits_apart) = sems(
                "ld_k edge_ready mvp_ready rstdp_ready xn_ready copied_x copied_k pu_ready pu_took tap0_ready "
                "conv_ready xc_ready absv_ready u_ready one_u_ready lnw_ready rel_fixed dt_ready dtx_ready bx_ready "
                "bt_ready da_ready scanned ht_ready y0_added y1_added cy_ready yp_added merged tu_ready tu_dve "
                "tu_act gated mvt_ready rstdt_ready ln2_ready h1_ready xt_ready h1_stored xt_stored dve_p dve_t "
                "pool_step rstdp_step rstdt_step w_fix turn_ends waits_apart")
            rstd_step = [rstdp_step, rstdt_step]
            DVE_P_STEPS, DVE_T_STEPS = 5, 2
            TURNS = dict(
                pool=dict(rstdp=1, tap0=(3, 4), one_u=9, rel=9, dtx=11, merge=1, gate=3, rstd2=6, h1=6, rstd3=7),
                act=dict(xnt=1, xin=(2, 4), silu=(5, 5), xd=6, dtv=(7, 8), u=8, lnw=9, dtxt=(12, 13), xtt=9, logit=10),
                dve=dict(stats1=0, xn=1, conv=(3, 4), fix=9, dt=10, yg=(1, 2), o=5, ln2=5, stats3=7, xt=8),
                pe=dict(xnt=1, inproj=(2, 3, 4, 5), xd=5, dtv=(6, 7), bc=9, dtxt=(12, 13), ygt=(1, 1), out=4, xtt=9, logit=10))
            NY1, NYP = NS // 2, NS // 2 - 1
            block = stage.enter_context(nc.Block("mamba"))


            def steps(eng, scan, project, finish, flush):
                for n in range(NS):
                    project(0, 0, n)
                def step(g, s, first=False, last=False):
                    for n in range(NS):
                        scan(g, s, n, first, last)
                        if not first:
                            finish(g - 1, 1 - s, n)
                        if not last:
                            project(g + 1, 1 - s, n)
                flush(0, 0, True)
                step(0, 0, first=True)
                with eng.Fori(0, GROUPS // 2 - 1) as i:
                    step(2 * i + 1, 1)
                    step(2 * i + 2, 0)
                step(GROUPS - 1, 1, last=True)
                flush(GROUPS - 1, 1, False)
                for n in range(NS):
                    finish(GROUPS - 1, 1, n)

            def apart(eng):
                eng.sem_inc(waits_apart, 1)

            def pu_index(name):
                return P_UNITS.index(name)

            def tu_taken(name, who):
                return sum(T_UNITS[u] == who for u in T_NAMES[:T_NAMES.index(name) + 1])

            @block.sync
            def _(sp):
                def load(g):
                    wait(sp, copied_k, 16 * g)
                    wait(sp, xn_ready, CH * g)
                    apart(sp)
                    for c in range(CH):
                        for b in range(NB):
                            src = k_scr.rearrange("(u hb) (q b c) (s a) -> u b c (hb q) s a", u=2, q=4, b=NB, s=8)
                            rows = slice(g, g + 1) if isinstance(g, int) else bass.ds(g, 1)
                            src = src[c, b, rows, :, :, :].rearrange("c r s a -> (c r) s a")
                            sp.dma_start(k_in[:, c, b * NA:(b + 1) * NA], src).then_inc(ld_k, 16)

                def keep_x(g, s):
                    sp.wait_ge(xn_ready, CH * (g + 1))
                    sp.dma_start(x_res[:, s, :, :], xn[:, :, :]).then_inc(copied_x, 16)

                def keep_k(g, s):
                    sp.wait_ge(ld_k, CH * NB * 16 * (g + 1))
                    sp.dma_start(k_res[:, s, :, :], k_in[:, :, :]).then_inc(copied_k, 16)

                def store(g):
                    rows = slice(g * GT, (g + 1) * GT) if isinstance(g, int) else bass.ds(g * GT, GT)
                    sp.wait_ge(h1_ready, g + 1)
                    sp.dma_start(h1_scr[rows, :].rearrange("(c p) d -> p c d", p=P), h1[:, :, :]).then_inc(h1_stored, 16)
                    sp.wait_ge(xt_ready, CH * (g + 1))
                    sp.dma_start(xt_scr[rows, :].rearrange("(c p) d -> p c d", p=P), xt[:, :, :]).then_inc(xt_stored, 16)

                def step(g, s):
                    if not (isinstance(g, int) and g == 0):
                        sp.wait_ge(tu_dve, NTD * g)
                        keep_x(g + 1, 1 - s)
                        sp.wait_ge(h1_ready, g)
                        apart(sp)
                        keep_k(g + 1, 1 - s)
                    else:
                        keep_x(g + 1, 1 - s)
                        keep_k(g + 1, 1 - s)
                    if not (isinstance(g, int) and g == GROUPS - 2):
                        load(g + 2)
                    if not (isinstance(g, int) and g == 0):
                        store(g - 1)

                load(0)
                keep_x(0, 0)
                keep_k(0, 0)
                load(1)
                step(0, 0)
                with sp.Fori(0, GROUPS // 2 - 2) as i:
                    step(2 * i + 1, 1)
                    step(2 * i + 2, 0)
                step(GROUPS - 3, 1)
                step(GROUPS - 2, 0)
                store(GROUPS - 2)
                store(GROUPS - 1)
                sp.wait_ge(h1_stored, GROUPS * 16)
                sp.wait_ge(xt_stored, GROUPS * 16)

            @block.gpsimd
            def _(pool):
                turn = TURNS["pool"]
                g_ = nc.gpsimd
                g_.memset(xin[:, :, 0:TAPS - 1], 0.0).then_inc(edge_ready, 1)

                def chained(ins, count):
                    ins.then_inc(pool_step, 1)
                    pool.wait_ge(pool_step, count)

                def inverse_root(which, ready, value, done):
                    pool.wait_ge(ready, value)
                    apart(pool)
                    g_.tensor_scalar(rstd[which][:, :], mv[which][:, :, 1], EPS, 1.0, ALU.add, ALU.mult).then_inc(rstd_step[which], 1)
                    pool.wait_ge(rstd_step[which], value)
                    g_.tensor_tensor(rstd[which][:, :], rstd[which][:, :], half_neg[:, 0:CH], ALU.pow).then_inc(done, 1)

                def bx_of(g, s, n):
                    it = g * NS + n
                    wait(pool, bt_ready, 2 * (it - 3))
                    if n == 0:
                        pool.wait_ge(pu_took, NPU * (g + 1))
                    apart(pool)
                    for c in range(CH):
                        g_.tensor_scalar(bx[:, n % 4, c, :], dtxt[:, s, c, :], bc[:, s, c, n + 1:n + 2], 1.0,
                                         ALU.mult, ALU.mult).then_inc(bx_ready, 1)

                def yp_of(g, s, n):
                    if n % 2 and n > 1:
                        i = n // 2
                        pool.wait_ge(cy_ready, NY1 * g + i + 1)
                        wait(pool, yp_added, NYP * g + i - 1)
                        g_.tensor_tensor(yp[:, s, :], yp[:, s, :], cy[:, i % 2, :], ALU.add).then_inc(yp_added, 1)

                def scan(g, s, n, first, last):
                    if n < NS - 2:
                        bx_of(g, s, n + 2)
                    elif not last:
                        bx_of(g + 1, 1 - s, n + 2 - NS)
                    if n >= 2:
                        yp_of(g, s, n - 2)
                    elif not first:
                        yp_of(g - 1, 1 - s, n - 2 + NS)

                def project(g, s, n):
                    if n == turn["rstdp"]:
                        inverse_root(0, mvp_ready, g + 1, rstdp_ready)
                    for kk in range(2):
                        if n != turn["tap0"][kk]:
                            continue
                        wait(pool, conv_ready, 2 * g)
                        wait(pool, xc_ready, 2 * g)
                        if kk == 0:
                            pool.wait_ge(edge_ready, 2)
                        pool.wait_ge(pu_took, NPU * g + pu_index(f"xin{kk}") + 1)
                        apart(pool)
                        for k in (2 * kk, 2 * kk + 1):
                            g_.tensor_scalar(cv[:, k, :], xin[:, k, 1:1 + GT], conv_w[:, k, 0:1], par[:, k, 4:5],
                                             ALU.mult, ALU.add).then_inc(tap0_ready, 1)
                    if n == turn["one_u"]:
                        pool.wait_ge(u_ready, g + 1)
                        apart(pool)
                        g_.tensor_scalar(ww[:, :, :], uu[:, :, :], 1.0, 1.0, ALU.add, ALU.mult).then_inc(one_u_ready, 1)
                    if n == turn["rel"]:
                        pool.wait_ge(w_fix, g + 1)
                        g_.tensor_tensor(relv[:, :, :], relv[:, :, :], absv[:, :, :], ALU.subtract).then_inc(rel_fixed, 1)
                    if n == turn["dtx"]:
                        pool.wait_ge(dt_ready, g + 1)
                        g_.tensor_tensor(dtx[:, :, :], dt[:, s, :, :], xc[:, s, :, :], ALU.mult).then_inc(dtx_ready, 1)

                def finish(g, s, n):
                    if n == turn["merge"]:
                        pool.wait_ge(y1_added, NY1 * (g + 1))
                        pool.wait_ge(yp_added, NYP * (g + 1))
                        g_.tensor_tensor(yt[:, s, 1, :], yt[:, s, 1, :], yp[:, s, :], ALU.add).then_inc(merged, 1)
                    if n == turn["gate"]:
                        pool.wait_ge(tu_dve, NTD * g + 2)
                        g_.tensor_tensor(yg[:, :, :], yg[:, :, :], zs[:, s, :, :], ALU.mult).then_inc(gated, 1)
                    if n == turn["rstd2"]:
                        inverse_root(1, mvt_ready, 2 * g + 1, rstdt_ready)
                    if n == turn["h1"]:
                        pool.wait_ge(ln2_ready, g + 1)
                        pool.wait_ge(copied_k, 16 * (g + 1))
                        chained(g_.tensor_tensor(o[:, :, :], o[:, :, :], ln_bc[:, 0:1, :].broadcast_to([P, CH, L]), ALU.mult), 2 * g + 1)
                        chained(g_.tensor_tensor(o[:, :, :], o[:, :, :], ln_bc[:, 1:2, :].broadcast_to([P, CH, L]), ALU.add), 2 * g + 2)
                        g_.tensor_tensor(h1[:, :, :], o[:, :, :], k_res[:, s, :, :], ALU.add).then_inc(h1_ready, 1)
                    if n == turn["rstd3"]:
                        inverse_root(1, mvt_ready, 2 * g + 2, rstdt_ready)
                    if n == NS - 1:
                        pool.wait_ge(h1_stored, 16 * (g + 1))
                        pool.sem_inc(turn_ends, 1)

                def flush(g, s, front):
                    if front:
                        bx_of(0, 0, 0)
                        bx_of(0, 0, 1)
                    else:
                        yp_of(g, s, NS - 1)

                steps(pool, scan, project, finish, flush)

            @block.scalar
            def _(act):
                turn = TURNS["act"]
                a = nc.scalar.activation

                def da_of(g, s, n):
                    it = g * NS + n
                    if n == 0:
                        act.wait_ge(dt_ready, g + 1)
                    for k in range(KD):
                        if k % 2 == 0:
                            wait(act, scanned, 2 * (it - 4) + k // 2 + 1)
                        ins = a(da[:, n % 4, k, :], dt[:, s, k, :], ACT.Exp, scale=neg_a[:, k, n:n + 1])
                        if k % 2:
                            ins.then_inc(da_ready, 1)

                def cy_of(g, s, n):
                    if n == 0:
                        for c in range(CH):
                            act.wait_ge(ht_ready, 2 * g * NS + c + 1)
                            a(yt[:, s, c, :], bank[4 + c][:, :], ACT.Copy, scale=bc[:, s, c, 1 + NS:2 + NS])\
                                .then_inc((y0_added, y1_added)[c], 1)
                    if n % 2:
                        i = n // 2
                        act.wait_ge(ht_ready, 2 * (g * NS + n) + 2)
                        if i == 0:
                            dst = yp[:, s, :]
                        else:
                            wait(act, yp_added, NYP * g + max(i - 2, 0))
                            dst = cy[:, i % 2, :]
                        a(dst, bank[5][:, :], ACT.Copy, scale=bc[:, s, 1, n + 1 + NS:n + 2 + NS]).then_inc(cy_ready, 1)

                def scan(g, s, n, first, last):
                    if n < NS - 1:
                        da_of(g, s, n + 1)
                    elif not last:
                        da_of(g + 1, 1 - s, 0)
                    if n >= 1:
                        cy_of(g, s, n - 1)
                    elif not first:
                        cy_of(g - 1, 1 - s, NS - 1)

                def project(g, s, n):
                    def unit(name):
                        act.wait_ge(pu_ready, NPU * g + pu_index(name) + 1)

                    if n == turn["xnt"]:
                        unit("xnt")
                        a(xnt[:, :, :], P_BANK[:, :].rearrange("p (j t) -> p j t", j=KL), ACT.Copy).then_inc(pu_took, 1)
                        if isinstance(g, int) and g == 0:
                            a(xin[:, :, TAPS - 1], xin_cls[:, :], ACT.Copy).then_inc(edge_ready, 1)
                    for kk in range(2):
                        if n != turn["xin"][kk]:
                            continue
                        unit(f"xin{kk}")
                        wait(act, conv_ready, 2 * g)
                        a(xin[:, 2 * kk:2 * kk + 2, TAPS:], P_BANK[:, :].rearrange("p (k t) -> p k t", k=2), ACT.Copy).then_inc(pu_took, 1)
                    for kk in range(2):
                        if n != turn["silu"][kk]:
                            continue
                        act.wait_ge(conv_ready, 2 * g + kk + 1)
                        a(xc[:, s, 2 * kk:2 * kk + 2, :], cv[:, 2 * kk:2 * kk + 2, :], ACT.Silu).then_inc(xc_ready, 1)
                        unit(f"z{kk}")
                        wait(act, gated, g - 1)
                        a(zs[:, s, 2 * kk:2 * kk + 2, :], P_BANK[:, :].rearrange("p (k t) -> p k t", k=2), ACT.Silu).then_inc(pu_took, 1)
                    if n == turn["xd"]:
                        unit("xd")
                        a(xdt[:, :], P_BANK[0:XD, 0:GT], ACT.Copy).then_inc(pu_took, 1)
                    for kk in range(2):
                        if n != turn["dtv"][kk]:
                            continue
                        unit(f"dtv{kk}")
                        wait(act, dt_ready, g)
                        for i in range(2):
                            k = 2 * kk + i
                            a(absv[:, k, :], P_BANK[:, i * GT:(i + 1) * GT], ACT.Abs, bias=par[:, k, 6:7]).then_inc(absv_ready, 1)
                            ins = a(relv[:, k, :], P_BANK[:, i * GT:(i + 1) * GT], ACT.Relu, bias=par[:, k, 6:7])
                        ins.then_inc(pu_took, 1)
                    if n == turn["u"]:
                        act.wait_ge(absv_ready, KD * (g + 1))
                        a(uu[:, :, :], absv[:, :, :], ACT.Exp, scale=-1.0).then_inc(u_ready, 1)
                    if n == turn["lnw"]:
                        unit("bc")
                        a(bc[:, s, :, :], P_BANK[:, 0:CH * XD].rearrange("p (c m) -> p c m", c=CH), ACT.Copy).then_inc(pu_took, 1)
                        act.wait_ge(one_u_ready, g + 1)
                        a(lw[:, :, :], ww[:, :, :], ACT.Ln).then_inc(lnw_ready, 1)
                    for c in range(2):
                        if n != turn["dtxt"][c]:
                            continue
                        unit(f"dtxt{c}")
                        a(dtxt[:, s, c, :], P_BANK[:, :], ACT.Copy).then_inc(pu_took, 1)

                def finish(g, s, n):
                    if n == turn["xtt"]:
                        act.wait_ge(tu_ready, NTU * g + 4)
                        a(xtt[:, :, :], T_BANK[:, :].rearrange("p (j t) -> p j t", j=KL), ACT.Copy).then_inc(tu_act, 1)
                    if n == turn["logit"]:
                        act.wait_ge(tu_ready, NTU * g + 5)
                        rows = slice(CH * g, CH * g + CH) if isinstance(g, int) else bass.ds(CH * g, CH)
                        a(logits[:, rows, :], T_BANK[:, 0:CH * NE].rearrange("p (c m) -> p c m", c=CH), ACT.Copy).then_inc(tu_act, 1)

                def flush(g, s, front):
                    if front:
                        da_of(0, 0, 0)
                    else:
                        cy_of(g, s, NS - 1)

                steps(act, scan, project, finish, flush)

            @block.vector
            def _(dve):
                turn = TURNS["dve"]
                v = nc.vector

                def stats(which, src, chain, count, done):
                    for c in range(CH):
                        ins = v.bn_stats(st[which][:, c, :], src[:, c, :])
                    ins.then_inc(chain, 1)
                    dve.wait_ge(chain, count)
                    apart(dve)
                    for c in range(CH):
                        ins = v.bn_aggr(mv[which][:, c, :], st[which][:, c, :])
                    ins.then_inc(done, 1)

                def norm(which, dst, src, c):
                    return v.tensor_scalar(dst[:, c, :], src[:, c, :], mv[which][:, c, 0:1], rstd[which][:, c:c + 1],
                                           ALU.subtract, ALU.mult)

                def scan_of(g, s, n):
                    it = g * NS + n
                    wait(dve, ht_ready, 2 * (it - 1))
                    for k in range(KD):
                        if k % 2 == 0:
                            dve.wait_ge(bt_ready, 2 * it + k // 2 + 1)
                            dve.wait_ge(da_ready, 2 * it + k // 2 + 1)
                        ins = v.tensor_tensor_scan(hs[:, n % 2, k, :], da[:, n % 4, k, :],
                                                   bank[2 * (n % 2) + k // 2][:, (k % 2) * GT:(k % 2 + 1) * GT],
                                                   h0[:, k, n:n + 1], ALU.mult, ALU.add)
                        if k % 2:
                            ins.then_inc(scanned, 1)

                def add_of(g, s, n):
                    it = g * NS + n
                    for c in range(CH):
                        if n == 0 or (c == 1 and n % 2):
                            continue
                        dve.wait_ge(ht_ready, 2 * it + c + 1)
                        scale = bc[:, s, c, n + 1 + NS:n + 2 + NS]
                        done = (y0_added, y1_added)[c]
                        dve.wait_ge(done, it if c == 0 else NY1 * g + n // 2)
                        v.scalar_tensor_tensor(yt[:, s, c, :], bank[4 + c][:, :], scale, yt[:, s, c, :], ALU.mult, ALU.add)\
                            .then_inc(done, 1)

                def scan(g, s, n, first, last):
                    scan_of(g, s, n)
                    if n >= 1:
                        add_of(g, s, n - 1)
                    elif not first:
                        add_of(g - 1, 1 - s, NS - 1)

                def project(g, s, n):
                    if n == turn["stats1"]:
                        dve.wait_ge(ld_k, (g + 1) * CH * NB * 16)
                        stats(0, k_in, dve_p, DVE_P_STEPS * g + 1, mvp_ready)
                    if n == turn["xn"]:
                        wait(dve, copied_x, 16 * g)
                        wait(dve, pu_took, NPU * (g - 1) + 1)
                        dve.wait_ge(rstdp_ready, g + 1)
                        for c in range(CH):
                            norm(0, xn, k_in, c).then_inc(xn_ready, 1)
                    for kk in range(2):
                        if n != turn["conv"][kk]:
                            continue
                        dve.wait_ge(tap0_ready, KD * g + 2 * kk + 2)
                        for tap in range(1, TAPS):
                            for k in (2 * kk, 2 * kk + 1):
                                ins = v.scalar_tensor_tensor(cv[:, k, :], xin[:, k, 1 + tap:1 + tap + GT], conv_w[:, k, tap:tap + 1],
                                                             cv[:, k, :], ALU.mult, ALU.add)
                            if tap < TAPS - 1:
                                ins.then_inc(dve_p, 1)
                                dve.wait_ge(dve_p, DVE_P_STEPS * g + 1 + 2 * kk + tap)
                        ins.then_inc(conv_ready, 1)
                    if n == turn["fix"]:
                        dve.wait_ge(one_u_ready, g + 1)
                        v.scalar_tensor_tensor(absv[:, :, :], ww[:, :, :], -1.0, uu[:, :, :], ALU.add, ALU.subtract).then_inc(w_fix, 1)
                    if n == turn["dt"]:
                        dve.wait_ge(lnw_ready, g + 1)
                        dve.wait_ge(rel_fixed, g + 1)
                        v.tensor_tensor(dt[:, s, :, :], lw[:, :, :], relv[:, :, :], ALU.add).then_inc(dt_ready, 1)

                def finish(g, s, n):
                    for kk in range(2):
                        if n != turn["yg"][kk]:
                            continue
                        dve.wait_ge(tu_ready, NTU * g + kk + 1)
                        for i in range(2):
                            k = 2 * kk + i
                            ins = v.scalar_tensor_tensor(yg[:, k, :], xc[:, s, k, :], par[:, k, 7:8], T_BANK[:, i * GT:(i + 1) * GT],
                                                         ALU.mult, ALU.add)
                        ins.then_inc(tu_dve, 1)
                    if n == turn["o"]:
                        dve.wait_ge(tu_ready, NTU * g + 3)
                        dve.wait_ge(copied_x, 16 * (g + 1))
                        v.tensor_tensor(o[:, :, :], T_BANK[:, :].rearrange("p (c d) -> p c d", c=CH), x_res[:, s, :, :],
                                        ALU.add).then_inc(tu_dve, 1)
                        dve.wait_ge(tu_dve, NTD * (g + 1))
                        stats(1, o, dve_t, DVE_T_STEPS * g + 1, mvt_ready)
                    if n == turn["ln2"]:
                        dve.wait_ge(rstdt_ready, 2 * g + 1)
                        for c in range(CH):
                            ins = norm(1, o, o, c)
                        ins.then_inc(ln2_ready, 1)
                    if n == turn["stats3"]:
                        dve.wait_ge(h1_ready, g + 1)
                        stats(1, h1, dve_t, DVE_T_STEPS * g + 2, mvt_ready)
                    if n == turn["xt"]:
                        dve.wait_ge(rstdt_ready, 2 * g + 2)
                        for c in range(CH):
                            norm(1, xt, h1, c).then_inc(xt_ready, 1)
                    if n == NS - 1:
                        dve.wait_ge(xt_stored, 16 * (g + 1))
                        dve.sem_inc(turn_ends, 1)

                def flush(g, s, front):
                    if not front:
                        add_of(g, s, NS - 1)

                steps(dve, scan, project, finish, flush)

            @block.tensor
            def _(pe):
                turn = TURNS["pe"]
                mm = nc.tensor.matmul

                def to_channels(g, s, n):
                    it = g * NS + n
                    pe.wait_ge(bx_ready, CH * (it + 1))
                    for kk in range(2):
                        b = bank[2 * (n % 2) + kk]
                        wait(pe, scanned, 2 * (it - 2) + kk + 1)
                        for i in range(2):
                            for c in range(CH):
                                k = 2 * kk + i
                                last = nc.tensor.transpose(b[:, i * GT + c * P:i * GT + (c + 1) * P],
                                                           bx[:, n % 4, c, k * P:(k + 1) * P], ident[:, :])
                        last.then_inc(bt_ready, 1)

                def to_time(g, s, n):
                    it = g * NS + n
                    pe.wait_ge(scanned, 2 * (it + 1))
                    for c in range(CH):
                        if c == 0:
                            wait(pe, y0_added, it)
                        elif n % 2:
                            pe.wait_ge(y1_added, NY1 * g + n // 2 + 1)
                        else:
                            wait(pe, cy_ready, NY1 * g + n // 2)
                        for k in range(KD):
                            last = nc.tensor.transpose(bank[4 + c][:, k * P:(k + 1) * P], hs[:, n % 2, k, c * P:(c + 1) * P], ident[:, :])
                        last.then_inc(ht_ready, 1)

                def scan(g, s, n, first, last):
                    if n >= 1:
                        to_time(g, s, n - 1)
                    elif not first:
                        to_time(g - 1, 1 - s, NS - 1)
                    if n < NS - 1:
                        to_channels(g, s, n + 1)
                    elif not last:
                        to_channels(g + 1, 1 - s, 0)

                def project(g, s, n):
                    def room(name):
                        wait(pe, pu_took, NPU * g + pu_index(name))

                    if n == turn["xnt"]:
                        room("xnt")
                        for c in range(CH):
                            pe.wait_ge(xn_ready, CH * g + c + 1)
                            for j in range(KL):
                                last = nc.tensor.transpose(P_BANK[:, j * GT + c * P:j * GT + (c + 1) * P],
                                                           xn[:, c, j * P:(j + 1) * P], ident[:, :])
                        last.then_inc(pu_ready, 1)
                    for i_unit, name in enumerate(("xin0", "xin1", "z0", "z1")):
                        if n != turn["inproj"][i_unit]:
                            continue
                        kk, at = i_unit % 2, DI * (i_unit // 2)
                        room(name)
                        for i in range(2):
                            for j in range(KL):
                                cols = slice(at + (2 * kk + i) * P, at + (2 * kk + i + 1) * P)
                                last = mm(P_BANK[:, i * GT:(i + 1) * GT], win[:, j, cols], xnt[:, j, :], start=(j == 0), stop=(j == KL - 1))
                        last.then_inc(pu_ready, 1)
                    if n == turn["xd"]:
                        room("xd")
                        pe.wait_ge(xc_ready, 2 * (g + 1))
                        for k in range(KD):
                            last = mm(P_BANK[0:XD, 0:GT], wxp[:, k, :], xc[:, s, k, :], start=(k == 0), stop=(k == KD - 1))
                        last.then_inc(pu_ready, 1)
                    for kk in range(2):
                        if n != turn["dtv"][kk]:
                            continue
                        room(f"dtv{kk}")
                        for i in range(2):
                            k = 2 * kk + i
                            last = mm(P_BANK[:, i * GT:(i + 1) * GT], dtw[0:1, k * P:(k + 1) * P], xdt[0:1, :], start=True, stop=True)
                        last.then_inc(pu_ready, 1)
                    if n == turn["bc"]:
                        room("bc")
                        apart(pe)
                        for c in range(CH):
                            last = nc.tensor.transpose(P_BANK[:, c * XD:(c + 1) * XD], xdt[:, c * P:(c + 1) * P], ident[0:XD, 0:XD])
                        last.then_inc(pu_ready, 1)
                    for c in range(2):
                        if n != turn["dtxt"][c]:
                            continue
                        room(f"dtxt{c}")
                        pe.wait_ge(dtx_ready, g + 1)
                        for k in range(KD):
                            last = nc.tensor.transpose(P_BANK[:, k * P:(k + 1) * P], dtx[:, k, c * P:(c + 1) * P], ident[:, :])
                        last.then_inc(pu_ready, 1)

                def finish(g, s, n):
                    for kk in range(2):
                        if n != turn["ygt"][kk]:
                            continue
                        if kk == 0:
                            pe.wait_ge(y0_added, NS * (g + 1))
                            pe.wait_ge(merged, g + 1)
                        else:
                            pe.wait_ge(tu_dve, NTD * g + 1)
                        for i in range(2):
                            for c in range(CH):
                                k = 2 * kk + i
                                last = nc.tensor.transpose(T_BANK[:, i * GT + c * P:i * GT + (c + 1) * P],
                                                           yt[:, s, c, k * P:(k + 1) * P], ident[:, :])
                        last.then_inc(tu_ready, 1)
                    if n == turn["out"]:
                        pe.wait_ge(tu_dve, NTD * g + 2)
                        pe.wait_ge(gated, g + 1)
                        for c in range(CH):
                            for k in range(KD):
                                last = mm(T_BANK[:, c * L:(c + 1) * L], yg[:, k, c * P:(c + 1) * P], wout[:, k, :],
                                          start=(k == 0), stop=(k == KD - 1))
                        last.then_inc(tu_ready, 1)
                    if n == turn["xtt"]:
                        pe.wait_ge(tu_dve, NTD * (g + 1))
                        for c in range(CH):
                            pe.wait_ge(xt_ready, CH * g + c + 1)
                            for j in range(KL):
                                last = nc.tensor.transpose(T_BANK[:, j * GT + c * P:j * GT + (c + 1) * P],
                                                           xt[:, c, j * P:(j + 1) * P], ident[:, :])
                        last.then_inc(tu_ready, 1)
                    if n == turn["logit"]:
                        pe.wait_ge(tu_act, NTA * g + 1)
                        for c in range(CH):
                            for j in range(KL):
                                last = mm(T_BANK[:, c * NE:(c + 1) * NE], xtt[:, j, c * P:(c + 1) * P], wg[:, j, :],
                                          start=(j == 0), stop=(j == KL - 1))
                        last.then_inc(tu_ready, 1)
                    if n == NS - 1:
                        pe.wait_ge(tu_act, NTA * (g + 1))
                        pe.sem_inc(turn_ends, 1)

                def flush(g, s, front):
                    if front:
                        to_channels(0, 0, 0)
                    else:
                        to_time(g, s, NS - 1)

                steps(pe, scan, project, finish, flush)

        stage = ExitStack()
        with stage:
            def sa(name, shape, dt=F32):
                return sb(name, shape, dt, stage)

            NT = 17
            xts = sa("xts", [P, 16, L])
            h1s = sa("h1s", [P, 16, L])
            top = sa("top", [P, NT, 8])
            topi = sa("topi", [P, NT, 8], U32)
            ef = sa("ef", [P, NT, 2])
            oh = sa("oh", [P, NT, 2, NE])
            ohb = sa("ohb", [P, NT, 2, NE], BF16)
            trib = sa("trib", [P, P], BF16)
            oneb = sa("oneb", [P, P], BF16)
            NC = 3 * NSEQ + 1
            entry = sa("entry", [P, 2 * NE, NC])
            within = sa("within", [P, 2 * NE, NC])
            before = sa("before", [P, 2 * NE, NC])
            cls_before = sa("cls_before", [P, 2 * NE, NSEQ])
            rank = sa("rank", [P, NT, 2, NE])
            rk = sa("rk", [P, NT, 2])
            keep = sa("keep", [P, NT, 2])
            slot_f = sa("slot_f", [P, NT, 2])
            drop = sa("drop", [P, NT, 2])
            gidx = sa("gidx", [P, NT, 2], U32)
            sidx = sa("sidx", [P, NT, 2], U32)
            ee = sa("ee", [P, NT])
            pw = sa("pw", [P, NT, 2])
            xr = sa("xr", [SLOT_P, SLOT_M, L])
            w1 = sa("w1", [P, KL, FF])
            w2 = sa("w2", [P, FF // P, L])
            ht = sa("ht", [P, 4, CAP // 2 + 1])
            w1s = sa("w1s", [P, 2, KL, FF], F32R)
            w2s = sa("w2s", [P, 2, FF // P, L], F32R)
            xes = sa("xes", [P, 2, KL, PITCH], F32R)
            hts = sa("hts", [P, 2, FF // P, PITCH], F32R)
            eo = sa("eo", [SLOT_P, 2, SLOT_M, L])
            ga = sa("ga", [P, 4, 2, L])
            KF = FF // P
            HALVES = [slice(0, CAP // 2 + CAP // 2 % 2), slice(CAP // 2 + CAP // 2 % 2, CAP)]
            PARTS = [(0, 0), (0, 1), (1, 0)]

            (ld_rows, ld_w1, ld_w2, w1_high, w1_split, w2_high, w2_split, x_high, x_split, h_high, h_split, tok_loaded, h1_loaded, rt_step, oh_ready, counts_ready, ee_in, ee_ready, idx_ready,
             w_ready, scattered, pad_ready, tr_ready, up_ready, gelu_done, down_ready, eo_taken, eo_stored0, eo_stored1,
             gath0, gath1, gath2, gath3, mixed, out_stored, mix_step, split_waits) = sems(
                "ld_rows ld_w1 ld_w2 w1_high w1_split w2_high w2_split x_high x_split h_high h_split tok_loaded h1_loaded rt_step oh_ready counts_ready ee_in ee_ready idx_ready w_ready "
                "scattered pad_ready tr_ready up_ready gelu_done down_ready eo_taken eo_stored0 eo_stored1 gath0 gath1 gath2 gath3 "
                "mixed out_stored mix_step split_waits")
            eo_stored = [eo_stored0, eo_stored1]
            gathered = [gath0, gath1, gath2, gath3]
            block = stage.enter_context(nc.Block("experts"))
            pairs = NE // 2
            WIDE = PITCH // 2

            def apart(eng):
                eng.sem_inc(split_waits, 1)

            def rows_of(e, n):
                return slice(e * n, (e + 1) * n) if isinstance(e, int) else bass.ds(e * n, n)

            @block.sync
            def _(sp):
                sp.dma_start(xts[:, :, :], xt_scr.rearrange("(j p) d -> p j d", p=P)).then_inc(tok_loaded, 16)
                fc, pj = c_fc.rearrange("e l f -> (e l) f"), c_proj.rearrange("e f d -> (e f) d")

                def load(e, s):
                    wait(sp, w1_split, 2 * e)
                    sp.dma_start(w1[:, :, :], fc[rows_of(e, L), :].rearrange("(j p) f -> p j f", p=P)).then_inc(ld_w1, 16)
                    if isinstance(e, int) and e == 0:
                        sp.dma_start(w2[:, :, :], pj[rows_of(e, FF), :].rearrange("(k p) d -> p k d", p=P)).then_inc(ld_w2, 16)
                        sp.wait_ge(scattered, 2 * NT * 16)
                    wait(sp, tr_ready, 4 * e)
                    sp.dma_start(xr[:, :, :], xe_scr[rows_of(e, PITCH), :].rearrange("(m p) d -> p m d", p=SLOT_P)).then_inc(ld_rows, 16)
                    if not (isinstance(e, int) and e == 0):
                        wait(sp, w2_split, 2 * e)
                        sp.dma_start(w2[:, :, :], pj[rows_of(e, FF), :].rearrange("(k p) d -> p k d", p=P)).then_inc(ld_w2, 16)

                load(0, 0)
                sp.dma_start(h1s[:, :, :], h1_scr.rearrange("(j p) d -> p j d", p=P)).then_inc(h1_loaded, 16)
                load(1, 1)
                with sp.Fori(1, pairs) as i:
                    load(2 * i, 0)
                    load(2 * i + 1, 1)
                for j in range(NT):
                    sp.wait_ge(mixed, j + 1)
                    if j < 16:
                        to, of = out[j // 2, 1 + (j % 2) * P:1 + (j % 2 + 1) * P, :], h1s[:, j, :]
                    else:
                        to, of = out[:, 0, :], h1_cls[0:NSEQ, :]
                    sp.dma_start(to, of).then_inc(out_stored, 16)
                sp.wait_ge(out_stored, NT * 16)

            @block.scalar
            def _(act):
                act.wait_ge(ee_in, 1)
                nc.scalar.activation(ee[:, :], ee[:, :], ACT.Exp).then_inc(ee_ready, 1)

                def rows_high(e):
                    for i in range(4):
                        act.wait_ge(tr_ready, 4 * e + i + 1)
                        if i == 0:
                            wait(act, up_ready, 16 * e)
                        cols = slice(i // 2 * WIDE, (i // 2 + 1) * WIDE)
                        nc.scalar.activation(xes[:, 0, i % 2, cols], bank[i % 2][:, 0:WIDE], ACT.Copy).then_inc(x_high, 1)

                def gelu(e, s):
                    for f in range(KF):
                        for h in range(2):
                            i = 2 * f + h
                            act.wait_ge(up_ready, 16 * e + i + 1)
                            wait(act, h_split, 16 * e + i - 3)
                            n = HALVES[h].stop - HALVES[h].start
                            nc.scalar.activation(ht[:, i % 4, 0:n], bank[2 + i % 4][:, 0:n], ACT.Gelu).then_inc(gelu_done, 1)
                    if not (isinstance(e, int) and e == NE - 1):
                        rows_high(e + 1)
                    act.wait_ge(eo_taken, SLOT_M * (e + 1))
                    act.dma_start(eo_scr[rows_of(e, PITCH), :].rearrange("(m p) d -> p m d", p=SLOT_P), eo[:, s, :, :])\
                        .then_inc(eo_stored[s], 16)

                rows_high(0)
                gelu(0, 0)
                gelu(1, 1)
                with act.Fori(1, pairs - 1) as i:
                    gelu(2 * i, 0)
                    gelu(2 * i + 1, 1)
                gelu(NE - 2, 0)
                gelu(NE - 1, 1)

            @block.vector
            def _(dve):
                v = nc.vector
                own = [0]

                def step(ins):
                    own[0] += 1
                    ins.then_inc(rt_step, 1)
                    dve.wait_ge(rt_step, own[0])

                v.memset(oneb[:, :], 1.0)
                v.memset(entry[:, :, 0:1], 0.0)
                v.memset(within[:, :, 0:1], 0.0)
                v.memset(within[:, :, 1:NC], 1.0)
                v.tensor_copy(trib[:, :], tri[:, :])
                for j in range(NT):
                    ins = v.max(top[:, j, :], logits[:, j, :])
                step(ins)
                for j in range(NT):
                    ins = v.max_index(topi[:, j, :], top[:, j, :], logits[:, j, :])
                step(ins)
                v.tensor_tensor(ee[:, :], top[:, :, 1], top[:, :, 0], ALU.subtract).then_inc(ee_in, 1)
                step(v.tensor_copy(ef[:, :, :], topi[:, :, 0:2]))
                step(v.tensor_tensor(oh[:, :, :, :], iota8[:, :].unsqueeze(1).unsqueeze(1).broadcast_to([P, NT, 2, NE]),
                                     ef[:, :, :].unsqueeze(3).broadcast_to([P, NT, 2, NE]), ALU.is_equal))
                v.tensor_copy(ohb[:, :, :, :], oh[:, :, :, :]).then_inc(oh_ready, 1)
                dve.wait_ge(ee_ready, 1)
                step(v.tensor_scalar(keep[:, :, 0], ee[:, :], 1.0, None, ALU.add))
                step(v.reciprocal(pw[:, :, 0], keep[:, :, 0]))
                step(v.tensor_tensor(pw[:, :, 1], ee[:, :], pw[:, :, 0], ALU.mult))
                dve.wait_ge(counts_ready, 1)
                count = bank[0][:, 0:16 * 2 * NE].rearrange("p (j k e) -> p j k e", j=16, k=2)
                prefix = bank[1][:, 0:16 * 2 * NE].rearrange("p (j k e) -> p j k e", j=16, k=2)
                entries = entry[:, :, 1:NC].rearrange("p x (q r) -> p x q r", r=3)
                v.tensor_copy(entries[:, :, :, 1:3], count.rearrange("p (q r) k e -> p (k e) q r", r=2))
                step(v.tensor_copy(entries[:, :, :, 0], oh[:, 16, :, :].rearrange("p k e -> p (k e)").unsqueeze(2)
                                   .broadcast_to([P, 2 * NE, NSEQ])))
                step(v.tensor_tensor_scan(before[:, :, :].rearrange("p x n -> p (x n)"), within[:, :, :].rearrange("p x n -> p (x n)"),
                                          entry[:, :, :].rearrange("p x n -> p (x n)"), 0.0, ALU.mult, ALU.add))
                seen = before[:, :, 0:NC - 1].rearrange("p x (q r) -> p x q r", r=3)
                v.tensor_tensor(rank[:, 0:16, :, :].rearrange("p (q r) k e -> p q r (k e)", r=2),
                                prefix.rearrange("p (q r) k e -> p q r (k e)", r=2),
                                seen[:, :, :, 1:3].rearrange("p x q r -> p q r x"), ALU.add)
                step(v.tensor_tensor(cls_before[:, :, :], seen[:, :, :, 0],
                                     ident[:, 0:NSEQ].unsqueeze(1).broadcast_to([P, 2 * NE, NSEQ]), ALU.mult))
                step(v.tensor_reduce(rank[:, 16, :, :].rearrange("p k e -> p (k e)"), cls_before[:, :, :], AX.X, ALU.add))
                step(v.tensor_tensor(rank[:, :, 1, :], rank[:, :, 1, :],
                                     before[:, 0:NE, NC - 1].unsqueeze(1).broadcast_to([P, NT, NE]), ALU.add))
                step(v.tensor_tensor(rank[:, :, :, :], rank[:, :, :, :], oh[:, :, :, :], ALU.mult))
                step(v.tensor_reduce(rk[:, :, :], rank[:, :, :, :], AX.X, ALU.add))
                v.tensor_scalar(keep[:, :, :], rk[:, :, :], float(CAP), None, ALU.is_lt)
                step(v.scalar_tensor_tensor(slot_f[:, :, :], ef[:, :, :], float(PITCH), rk[:, :, :], ALU.mult, ALU.add))
                v.tensor_scalar(drop[:, :, :], keep[:, :, :], -OUT_OF_RANGE, OUT_OF_RANGE, ALU.mult, ALU.add)
                step(v.tensor_tensor(slot_f[:, :, :], slot_f[:, :, :], keep[:, :, :], ALU.mult))
                v.tensor_copy(gidx[:, :, :], slot_f[:, :, :])
                step(v.tensor_tensor(drop[:, :, :], drop[:, :, :], slot_f[:, :, :], ALU.add))
                v.tensor_copy(sidx[:, :, :], drop[:, :, :]).then_inc(idx_ready, 1)
                v.tensor_tensor(pw[:, :, :], pw[:, :, :], keep[:, :, :], ALU.mult).then_inc(w_ready, 1)
                v.memset(hts[:, 0, :, CAP:PITCH].bitcast(F32), 0.0)
                v.memset(hts[:, 1, :, CAP:PITCH].bitcast(F32), 0.0).then_inc(pad_ready, 1)

                def rows_low(e, turns=range(4)):
                    for i in turns:
                        dve.wait_ge(x_high, 4 * e + i + 1)
                        cols = slice(i // 2 * WIDE, (i // 2 + 1) * WIDE)
                        v.tensor_tensor(xes[:, 1, i % 2, cols], bank[i % 2][:, 0:WIDE], xes[:, 0, i % 2, cols], ALU.subtract)\
                            .then_inc(x_split, 1)

                def w1_low(e):
                    for j in range(KL):
                        dve.wait_ge(w1_high, KL * e + j + 1)
                        v.tensor_tensor(w1s[:, 1, j, :], w1[:, j, :], w1s[:, 0, j, :], ALU.subtract).then_inc(w1_split, 1)

                def w2_low(e, i):
                    dve.wait_ge(w2_high, 2 * e + i + 1)
                    fs = slice(i * KF // 2, (i + 1) * KF // 2)
                    v.tensor_tensor(w2s[:, 1, fs, :], w2[:, fs, :], w2s[:, 0, fs, :], ALU.subtract).then_inc(w2_split, 1)

                def hidden_low(e):
                    for f in range(KF):
                        if f in (2, 4):
                            w2_low(e, f // 2 - 1)
                        for h in range(2):
                            i = 2 * f + h
                            dve.wait_ge(h_high, 16 * e + i + 1)
                            n = HALVES[h].stop - HALVES[h].start
                            v.tensor_tensor(hts[:, 1, f, HALVES[h]], ht[:, i % 4, 0:n], hts[:, 0, f, HALVES[h]], ALU.subtract)\
                                .then_inc(h_split, 1)

                def outputs(e, s, ms):
                    if 0 in ms:
                        wait(dve, eo_stored[s], 8 * (e - s))
                    for m in ms:
                        dve.wait_ge(down_ready, SLOT_M * e + m + 1)
                        v.tensor_copy(eo[:, s, m, :], bank[6 + m % 2][0:SLOT_P, 0:L]).then_inc(eo_taken, 1)

                def expert(e, s, last=False):
                    hidden_low(e)
                    if not last:
                        rows_low(e + 1, (0, 1))
                    outputs(e, s, [0])
                    if not last:
                        rows_low(e + 1, (2, 3))
                        w1_low(e + 1)
                    outputs(e, s, range(1, SLOT_M))

                w1_low(0)
                rows_low(0)
                expert(0, 0)
                expert(1, 1)
                with dve.Fori(1, pairs - 1) as i:
                    expert(2 * i, 0)
                    expert(2 * i + 1, 1)
                expert(NE - 2, 0)
                expert(NE - 1, 1, last=True)
                for j in range(NT):
                    n = P if j < 16 else NSEQ
                    src = h1s[:, j, :] if j < 16 else h1_cls[0:NSEQ, :]
                    dve.wait_ge(gathered[j % 4], 32 * (j // 4 + 1))
                    if j == 0:
                        dve.wait_ge(h1_loaded, 16)
                        dve.wait_ge(w_ready, 1)
                    v.scalar_tensor_tensor(src, ga[0:n, j % 4, 0, :], pw[0:n, j, 0:1], src, ALU.mult, ALU.add).then_inc(mix_step, 1)
                    dve.wait_ge(mix_step, j + 1)
                    v.scalar_tensor_tensor(src, ga[0:n, j % 4, 1, :], pw[0:n, j, 1:2], src, ALU.mult, ALU.add).then_inc(mixed, 1)

            @block.gpsimd
            def _(pool):
                def high(dst, src):
                    return nc.gpsimd.tensor_scalar(dst, src, 1.0, 1.0, ALU.mult, ALU.mult)

                def w1_round(e):
                    wait(pool, up_ready, 16 * e)
                    pool.wait_ge(ld_w1, 16 * (e + 1))
                    apart(pool)
                    for j in range(KL):
                        high(w1s[:, 0, j, :], w1[:, j, :]).then_inc(w1_high, 1)

                pool.wait_ge(tok_loaded, 16)
                pool.wait_ge(idx_ready, 1)
                for j in range(NT):
                    n = P if j < 16 else NSEQ
                    src = xts[:, j, :] if j < 16 else xt_cls[0:NSEQ, :]
                    for k in range(2):
                        nc.gpsimd.indirect_dma_start(xe_scr, bass.IndirectOffsetOnAxis(ap=sidx[0:n, j, k:k + 1], axis=0), src, None,
                                                     bounds_check=NE * PITCH - 1, oob_is_err=False).then_inc(scattered, 16)

                def w2_round(e, i):
                    if i == 0:
                        wait(pool, down_ready, SLOT_M * e)
                        pool.wait_ge(ld_w2, 16 * (e + 1))
                        apart(pool)
                    fs = slice(i * KF // 2, (i + 1) * KF // 2)
                    high(w2s[:, 0, fs, :], w2[:, fs, :]).then_inc(w2_high, 1)

                def expert(e, last=False):
                    for f in range(KF):
                        if f in (1, 2):
                            w2_round(e, f - 1)
                        for h in range(2):
                            i = 2 * f + h
                            pool.wait_ge(gelu_done, 16 * e + i + 1)
                            if i == 0:
                                wait(pool, down_ready, SLOT_M * e)
                            apart(pool)
                            n = HALVES[h].stop - HALVES[h].start
                            high(hts[:, 0, f, HALVES[h]], ht[:, i % 4, 0:n]).then_inc(h_high, 1)
                    if not last:
                        w1_round(e + 1)

                w1_round(0)
                expert(0)
                with pool.Fori(0, pairs - 1) as i:
                    expert(2 * i + 1)
                    expert(2 * i + 2)
                expert(NE - 1, last=True)
                for s in range(2):
                    pool.wait_ge(eo_stored[s], 8 * NE)
                for j in range(NT):
                    n = P if j < 16 else NSEQ
                    wait(pool, mixed, j - 3)
                    for k in range(2):
                        nc.gpsimd.indirect_dma_start(ga[0:n, j % 4, k, :], None, eo_scr,
                                                     bass.IndirectOffsetOnAxis(ap=gidx[0:n, j, k:k + 1], axis=0),
                                                     bounds_check=NE * PITCH - 1, oob_is_err=False).then_inc(gathered[j % 4], 16)

            @block.tensor
            def _(pe):
                mm = nc.tensor.matmul
                n = 16 * 2 * NE
                pe.wait_ge(oh_ready, 1)
                flat = ohb[:, 0:16, :, :].rearrange("p j k e -> p (j k e)")
                mm(bank[0][:, 0:n], oneb[:, :], flat, start=True, stop=True)
                mm(bank[1][:, 0:n], trib[:, :], flat, start=True, stop=True).then_inc(counts_ready, 1)
                pe.wait_ge(idx_ready, 1)

                def rows_in(e, turns):
                    pe.wait_ge(ld_rows, 16 * (e + 1))
                    for i in turns:
                        j, h = i % 2, i // 2
                        wait(pe, x_split, 4 * e + i - 1)
                        for m in range(3):
                            last = nc.tensor.transpose(bank[i % 2][:, m * SLOT_P:(m + 1) * SLOT_P],
                                                       xr[:, 3 * h + m, j * P:(j + 1) * P], ident[0:SLOT_P, 0:SLOT_P])
                        last.then_inc(tr_ready, 1)

                def up(e, s):
                    pe.wait_ge(w1_split, KL * (e + 1))
                    pe.wait_ge(x_split, 4 * (e + 1))
                    for f in range(KF):
                        for h in range(2):
                            i = 2 * f + h
                            wait(pe, gelu_done, 16 * e + i - 3)
                            n = HALVES[h].stop - HALVES[h].start
                            products = [(j, w, x) for w, x in PARTS for j in range(KL)]
                            for step, (j, w, x) in enumerate(products):
                                last = mm(bank[2 + i % 4][:, 0:n], w1s[:, w, j, f * P:(f + 1) * P], xes[:, x, j, HALVES[h]],
                                          start=(step == 0), stop=(step == len(products) - 1))
                            last.then_inc(up_ready, 1)

                def down(e, s, last=False):
                    if not last:
                        rows_in(e + 1, (0, 1))
                    pe.wait_ge(w2_split, 2 * (e + 1))
                    pe.wait_ge(h_split, 16 * (e + 1))
                    for m in range(SLOT_M):
                        wait(pe, eo_taken, SLOT_M * e + m - 1)
                        products = [(f, w, x) for w, x in PARTS for f in range(KF)]
                        for step, (f, w, x) in enumerate(products):
                            product = mm(bank[6 + m % 2][0:SLOT_P, 0:L], hts[:, x, f, m * SLOT_P:(m + 1) * SLOT_P], w2s[:, w, f, :],
                                      start=(step == 0), stop=(step == len(products) - 1))
                        product.then_inc(down_ready, 1)
                        if m == 0 and not last:
                            rows_in(e + 1, (2, 3))

                rows_in(0, range(4))
                pe.wait_ge(pad_ready, 1)
                up(0, 0)
                down(0, 0)
                with pe.Fori(0, pairs - 1) as i:
                    up(2 * i + 1, 1)
                    down(2 * i + 1, 1)
                    up(2 * i + 2, 0)
                    down(2 * i + 2, 0)
                up(NE - 1, 1)
                down(NE - 1, 1, last=True)


_OUTS = [((NSEQ, HEADS + 1, L), 'float32')]


def kernel(**inputs):
    import numpy as _np
    import concourse.bacc as _bacc
    from concourse import mybir as _mybir
    from concourse.bass_utils import run_bass_kernel_spmd as _run

    i = {k: _np.asarray(v) for k, v in inputs.items()}

    def fold(a):
        return a.reshape(2, HEADS // 2, NST).transpose(0, 2, 1).reshape(P, HEADS // 2)

    def channels(a):
        return a.reshape((KD, P) + a.shape[1:]).swapaxes(0, 1)

    laid = {
        "x": i["x"].reshape(NSEQ, 2, HEADS // 2, NST, 2).transpose(1, 3, 4, 2, 0).reshape(P, 2, HEADS // 2, NSEQ),
        "s4": _np.stack([fold(i["L0_tok_inv_A_real"]), fold(i["L0_tok_A_imag"]), fold(i["L0_tok_B_ri"][..., 0]),
                         fold(i["L0_tok_B_ri"][..., 1]),
                         fold(_np.broadcast_to(i["L0_tok_log_dt"][:, None], (HEADS, NST)))], axis=1),
        "cls": i["cls_tok"].reshape(1, L),
        "w_in": i["L0_attn_in_proj_w"].T.reshape(KL, P, 2 * DI).transpose(1, 0, 2),
        "dpar": _np.concatenate([channels(i["L0_attn_conv_w"][:, 0, :]), channels(i["L0_attn_conv_b"][:, None]),
                                 channels(i["L0_attn_dt_proj_w"]), channels(i["L0_attn_dt_proj_b"][:, None]),
                                 channels(i["L0_attn_D"][:, None]), channels(i["L0_attn_A_log"])], axis=2),
        "dtw_row": i["L0_attn_dt_proj_w"].reshape(1, DI),
        "w_xp": channels(i["L0_attn_x_proj_w"].T),
        "w_out": channels(i["L0_attn_out_proj_w"].T),
        "ln_rows": _np.stack([i["L0_attn_ln_gamma"], i["L0_attn_ln_beta"]]),
        "w_g": i["L0_ffn_w_g"].reshape(KL, P, NE).transpose(1, 0, 2),
        "c_fc": i["L0_ffn_c_fc"],
        "c_proj": i["L0_ffn_c_proj"],
        "ident_in": _np.eye(P, dtype=_np.float32),
        "tri_in": _np.triu(_np.ones((P, P), _np.float32), 1),
        "iota_in": _np.arange(NE, dtype=_np.float32)[None, :],
    }
    nc = _bacc.Bacc("TRN2", target_bir_lowering=False, num_devices=1)
    arrays, args = {}, []
    for name, a in laid.items():
        a = _np.ascontiguousarray(a)
        arrays[f"in_{name}"] = a
        args.append(nc.dram_tensor(f"in_{name}", a.shape, _mybir.dt.from_np(a.dtype), kind="ExternalInput").ap())
    for n, (shape, dtype) in enumerate(_OUTS):
        dt = _mybir.dt.from_np(_np.dtype(dtype))
        args.append(nc.dram_tensor(f"out_{n}", shape, dt, kind="ExternalOutput").ap())
    vit_tower_kernel(nc, *args)
    r = _run(nc, [arrays], core_ids=[0])
    return r.results[0]["out_0"]
```
